# Optimizing a Trainium2 kernel written in Bass

```python
import numpy as np
import jax
import jax.numpy as jnp

def _softmax(x, axis=-1):
    return jax.nn.softmax(x, axis=axis)

def _gelu(x):
    return jax.nn.gelu(x, approximate=True)

def _silu(x):
    return jax.nn.silu(x)

def _sigmoid(x):
    return jax.nn.sigmoid(x)

def _layernorm(x, axis=-1, eps=1e-05):
    m = jnp.mean(x, axis=axis, keepdims=True)
    v = jnp.var(x, axis=axis, keepdims=True)
    return (x - m) / jnp.sqrt(v + eps)

def _scatter_add(tgt, idx, src, axis=0):
    return tgt.at[idx].add(src)

def _segment_sum(src, seg, n):
    return jax.ops.segment_sum(src, seg, n)
kernel_name = 'mk_audio_tower_d2_tok_audfeat1024_r4_da7015'

def setup_inputs(seed: int=0):
    np.random.seed(seed)
    _w = jnp.asarray

    def _rec_inputs():
        import jax
        import jax.numpy as jnp
        _rk = jax.random.key(seed)
        x = -0.000125008 + 0.999885 * jax.random.normal(jax.random.fold_in(_rk, 1), (64, 125, 256), jnp.float32)
        return x
    x = _rec_inputs()

    def _L0_tok_setup():
        import jax, jax.numpy as jnp
        import numpy as np
        D = 256
        HEADS = 4
        FACTOR = 8
        key = jax.random.key(seed)
        kx, kq, kk, kv = jax.random.split(key, 4)
        x = jax.random.normal(kx, (8, 1024, D), dtype=jnp.float32)
        q = jax.random.normal(kq, (HEADS, D), dtype=jnp.float32)
        Wk = jax.random.normal(kk, (D, D), dtype=jnp.float32) * (1.0 / np.sqrt(D))
        Wv = jax.random.normal(kv, (D, D), dtype=jnp.float32) * (1.0 / np.sqrt(D))
        return {'x': x, 'q': q, 'Wk': Wk, 'Wv': Wv}
    _L0_tok_all = _L0_tok_setup()
    _L0_tok_in = {k: v for k, v in _L0_tok_all.items() if k in ('q', 'Wk', 'Wv')}
    del _L0_tok_all

    def _L0_attn_setup():
        import jax, jax.numpy as jnp
        import numpy as np
        D = 256
        H = 16
        S = 512
        B = 2
        LN_EPS = 1e-05
        key = jax.random.key(seed)
        ks = jax.random.split(key, 8)
        x = jax.random.normal(ks[0], (B, S, D), dtype=jnp.float32)
        W_w = jax.random.normal(ks[1], (3 * D, D), dtype=jnp.float32) * 0.02
        W_b = jnp.zeros((3 * D,), dtype=jnp.float32)
        proj_w = jax.random.normal(ks[2], (D, D), dtype=jnp.float32) * 0.02
        proj_b = jnp.zeros((D,), dtype=jnp.float32)
        ln_g = jnp.ones((D,), dtype=jnp.float32)
        ln_b = jnp.zeros((D,), dtype=jnp.float32)
        rpb = jax.random.normal(ks[3], (2 * S - 1, H), dtype=jnp.float32)
        return {'x': x, 'W_w': W_w, 'W_b': W_b, 'proj_w': proj_w, 'proj_b': proj_b, 'ln_g': ln_g, 'ln_b': ln_b, 'rpb': rpb}
    _L0_attn_all = _L0_attn_setup()
    _L0_attn_in = {k: v for k, v in _L0_attn_all.items() if k in ('W_w', 'W_b', 'proj_w', 'proj_b', 'ln_g', 'ln_b', 'rpb')}
    del _L0_attn_all

    def _L0_ffn_setup():
        import jax, jax.numpy as jnp
        import numpy as np
        B, S, D, F, E, K = (4, 512, 256, 1024, 8, 2)
        FS = 256
        LN_EPS = 1e-05

        def _swiglu(x, gu_w, dn_w):
            gate, up = jnp.split(x @ gu_w, 2, axis=-1)
            gate = jnp.clip(gate, -10.0, 10.0)
            return jax.nn.silu(gate) * up @ dn_w
        key = jax.random.key(seed)
        ks = jax.random.split(key, 6)
        s = 0.02
        return {'x': jax.random.normal(ks[0], (B, S, D), jnp.float32), 'ln_gamma': jnp.ones((D,), jnp.float32), 'ln_beta': jnp.zeros((D,), jnp.float32), 'router_w': jax.random.normal(ks[1], (D, E), jnp.float32) * s, 'gate_up_w': jax.random.normal(ks[2], (E, D, 2 * F), jnp.float32) * s, 'down_w': jax.random.normal(ks[3], (E, F, D), jnp.float32) * s, 'shared_gate_up_w': jax.random.normal(ks[4], (D, 2 * FS), jnp.float32) * s, 'shared_down_w': jax.random.normal(ks[5], (FS, D), jnp.float32) * s}
    _L0_ffn_all = _L0_ffn_setup()
    _L0_ffn_in = {k: v for k, v in _L0_ffn_all.items() if k in ('ln_gamma', 'ln_beta', 'router_w', 'gate_up_w', 'down_w', 'shared_gate_up_w', 'shared_down_w')}
    del _L0_ffn_all

    def _L1_attn_setup():
        import math
        import jax, jax.numpy as jnp
        import numpy as np
        EMBED_DIM = 256
        ZDIM = 128
        CHUNK = 512
        DSTATE = 16
        DT_RANK = math.ceil(EMBED_DIM / 16)

        def silu(x):
            return x * jax.nn.sigmoid(x)

        def rmsnorm(x, w, eps=1e-05):
            var = jnp.mean(x * x, axis=-1, keepdims=True)
            return x * jax.lax.rsqrt(var + eps) * w

        def _rotary(v, sin, cos):
            x1, x2 = jnp.split(v, 2, axis=-1)
            return jnp.concatenate([x1 * cos - x2 * sin, x2 * cos + x1 * sin], axis=-1)

        def rel_pos_bias(alpha, beta, n):
            half = ZDIM // 2
            freqs = jnp.exp(jnp.arange(half, dtype=jnp.float32) * (-math.log(10000.0) / half))
            ang = jnp.arange(n, dtype=jnp.float32)[:, None] * freqs[None, :]
            sin, cos = (jnp.sin(ang), jnp.cos(ang))
            a = _rotary(jnp.broadcast_to(alpha, (n, ZDIM)), sin, cos)
            b = _rotary(jnp.broadcast_to(beta, (n, ZDIM)), sin, cos)
            return jnp.einsum('mk,nk->mn', a, b)

        def s6(u, xproj_w, dt_w, dt_b, A_log, D_p):
            x_dbl = u @ xproj_w.T
            dt, Bm, Cm = jnp.split(x_dbl, [DT_RANK, DT_RANK + DSTATE], axis=-1)
            dt = jax.nn.softplus(dt @ dt_w.T + dt_b)
            A = -jnp.exp(A_log)

            def step(h, inp):
                dt_t, B_t, C_t, u_t = inp
                dA = jnp.exp(dt_t[..., None] * A)
                h = dA * h + (dt_t * u_t)[..., None] * B_t[:, None, :]
                y = jnp.einsum('bdn,bn->bd', h, C_t)
                return (h, y)
            B, L, D = u.shape
            h0 = jnp.zeros((B, D, DSTATE), u.dtype)
            xs = (dt.transpose(1, 0, 2), Bm.transpose(1, 0, 2), Cm.transpose(1, 0, 2), u.transpose(1, 0, 2))
            _, ys = jax.lax.scan(step, h0, xs)
            return ys.transpose(1, 0, 2) + u * D_p
        key = jax.random.key(seed)
        ks = jax.random.split(key, 12)
        std = 0.02
        B, L, D = (2, 1024, EMBED_DIM)
        f32 = jnp.float32
        inp = {'x': jax.random.normal(ks[0], (B, L, D), f32), 'norm_w': jnp.ones((D,), f32), 'v_w': jax.random.normal(ks[1], (D, D), f32) * std, 'v_b': jnp.zeros((D,), f32), 'mx_w': jax.random.normal(ks[2], (ZDIM + D + 2 * D, D), f32) * std, 'mx_b': jnp.zeros((ZDIM + 3 * D,), f32), 'h_w': jax.random.normal(ks[3], (D, D), f32) * std, 'h_b': jnp.zeros((D,), f32), 'gamma': jax.random.normal(ks[4], (2, ZDIM), f32) * std, 'beta': jnp.zeros((2, ZDIM), f32), 'alpha_rb': jax.random.normal(ks[5], (1, ZDIM), f32) * std, 'beta_rb': jax.random.normal(ks[6], (1, ZDIM), f32) * std, 'xproj_w': jax.random.normal(ks[7], (DT_RANK + 2 * DSTATE, D), f32) * std, 'dt_w': jax.random.normal(ks[8], (D, DT_RANK), f32) * std, 'dt_b': jnp.full((D,), -4.6, f32), 'A_log': jnp.log(jnp.broadcast_to(jnp.arange(1, DSTATE + 1, dtype=f32), (D, DSTATE))), 'D_p': jnp.ones((D,), f32)}
        return inp
    _L1_attn_all = _L1_attn_setup()
    _L1_attn_in = {k: v for k, v in _L1_attn_all.items() if k in ('norm_w', 'v_w', 'v_b', 'mx_w', 'mx_b', 'h_w', 'h_b', 'gamma', 'beta', 'alpha_rb', 'beta_rb', 'xproj_w', 'dt_w', 'dt_b', 'A_log', 'D_p')}
    del _L1_attn_all

    def _L1_ffn_setup():
        import jax, jax.numpy as jnp
        import numpy as np
        H = 16
        TOP_K = 2
        EPS = 1e-05

        def _layer_norm(x, g, b):
            m = x.mean(-1, keepdims=True)
            v = ((x - m) ** 2).mean(-1, keepdims=True)
            return (x - m) * jax.lax.rsqrt(v + EPS) * g + b

        def _block(x, ln1_g, ln1_b, ln2_g, ln2_b, w_qkv, w_o, w_gate, w1, b1, w2, b2):
            B, S, D = x.shape
            hd = D // H
            h = _layer_norm(x, ln1_g, ln1_b)
            qkv = h @ w_qkv
            q, k, v = jnp.split(qkv, 3, axis=-1)
            q = q.reshape(B, S, H, hd)
            k = k.reshape(B, S, H, hd)
            v = v.reshape(B, S, H, hd)
            scores = jnp.einsum('bqhd,bkhd->bhqk', q, k) * hd ** (-0.5)
            causal = jnp.tril(jnp.ones((S, S), bool))
            scores = jnp.where(causal, scores, jnp.finfo(scores.dtype).min)
            attn = jax.nn.softmax(scores, axis=-1)
            o = jnp.einsum('bhqk,bkhd->bqhd', attn, v).reshape(B, S, D)
            x_resid = x + o @ w_o
            moe_in = _layer_norm(x_resid, ln2_g, ln2_b)
            N = B * S
            xf = moe_in.reshape(N, D)
            probs = jax.nn.softmax(xf @ w_gate, axis=-1)
            top_w, top_i = jax.lax.top_k(probs, TOP_K)
            top_w = top_w / top_w.sum(-1, keepdims=True)
            E = w1.shape[0]
            out = jnp.zeros_like(xf)
            for e in range(E):
                gate_e = jnp.sum(jnp.where(top_i == e, top_w, 0.0), axis=-1)
                he = jax.nn.gelu(xf @ w1[e] + b1[e])
                out = out + gate_e[:, None] * (he @ w2[e] + b2[e])
            return out.reshape(B, S, D) + x_resid
        key = jax.random.key(seed)
        ks = jax.random.split(key, 12)
        B, S, D, F, E = (8, 128, 256, 1024, 8)
        inp = {'x': jax.random.normal(ks[0], (B, S, D), jnp.float32), 'ln1_g': jnp.ones((D,), jnp.float32), 'ln1_b': jnp.zeros((D,), jnp.float32), 'ln2_g': jnp.ones((D,), jnp.float32), 'ln2_b': jnp.zeros((D,), jnp.float32), 'w_qkv': jax.random.normal(ks[1], (D, 3 * D), jnp.float32) * D ** (-0.5), 'w_o': jax.random.normal(ks[2], (D, D), jnp.float32) * D ** (-0.5), 'w_gate': jax.random.normal(ks[3], (D, E), jnp.float32) * D ** (-0.5), 'w1': jax.random.normal(ks[4], (E, D, F), jnp.float32) * D ** (-0.5), 'b1': jnp.zeros((E, F), jnp.float32), 'w2': jax.random.normal(ks[5], (E, F, D), jnp.float32) * F ** (-0.5), 'b2': jnp.zeros((E, D), jnp.float32)}
        return inp
    _L1_ffn_all = _L1_ffn_setup()
    _L1_ffn_in = {k: v for k, v in _L1_ffn_all.items() if k in ('ln1_g', 'ln1_b', 'ln2_g', 'ln2_b', 'w_qkv', 'w_o', 'w_gate', 'w1', 'b1', 'w2', 'b2')}
    del _L1_ffn_all
    return {'x': x, 'L0_tok_q': _L0_tok_in['q'], 'L0_tok_Wk': _L0_tok_in['Wk'], 'L0_tok_Wv': _L0_tok_in['Wv'], 'L0_attn_W_w': _L0_attn_in['W_w'], 'L0_attn_W_b': _L0_attn_in['W_b'], 'L0_attn_proj_w': _L0_attn_in['proj_w'], 'L0_attn_proj_b': _L0_attn_in['proj_b'], 'L0_attn_ln_g': _L0_attn_in['ln_g'], 'L0_attn_ln_b': _L0_attn_in['ln_b'], 'L0_attn_rpb': _L0_attn_in['rpb'], 'L0_ffn_ln_gamma': _L0_ffn_in['ln_gamma'], 'L0_ffn_ln_beta': _L0_ffn_in['ln_beta'], 'L0_ffn_router_w': _L0_ffn_in['router_w'], 'L0_ffn_gate_up_w': _L0_ffn_in['gate_up_w'], 'L0_ffn_down_w': _L0_ffn_in['down_w'], 'L0_ffn_shared_gate_up_w': _L0_ffn_in['shared_gate_up_w'], 'L0_ffn_shared_down_w': _L0_ffn_in['shared_down_w'], 'L1_attn_norm_w': _L1_attn_in['norm_w'], 'L1_attn_v_w': _L1_attn_in['v_w'], 'L1_attn_v_b': _L1_attn_in['v_b'], 'L1_attn_mx_w': _L1_attn_in['mx_w'], 'L1_attn_mx_b': _L1_attn_in['mx_b'], 'L1_attn_h_w': _L1_attn_in['h_w'], 'L1_attn_h_b': _L1_attn_in['h_b'], 'L1_attn_gamma': _L1_attn_in['gamma'], 'L1_attn_beta': _L1_attn_in['beta'], 'L1_attn_alpha_rb': _L1_attn_in['alpha_rb'], 'L1_attn_beta_rb': _L1_attn_in['beta_rb'], 'L1_attn_xproj_w': _L1_attn_in['xproj_w'], 'L1_attn_dt_w': _L1_attn_in['dt_w'], 'L1_attn_dt_b': _L1_attn_in['dt_b'], 'L1_attn_A_log': _L1_attn_in['A_log'], 'L1_attn_D_p': _L1_attn_in['D_p'], 'L1_ffn_ln1_g': _L1_ffn_in['ln1_g'], 'L1_ffn_ln1_b': _L1_ffn_in['ln1_b'], 'L1_ffn_ln2_g': _L1_ffn_in['ln2_g'], 'L1_ffn_ln2_b': _L1_ffn_in['ln2_b'], 'L1_ffn_w_qkv': _L1_ffn_in['w_qkv'], 'L1_ffn_w_o': _L1_ffn_in['w_o'], 'L1_ffn_w_gate': _L1_ffn_in['w_gate'], 'L1_ffn_w1': _L1_ffn_in['w1'], 'L1_ffn_b1': _L1_ffn_in['b1'], 'L1_ffn_w2': _L1_ffn_in['w2'], 'L1_ffn_b2': _L1_ffn_in['b2']}

def reference(x, L0_tok_q, L0_tok_Wk, L0_tok_Wv, L0_attn_W_w, L0_attn_W_b, L0_attn_proj_w, L0_attn_proj_b, L0_attn_ln_g, L0_attn_ln_b, L0_attn_rpb, L0_ffn_ln_gamma, L0_ffn_ln_beta, L0_ffn_router_w, L0_ffn_gate_up_w, L0_ffn_down_w, L0_ffn_shared_gate_up_w, L0_ffn_shared_down_w, L1_attn_norm_w, L1_attn_v_w, L1_attn_v_b, L1_attn_mx_w, L1_attn_mx_b, L1_attn_h_w, L1_attn_h_b, L1_attn_gamma, L1_attn_beta, L1_attn_alpha_rb, L1_attn_beta_rb, L1_attn_xproj_w, L1_attn_dt_w, L1_attn_dt_b, L1_attn_A_log, L1_attn_D_p, L1_ffn_ln1_g, L1_ffn_ln1_b, L1_ffn_ln2_g, L1_ffn_ln2_b, L1_ffn_w_qkv, L1_ffn_w_o, L1_ffn_w_gate, L1_ffn_w1, L1_ffn_b1, L1_ffn_w2, L1_ffn_b2):
    import jax
    import jax.numpy as jnp

    def _L0_tok_ref(x, q, Wk, Wv):
        import jax, jax.numpy as jnp
        import numpy as np
        D = 256
        HEADS = 4
        FACTOR = 8
        B, T, Dm = x.shape
        W = FACTOR
        pad = -T % W
        if pad:
            x = jnp.pad(x, ((0, 0), (0, pad), (0, 0)))
        T2 = x.shape[1] // W
        xw = x.reshape(B, T2, W, Dm)
        k = jnp.einsum('btwd,ed->btwe', xw, Wk)
        v = jnp.einsum('btwd,ed->btwe', xw, Wv)
        attn = jnp.einsum('hd,btwd->bhtw', q, k) / np.sqrt(Dm).astype(np.float32)
        w = jax.nn.softmax(attn, axis=-1)
        out = jnp.einsum('bhtw,btwd->bhtd', w, v).mean(axis=1)
        return out

    def _L0_attn_ref(x, W_w, W_b, proj_w, proj_b, ln_g, ln_b, rpb):
        import jax, jax.numpy as jnp
        import numpy as np
        D = 256
        H = 16
        S = 512
        B = 2
        LN_EPS = 1e-05
        b, s, d = x.shape
        hd = d // H
        qkv = x @ W_w.T + W_b
        q, k, v = jnp.split(qkv, 3, axis=-1)
        q, k, v = (z.reshape(b, s, H, hd).transpose(0, 2, 1, 3) for z in (q, k, v))
        attn = jnp.einsum('bhqd,bhkd->bhqk', q, k) / jnp.sqrt(jnp.float32(d))
        causal = jnp.triu(jnp.ones((s, s), dtype=bool), k=1)
        attn = jnp.where(causal[None, None], -jnp.inf, attn)
        rel_idx = jnp.arange(s)[None, :] - jnp.arange(s)[:, None] + (s - 1)
        bias = rpb[rel_idx].transpose(2, 0, 1)
        attn = attn + bias[None]
        w = jax.nn.softmax(attn, axis=-1)
        o = jnp.einsum('bhqk,bhkd->bhqd', w, v)
        o = o.transpose(0, 2, 1, 3).reshape(b, s, d)
        out = o @ proj_w.T + proj_b
        y = x + out
        mu = jnp.mean(y, axis=-1, keepdims=True)
        var = jnp.var(y, axis=-1, keepdims=True)
        return (y - mu) / jnp.sqrt(var + LN_EPS) * ln_g + ln_b

    def _L0_ffn_ref(x, ln_gamma, ln_beta, router_w, gate_up_w, down_w, shared_gate_up_w, shared_down_w):
        import jax, jax.numpy as jnp
        import numpy as np
        B, S, D, F, E, K = (4, 512, 256, 1024, 8, 2)
        FS = 256
        LN_EPS = 1e-05

        def _swiglu(x, gu_w, dn_w):
            gate, up = jnp.split(x @ gu_w, 2, axis=-1)
            gate = jnp.clip(gate, -10.0, 10.0)
            return jax.nn.silu(gate) * up @ dn_w
        b, s, d = x.shape
        xf = x.reshape(-1, d)
        mu = jnp.mean(xf, axis=-1, keepdims=True)
        var = jnp.var(xf, axis=-1, keepdims=True)
        xn = (xf - mu) * jax.lax.rsqrt(var + LN_EPS) * ln_gamma + ln_beta
        logits = xn @ router_w
        probs = jax.nn.softmax(logits, axis=-1)
        topv, topi = jax.lax.top_k(probs, K)
        topv = topv / jnp.sum(topv, axis=-1, keepdims=True)
        comb = jnp.sum(jax.nn.one_hot(topi, E, dtype=xn.dtype) * topv[..., None], axis=1)
        out = jnp.zeros_like(xf)
        for e in range(E):
            out = out + comb[:, e:e + 1] * _swiglu(xn, gate_up_w[e], down_w[e])
        out = out + _swiglu(xn, shared_gate_up_w, shared_down_w)
        return out.reshape(b, s, d)

    def _L1_attn_ref(x, norm_w, v_w, v_b, mx_w, mx_b, h_w, h_b, gamma, beta, alpha_rb, beta_rb, xproj_w, dt_w, dt_b, A_log, D_p):
        import math
        import jax, jax.numpy as jnp
        import numpy as np
        EMBED_DIM = 256
        ZDIM = 128
        CHUNK = 512
        DSTATE = 16
        DT_RANK = math.ceil(EMBED_DIM / 16)

        def silu(x):
            return x * jax.nn.sigmoid(x)

        def rmsnorm(x, w, eps=1e-05):
            var = jnp.mean(x * x, axis=-1, keepdims=True)
            return x * jax.lax.rsqrt(var + eps) * w

        def _rotary(v, sin, cos):
            x1, x2 = jnp.split(v, 2, axis=-1)
            return jnp.concatenate([x1 * cos - x2 * sin, x2 * cos + x1 * sin], axis=-1)

        def rel_pos_bias(alpha, beta, n):
            half = ZDIM // 2
            freqs = jnp.exp(jnp.arange(half, dtype=jnp.float32) * (-math.log(10000.0) / half))
            ang = jnp.arange(n, dtype=jnp.float32)[:, None] * freqs[None, :]
            sin, cos = (jnp.sin(ang), jnp.cos(ang))
            a = _rotary(jnp.broadcast_to(alpha, (n, ZDIM)), sin, cos)
            b = _rotary(jnp.broadcast_to(beta, (n, ZDIM)), sin, cos)
            return jnp.einsum('mk,nk->mn', a, b)

        def s6(u, xproj_w, dt_w, dt_b, A_log, D_p):
            x_dbl = u @ xproj_w.T
            dt, Bm, Cm = jnp.split(x_dbl, [DT_RANK, DT_RANK + DSTATE], axis=-1)
            dt = jax.nn.softplus(dt @ dt_w.T + dt_b)
            A = -jnp.exp(A_log)

            def step(h, inp):
                dt_t, B_t, C_t, u_t = inp
                dA = jnp.exp(dt_t[..., None] * A)
                h = dA * h + (dt_t * u_t)[..., None] * B_t[:, None, :]
                y = jnp.einsum('bdn,bn->bd', h, C_t)
                return (h, y)
            B, L, D = u.shape
            h0 = jnp.zeros((B, D, DSTATE), u.dtype)
            xs = (dt.transpose(1, 0, 2), Bm.transpose(1, 0, 2), Cm.transpose(1, 0, 2), u.transpose(1, 0, 2))
            _, ys = jax.lax.scan(step, h0, xs)
            return ys.transpose(1, 0, 2) + u * D_p
        B, L, D = x.shape
        residual = x
        xn = rmsnorm(x, norm_w)
        v = silu(xn @ v_w.T + v_b)
        mx = silu(s6(xn, xproj_w, dt_w, dt_b, A_log, D_p))
        base = mx @ mx_w.T + mx_b
        u, zr, hx = jnp.split(base, [D, D + ZDIM + D], axis=-1)
        u = jax.nn.sigmoid(u)
        zr = silu(zr)
        z, r = jnp.split(zr, [ZDIM], axis=-1)
        z = z[..., None, :] * gamma + beta
        q, k = (z[..., 0, :], z[..., 1, :])
        c = min(CHUNK, L)
        nc = L // c
        qh = q.reshape(B, nc, c, ZDIM) * ZDIM ** (-0.5)
        kh = k.reshape(B, nc, c, ZDIM)
        vh = v.reshape(B, nc, c, D)
        bias = rel_pos_bias(alpha_rb, beta_rb, c)
        mask = jnp.triu(jnp.full((c, c), -jnp.inf, jnp.float32), 1)
        qk = jnp.einsum('bnqz,bnkz->bnqk', qh, kh) + bias + mask
        attn = jax.nn.softmax(qk.astype(jnp.float32), axis=-1).astype(qk.dtype)
        h = jnp.einsum('bnqk,bnkd->bnqd', attn, vh).reshape(B, L, D)
        h = silu(hx + h * r @ h_w.T + h_b)
        return residual + u * (h - residual)

    def _L1_ffn_ref(x, ln1_g, ln1_b, ln2_g, ln2_b, w_qkv, w_o, w_gate, w1, b1, w2, b2):
        import jax, jax.numpy as jnp
        import numpy as np
        H = 16
        TOP_K = 2
        EPS = 1e-05

        def _layer_norm(x, g, b):
            m = x.mean(-1, keepdims=True)
            v = ((x - m) ** 2).mean(-1, keepdims=True)
            return (x - m) * jax.lax.rsqrt(v + EPS) * g + b

        def _block(x, ln1_g, ln1_b, ln2_g, ln2_b, w_qkv, w_o, w_gate, w1, b1, w2, b2):
            B, S, D = x.shape
            hd = D // H
            h = _layer_norm(x, ln1_g, ln1_b)
            qkv = h @ w_qkv
            q, k, v = jnp.split(qkv, 3, axis=-1)
            q = q.reshape(B, S, H, hd)
            k = k.reshape(B, S, H, hd)
            v = v.reshape(B, S, H, hd)
            scores = jnp.einsum('bqhd,bkhd->bhqk', q, k) * hd ** (-0.5)
            causal = jnp.tril(jnp.ones((S, S), bool))
            scores = jnp.where(causal, scores, jnp.finfo(scores.dtype).min)
            attn = jax.nn.softmax(scores, axis=-1)
            o = jnp.einsum('bhqk,bkhd->bqhd', attn, v).reshape(B, S, D)
            x_resid = x + o @ w_o
            moe_in = _layer_norm(x_resid, ln2_g, ln2_b)
            N = B * S
            xf = moe_in.reshape(N, D)
            probs = jax.nn.softmax(xf @ w_gate, axis=-1)
            top_w, top_i = jax.lax.top_k(probs, TOP_K)
            top_w = top_w / top_w.sum(-1, keepdims=True)
            E = w1.shape[0]
            out = jnp.zeros_like(xf)
            for e in range(E):
                gate_e = jnp.sum(jnp.where(top_i == e, top_w, 0.0), axis=-1)
                he = jax.nn.gelu(xf @ w1[e] + b1[e])
                out = out + gate_e[:, None] * (he @ w2[e] + b2[e])
            return out.reshape(B, S, D) + x_resid
        return _block(x, ln1_g, ln1_b, ln2_g, ln2_b, w_qkv, w_o, w_gate, w1, b1, w2, b2)
    h = _L0_tok_ref(x, L0_tok_q, L0_tok_Wk, L0_tok_Wv)
    h = h + _L0_attn_ref(_layernorm(h, axis=-1), L0_attn_W_w, L0_attn_W_b, L0_attn_proj_w, L0_attn_proj_b, L0_attn_ln_g, L0_attn_ln_b, L0_attn_rpb)
    h = h + _L0_ffn_ref(_layernorm(h, axis=-1), L0_ffn_ln_gamma, L0_ffn_ln_beta, L0_ffn_router_w, L0_ffn_gate_up_w, L0_ffn_down_w, L0_ffn_shared_gate_up_w, L0_ffn_shared_down_w)
    h = h + _L1_attn_ref(_layernorm(h, axis=-1), L1_attn_norm_w, L1_attn_v_w, L1_attn_v_b, L1_attn_mx_w, L1_attn_mx_b, L1_attn_h_w, L1_attn_h_b, L1_attn_gamma, L1_attn_beta, L1_attn_alpha_rb, L1_attn_beta_rb, L1_attn_xproj_w, L1_attn_dt_w, L1_attn_dt_b, L1_attn_A_log, L1_attn_D_p)
    h = h + _L1_ffn_ref(_layernorm(h, axis=-1), L1_ffn_ln1_g, L1_ffn_ln1_b, L1_ffn_ln2_g, L1_ffn_ln2_b, L1_ffn_w_qkv, L1_ffn_w_o, L1_ffn_w_gate, L1_ffn_w1, L1_ffn_b1, L1_ffn_w2, L1_ffn_b2)
    return h

_drawn_inputs = setup_inputs


def setup_inputs(seed=0):
    import zlib

    import numpy as np

    out = dict(_drawn_inputs(seed))
    spreads = {'L0_attn_W_b': (0.0, 0.1),
     'L0_attn_proj_b': (0.0, 0.1),
     'L0_attn_ln_g': (1.0, 0.2),
     'L0_attn_ln_b': (0.0, 0.1),
     'L0_ffn_ln_gamma': (1.0, 0.6),
     'L0_ffn_ln_beta': (0.0, 0.757),
     'L1_attn_norm_w': (1.0, 0.6),
     'L1_attn_v_b': (0.0, 0.8),
     'L1_attn_mx_b': (0.0, 0.274),
     'L1_attn_h_b': (0.0, 2.0),
     'L1_attn_beta': (0.0, 0.8),
     'L1_attn_dt_b': (-4.599999904632568, 0.6),
     'L1_attn_D_p': (1.0, 0.6),
     'L1_ffn_ln1_g': (1.0, 0.6),
     'L1_ffn_ln1_b': (0.0, 0.8),
     'L1_ffn_ln2_g': (1.0, 0.6),
     'L1_ffn_ln2_b': (0.0, 0.766),
     'L1_ffn_b1': (0.0, 2.0),
     'L1_ffn_b2': (0.0, 1.989)}
    factors = {'L0_ffn_shared_gate_up_w': 2.7,
     'L0_ffn_shared_down_w': 3.04,
     'L1_attn_v_w': 8.0,
     'L1_attn_h_w': 8.0,
     'L1_attn_gamma': 8.0,
     'L1_attn_alpha_rb': 8.0,
     'L1_attn_beta_rb': 23.156,
     'L1_attn_xproj_w': 8.0,
     'L1_attn_dt_w': 8.0,
     'L1_attn_A_log': 8.0}
    for name, (base, spread) in spreads.items():
        noise = np.random.default_rng([zlib.crc32(name.encode()), seed]).standard_normal(out[name].shape)
        drawn = base * np.exp(spread * noise) if base else spread * noise
        out[name] = jnp.asarray(drawn.astype(out[name].dtype))
    for name, factor in factors.items():
        out[name] = (out[name] * factor).astype(out[name].dtype)
    return out
```

```python
from contextlib import ExitStack

import numpy as np

import concourse.bass as bass
from concourse import mybir

F32 = mybir.dt.float32
U32 = mybir.dt.uint32
ALU = mybir.AluOpType
ACT = mybir.ActivationFunctionType
AX = mybir.AxisListType

P = 128
D = 256
KD = D // P
CLIPS, FRAMES, WIN = 64, 125, 8
S = 16
TOK = CLIPS * S
T = TOK // P
HALF = TOK // 2
HT = T // 2
POOL_HEADS = 4
H, HD = 16, 16
G = 4
E = 8
F = 1024
FB = F // P
FS = 256
Z = 128
NS = 16
DTR = 16
EPS = 1e-5
NEG = -1e30


def layout(sizes):
    at, out = 0, {}
    for name, n in sizes:
        out[name] = (at, at + n)
        at += n
    return out, at


TOK_PACK, TOK_N = layout([("wk", KD * D), ("q", KD * POOL_HEADS), ("wv", KD * D), ("ident", P)])
L0_PACK, L0_N = layout([
    ("wq", KD * 512), ("wk", KD * 512), ("wv", KD * D), ("wo", KD * D), ("bq", G), ("bk", G),
    ("rel", H * 32), ("mask32", 32), ("ln_g", D), ("ln_b", D), ("gamma", KD), ("beta", KD),
    ("router", KD * E), ("sgu", KD * 2 * FS), ("sdn", FS // P * D), ("iota", E)])
GA_PACK, GA_N = layout([
    ("norm", KD), ("v", KD * D), ("mx", KD * 896), ("mxb", 3), ("h", KD * D), ("xproj", KD * 48),
    ("dt", D), ("A", KD * NS), ("D", KD), ("dtb", KD), ("gamma", 2), ("beta", 2),
    ("cos", S), ("sin", S), ("al", 1), ("als", 1), ("be", 1), ("bes", 1), ("mask", P)])
L1_PACK, L1_N = layout([
    ("wq", KD * 512), ("wk", KD * 512), ("wv", KD * D), ("wo", KD * D), ("g1", KD), ("b1", KD),
    ("g2", KD), ("b2", KD), ("router", KD * E), ("eb1", E * FB), ("eb2", D)])
ROW_PACK, ROW_N = layout([
    ("one", P), ("wv", D), ("wo", D), ("v", D), ("u", D), ("hx", D), ("h", D)])


def tower(nc, x, tok_w, l0_w, ga_w, l1_w, rows_w, moe0_gu, moe0_dn, moe1_up, moe1_dn, out, stop=99):
    ctx = ExitStack()
    with ctx:
        def sb(name, cols, rows=P, dt=F32):
            return ctx.enter_context(nc.sbuf_tensor(name, [rows, cols], dt))

        def sem(name):
            return ctx.enter_context(nc.semaphore(name))

        big = sb("big", T * WIN * D)
        tok_c = sb("tok_c", TOK_N)
        l0_c = sb("l0_c", L0_N)
        ga_c = sb("ga_c", GA_N)
        row_c = sb("row_c", ROW_N, rows=32)
        h_ = sb("h_rows", T * D)
        xh_ = sb("xh_rows", T * D)
        ya_ = sb("ya_rows", T * D)
        v_ = sb("v_rows", T * D)
        ub_ = sb("ub_rows", T * D)
        xc_ = sb("x_cols", KD * TOK)
        fm = sb("fm", 8 * TOK)
        stat = sb("stat", T * 6)
        mv = sb("mv", T * 2)
        ve = sb("ve", T * 2)
        rs = sb("rs", T * 2)
        neghalf = sb("neghalf", T * 2)
        smx = sb("smx", 2 * H)
        ssum = sb("ssum", 2 * H)
        tsc = sb("tsc", 2 * WIN * POOL_HEADS)
        tmx = sb("tmx", 2 * POOL_HEADS)
        tsum = sb("tsum", 2 * POOL_HEADS)
        wbar = sb("wbar", 2 * WIN)
        qk = sb("qk", KD * POOL_HEADS)
        lg = sb("lg", T * E)
        top = sb("top", T * 8)
        idx = sb("idx", T * 8, dt=U32)
        idf = sb("idf", T * 2)
        wgt = sb("wgt", T * 3)
        comb = sb("comb", T * E)
        comb2 = sb("comb2", T * E)
        avec = sb("avec", KD * NS)
        eb_now = sb("eb_now", 2 * FB)
        rot = sb("rot", 4 * S)

        def rows3(a):
            return a[:, 0:T * D].rearrange("p (t d) -> p t d", t=T)

        h, xh, ya, v, ub = rows3(h_), rows3(xh_), rows3(ya_), rows3(v_), rows3(ub_)
        xc = xc_[:, :].rearrange("p (k n) -> p k n", k=KD)
        frames = big[:, :].rearrange("p (t w d) -> p t w d", t=T, w=WIN)
        tail = 12288
        assert tail == 2 * (KD * 2 * F + FB * D)
        gu_w = big[:, 0:2 * KD * 2 * F].rearrange("p (b k f) -> p b k f", b=2, k=KD)
        up_w = big[:, 0:2 * KD * F].rearrange("p (b k f) -> p b k f", b=2, k=KD)
        dn_w = big[:, 2 * KD * 2 * F:tail].rearrange("p (b f d) -> p b f d", b=2, f=FB)
        gclip = big[:, tail:tail + 1024].rearrange("p (b n) -> p b n", b=2)
        gact = big[:, tail + 1024:tail + 2048].rearrange("p (b n) -> p b n", b=2)
        hid = big[:, tail + 2048:tail + 3072].rearrange("p (b n) -> p b n", b=2)
        sc = big[:, tail:tail + 1024].rearrange("p (b h c) -> p b h c", b=2, c=32)
        pT = big[:, tail + 1024:tail + 2048].rearrange("p (b h c) -> p b h c", b=2, c=32)
        oT = big[:, tail + 2048:tail + 2560].rearrange("p (b k n) -> p b k n", b=2, k=KD)
        gsc = big[:, tail:tail + 256].rearrange("p (b n) -> p b n", b=2)
        gpT = big[:, tail + 256:tail + 512].rearrange("p (b n) -> p b n", b=2)
        ghr = big[:, tail + 512:tail + 1024].rearrange("p (b k n) -> p b k n", b=2, k=KD)
        ghh = big[:, tail + 1024:tail + 1536].rearrange("p (b n) -> p b n", b=2)
        gbias = big[:, tail + 1536:tail + 1664]
        rot_a = big[:, tail + 1664:tail + 1792]
        rot_b = big[:, tail + 1792:tail + 1920]
        combT = big[:, tail + 3072:tail + 4096].rearrange("p (t n) -> p t n", t=T)
        qc = fm[:, 0:4 * TOK].rearrange("p (m n) -> p m n", m=4)
        kc = fm[:, 4 * TOK:].rearrange("p (m n) -> p m n", m=4)
        xwT = fm[:, 0:4096].rearrange("p (b w n) -> p b w n", b=2, w=2 * WIN)
        plT = fm[:, 4096:4608].rearrange("p (b k n) -> p b k n", b=2, k=KD)
        pooled = fm[:, 4608:5120].rearrange("p (b d) -> p b d", b=2)
        scan4 = fm[:, :].rearrange("p (a k n) -> p a k n", a=4, k=KD)
        dA, dBu, hs, hC = scan4[:, 0], scan4[:, 1], scan4[:, 2], scan4[:, 3]
        mxT = fm[:, 0:2048].rearrange("p (k n) -> p k n", k=KD)
        rT = fm[:, 2048:4096].rearrange("p (k n) -> p k n", k=KD)
        zT = fm[:, 4096:5120]
        zq = fm[:, 5120:6144]
        zk = fm[:, 6144:7168]
        ypre = xc
        dt = ya_[:, :].rearrange("p (k n) -> p k n", k=KD)
        dtu = ub_[:, :].rearrange("p (k n) -> p k n", k=KD)
        splus = v_[:, :]
        xdbl = fm[0:48, 0:TOK]
        xd = sb("xd", TOK, rows=48)

        def part(tensor, where, name, k=None, rows=P):
            a, b = where[name]
            ap = tensor[0:rows, a:b]
            return ap.rearrange("p (k n) -> p k n", k=k) if k else ap

        ident = part(tok_c, TOK_PACK, "ident")
        w0 = {n: part(l0_c, L0_PACK, n, k) for n, k in (
            ("wq", KD), ("wk", KD), ("wv", KD), ("wo", KD), ("bq", None), ("bk", None), ("mask32", None),
            ("ln_g", None), ("ln_b", None), ("gamma", None), ("beta", None), ("router", KD), ("sgu", KD),
            ("sdn", FS // P), ("iota", None))}
        rel = part(l0_c, L0_PACK, "rel").rearrange("p (h c) -> p h c", c=32)
        w1 = {n: part(l0_c, L1_PACK, n, k) for n, k in (
            ("wq", KD), ("wk", KD), ("wv", KD), ("wo", KD), ("g1", None), ("b1", None), ("g2", None),
            ("b2", None), ("router", KD), ("eb1", E))}
        eb2 = part(l0_c, L1_PACK, "eb2", rows=32)
        ga = {n: part(ga_c, GA_PACK, n, k) for n, k in (
            ("norm", None), ("v", KD), ("mx", KD), ("mxb", None), ("h", KD), ("xproj", KD), ("A", None),
            ("D", None), ("dtb", None), ("gamma", None), ("beta", None), ("cos", None), ("sin", None),
            ("al", None), ("als", None), ("be", None), ("bes", None), ("mask", None))}
        dtw = part(ga_c, GA_PACK, "dt", rows=DTR)
        row = {n: part(row_c, ROW_PACK, n, rows=32) for n in ROW_PACK}
        mask32 = sb("mask32", 32)
        iota = sb("iota", E)

        ps = ctx.enter_context(nc.psum_tensor("ps", [P, 8, 512], F32))

        w_tok, w_l0, w_ga, w_l1 = sem("w_tok"), sem("w_l0"), sem("w_ga"), sem("w_l1")
        x_in = [sem(f"x_in{t}") for t in range(T)]
        out_done = sem("out_done")
        dve_step, act_step, pool_step = sem("dve_step"), sem("act_step"), sem("pool_step")
        consts = sem("consts")
        qk_sum, qk_ready = sem("qk_sum"), sem("qk_ready")
        xw_turned, xw_copied, tok_scored, tok_shift = (sem(n) for n in ("xw_turned", "xw_copied", "tok_scored", "tok_shift"))
        tok_exp, tok_pooled, pool_turned, pool_copied = (sem(n) for n in ("tok_exp", "tok_pooled", "pool_turned", "pool_copied"))
        tok_out, h_ready, tok_score_taken = sem("tok_out"), sem("h_ready"), sem("tok_score_taken")
        var_ready, rstd_ready, normed, turned, cols_ready = (sem(n) for n in ("var_ready", "rstd_ready", "normed", "turned", "cols_ready"))
        qv_filled, qv_taken, k_filled, k_taken = (sem(n) for n in ("qv_filled", "qv_taken", "k_filled", "k_taken"))
        scored, shifted, exped, probs_ready = (sem(n) for n in ("scored", "shifted", "exped", "probs_ready"))
        score_taken = sem("score_taken")
        mixed, mix_copied, mix_turned, mixT_copied, projected, resid_ready = (
            sem(n) for n in ("mixed", "mix_copied", "mix_turned", "mixT_copied", "projected", "resid_ready"))
        routed, top_diff, top_exp, comb_ready = (sem(n) for n in ("routed", "top_diff", "top_exp", "comb_ready"))
        sh_filled, sh_clipped, sh_act, sh_hid, sh_down, sh_added = (
            sem(n) for n in ("sh_filled", "sh_clipped", "sh_act", "sh_hid", "sh_down", "sh_added"))
        gu_loaded = [sem(f"gu_loaded{b}") for b in range(2)]
        expert_used = sem("expert_used")
        gu_filled, clipped, silued, hid_ready, down_filled, combined = (
            sem(n) for n in ("gu_filled", "clipped", "silued", "hid_ready", "down_filled", "combined"))
        up_loaded = [sem(f"up_loaded{b}") for b in range(2)]
        up_used, eb_copied = sem("up_used"), sem("eb_copied")
        up_filled, gelued, down1_filled, combined1 = (sem(n) for n in ("up_filled", "gelued", "down1_filled", "combined1"))
        comb_turned, comb_copied, bias_filled, bias_added = (
            sem(n) for n in ("comb_turned", "comb_copied", "bias_filled", "bias_added"))
        gv_filled, gv_done, xd_filled, xd_copied = (sem(n) for n in ("gv_filled", "gv_done", "xd_filled", "xd_copied"))
        dt_filled, dt_abs, dt_log, dt_relu, dtu_ready, a_exp, a_ready = (
            sem(n) for n in ("dt_filled", "dt_abs", "dt_log", "dt_relu", "dtu_ready", "a_exp", "a_ready"))
        b_spread, c_spread, decay, b_used, c_used, scanned, y_summed = (
            sem(n) for n in ("b_spread", "c_spread", "decay", "b_used", "c_used", "scanned", "y_summed"))
        y_ready, mx_ready, zr_filled, zr_done, qk_cols, u_filled, u_done = (
            sem(n) for n in ("y_ready", "mx_ready", "zr_filled", "zr_done", "qk_cols", "u_filled", "u_done"))
        rot_ready, rot_filled, gbias_ready = sem("rot_ready"), sem("rot_filled"), sem("gbias_ready")
        g_scored, g_shifted, g_exped, g_probs, g_turned, g_copied = (
            sem(n) for n in ("g_scored", "g_shifted", "g_exped", "g_probs", "g_turned", "g_copied"))
        g_mixed, g_gated, g_out, g_silu, g_done = (sem(n) for n in ("g_mixed", "g_gated", "g_out", "g_silu", "g_done"))

        block = ctx.enter_context(nc.Block())

        NORM_SCALE = {1: (w0["gamma"], w0["beta"]), 2: (ga["norm"], None), 3: (w1["g1"], w1["b1"]), 4: (w1["g2"], w1["b2"])}

        @block.sync
        def _(sp):
            sp.dma_start(tok_c[:, :], tok_w).then_inc(w_tok, 16)
            for t in range(T):
                sp.dma_start(frames[:, t], x[t].rearrange("p (w d) -> p w d", w=WIN)).then_inc(x_in[t], 16)
            if stop >= 1:
                sp.dma_start(l0_c[:, :], l0_w).then_inc(w_l0, 16)
                sp.dma_start(row_c[:, :], rows_w).then_inc(w_l0, 16)
                sp.dma_start(ga_c[:, :], ga_w).then_inc(w_ga, 16)
            if stop >= 2:
                sp.wait_ge(tok_pooled, T)
                for b in range(2):
                    sp.dma_start(gu_w[:, b], moe0_gu[b]).then_inc(gu_loaded[b], 16)
                    sp.dma_start(dn_w[:, b], moe0_dn[b]).then_inc(gu_loaded[b], 16)
                with sp.Fori(1, E // 2) as i:
                    for b in range(2):
                        sp.wait_ge(expert_used, i * 2 + (b - 1))
                        sp.dma_start(gu_w[:, b], moe0_gu[bass.ds(i * 2 + b, 1)].rearrange("o p k f -> p (o k) f")).then_inc(gu_loaded[b], 16)
                        sp.dma_start(dn_w[:, b], moe0_dn[bass.ds(i * 2 + b, 1)].rearrange("o p f d -> p (o f) d")).then_inc(gu_loaded[b], 16)
            if stop >= 4:
                sp.wait_ge(sh_added, T)
                sp.dma_start(l0_c[:, 0:L1_N], l1_w).then_inc(w_l1, 16)
            if stop >= 5:
                for b in range(2):
                    sp.wait_ge(expert_used, E - 1 + b)
                    sp.wait_ge(expert_used, E)
                    sp.dma_start(up_w[:, b], moe1_up[b]).then_inc(up_loaded[b], 16)
                    sp.dma_start(dn_w[:, b], moe1_dn[b]).then_inc(up_loaded[b], 16)
                with sp.Fori(1, E // 2) as i:
                    for b in range(2):
                        sp.wait_ge(up_used, i * 2 + (b - 1))
                        sp.dma_start(up_w[:, b], moe1_up[bass.ds(i * 2 + b, 1)].rearrange("o p k f -> p (o k) f")).then_inc(up_loaded[b], 16)
                        sp.dma_start(dn_w[:, b], moe1_dn[bass.ds(i * 2 + b, 1)].rearrange("o p f d -> p (o f) d")).then_inc(up_loaded[b], 16)
            done = {0: (h_ready, T), 1: (h_ready, 2 * T), 2: (combined, E * T), 3: (g_done, T), 4: (h_ready, 3 * T), 5: (combined1, E * T)}[min(stop, 5)]
            sp.wait_ge(*done)
            sp.dma_start(out.rearrange("(t p) d -> p t d", p=P), h).then_inc(out_done, 16)
            sp.wait_ge(out_done, 16)

        @block.tensor
        def _(pe):
            def mm(o, a, b, start, stop_, **kw):
                return nc.tensor.matmul(o, a, b, start=start, stop=stop_, **kw)

            def turn_cols(n):
                src = xh if n == 0 else ya
                for half in range(2):
                    pe.wait_ge(normed, n * T + HT * (half + 1))
                    for k in range(KD):
                        for i in range(HT):
                            last = nc.tensor.transpose(ps[:, 2 * half + k, P * i:P * i + P],
                                                       src[:, HT * half + i, P * k:P * k + P], ident)
                        last.then_inc(turned, 1)

            def project(n, w, bias):
                jd, ja = n * 16, n * 8
                for half in range(2):
                    pe.wait_ge(cols_ready, (0, 3)[n] * 4 + 2 * half + 2)
                    tok = slice(HALF * half, HALF * half + HALF)
                    for m in range(G):
                        if jd - n * 16 >= 2:
                            pe.wait_ge(qv_taken, jd - 1)
                        for k in range(KD):
                            last = mm(ps[:, 4 + jd % 2, :], w["wq"][:, k, P * m:P * m + P], xc[:, k, tok], k == 0, k == 1)
                        last.then_inc(qv_filled, 1)
                        jd += 1
                        if ja - n * 8 >= 2:
                            pe.wait_ge(k_taken, ja - 1)
                        for k in range(KD):
                            last = mm(ps[:, 6 + ja % 2, :], w["wk"][:, k, P * m:P * m + P], xc[:, k, tok], k == 0, k == 1)
                        last.then_inc(k_filled, 1)
                        ja += 1
                    for t in range(HT * half, HT * half + HT):
                        pe.wait_ge(qv_taken, jd - 1)
                        o = ps[:, 4 + jd % 2, 0:D]
                        for k in range(KD):
                            last = mm(o, xc[:, k, P * t:P * t + P], w["wv"][:, k, :], k == 0, k == 1 and not bias)
                        if bias:
                            last = mm(o, row["one"], row["wv"], False, True)
                        last.then_inc(qv_filled, 1)
                        jd += 1

            def attend(n, w, bias):
                pe.wait_ge(qv_taken, 16 * (n + 1))
                pe.wait_ge(k_taken, 8 * (n + 1))
                b0 = n * T

                def scores(t):
                    if t >= 1:
                        pe.wait_ge(score_taken, b0 + t)
                    for m in range(G):
                        for g in range(G):
                            for j in range(G):
                                tok = slice(P * t + 32 * g, P * t + 32 * g + 32)
                                c = 32 * m
                                last = mm(ps[32 * g:32 * g + 32, j, c:c + 32], qc[32 * j:32 * j + 32, m, tok],
                                          kc[32 * j:32 * j + 32, m, tok], True, True)
                    last.then_inc(scored, 1)

                def mix(t):
                    pe.wait_ge(probs_ready, b0 + t + 1)
                    if t >= 2:
                        pe.wait_ge(mix_copied, b0 + t - 1)
                    for hh in range(H):
                        for g in range(G):
                            c = HD * hh
                            q = slice(32 * g, 32 * g + 32)
                            last = mm(ps[q, 4 + t % 2, c:c + HD], pT[q, t % 2, (hh % G) * G + hh // G, :],
                                      v[q, t, HD * hh:HD * hh + HD], True, True)
                    last.then_inc(mixed, 1)

                def turn_mix(t):
                    pe.wait_ge(mix_copied, b0 + t + 1)
                    if t >= 1:
                        pe.wait_ge(mixT_copied, b0 + t)
                    for k in range(KD):
                        last = nc.tensor.transpose(ps[:, 6, P * k:P * k + P], ya[:, t, P * k:P * k + P], ident)
                    last.then_inc(mix_turned, 1)

                def out_proj(t):
                    pe.wait_ge(mixT_copied, b0 + t + 1)
                    if t >= 1:
                        pe.wait_ge(resid_ready, b0 + t)
                    o = ps[:, 7, 0:D]
                    for k in range(KD):
                        last = mm(o, oT[:, t % 2, k, :], w["wo"][:, k, :], k == 0, k == 1 and not bias)
                    if bias:
                        last = mm(o, row["one"], row["wo"], False, True)
                    last.then_inc(projected, 1)

                for i in range(T + 3):
                    if i < T:
                        scores(i)
                    if 1 <= i <= T:
                        mix(i - 1)
                    if 2 <= i <= T + 1:
                        turn_mix(i - 2)
                    if i >= 3:
                        out_proj(i - 3)

            def route(n, w):
                pe.wait_ge(cols_ready, (1, 4)[n] * 4 + 4)
                for t in range(T):
                    for k in range(KD):
                        last = mm(ps[:, 4, E * t:E * t + E], xc[:, k, P * t:P * t + P], w["router"][:, k, :], k == 0, k == 1)
                last.then_inc(routed, 1)

            pe.wait_ge(w_tok, 16)
            wk = part(tok_c, TOK_PACK, "wk", KD)
            qh = part(tok_c, TOK_PACK, "q", KD)
            wv = part(tok_c, TOK_PACK, "wv", KD)
            for m in range(KD):
                for k in range(KD):
                    last = mm(ps[:, 7, POOL_HEADS * m:POOL_HEADS * m + POOL_HEADS], wk[:, k, P * m:P * m + P], qh[:, k, :], k == 0, k == 1)
            last.then_inc(qk_sum, 1)
            for i in range(T + 1):
                if i < T:
                    pe.wait_ge(x_in[i], 16)
                    for b in range(4):
                        if i >= 1:
                            pe.wait_ge(xw_copied, 4 * (i - 1) + b + 1)
                        for c in range(4):
                            w, k = 2 * b + c // 2, c % 2
                            last = nc.tensor.transpose(ps[:, b, P * c:P * c + P], frames[:, i, w, P * k:P * k + P], ident)
                        last.then_inc(xw_turned, 1)
                if i >= 1:
                    t = i - 1
                    pe.wait_ge(tok_pooled, t + 1)
                    if t >= 1:
                        pe.wait_ge(pool_copied, t)
                    for k in range(KD):
                        last = nc.tensor.transpose(ps[:, 5, P * k:P * k + P], pooled[:, t % 2, P * k:P * k + P], ident)
                    last.then_inc(pool_turned, 1)
                if i < T:
                    if i == 0:
                        pe.wait_ge(qk_ready, 1)
                    pe.wait_ge(xw_copied, 4 * (i + 1))
                    if i >= 1:
                        pe.wait_ge(tok_score_taken, i)
                    for w in range(WIN):
                        for k in range(KD):
                            last = mm(ps[:, 4, POOL_HEADS * w:POOL_HEADS * w + POOL_HEADS], xwT[:, i % 2, 2 * w + k, :],
                                      qk[:, POOL_HEADS * k:POOL_HEADS * k + POOL_HEADS], k == 0, k == 1)
                    last.then_inc(tok_scored, 1)
                if i >= 1:
                    t = i - 1
                    pe.wait_ge(pool_copied, t + 1)
                    if t >= 2:
                        pe.wait_ge(h_ready, t - 1)
                    for k in range(KD):
                        last = mm(ps[:, 6, D * (t % 2):D * (t % 2) + D], plT[:, t % 2, k, :], wv[:, k, :], k == 0, k == 1)
                    last.then_inc(tok_out, 1)
            if stop < 1:
                return
            pe.wait_ge(w_l0, 32)
            turn_cols(0)
            project(0, w0, True)
            attend(0, w0, True)
            if stop < 2:
                return
            turn_cols(1)
            route(0, w0)
            for half in range(2):
                tok = slice(HALF * half, HALF * half + HALF)
                for fb in range(FS // P):
                    n = 2 * half + fb
                    if n >= 2:
                        pe.wait_ge(sh_hid, n - 1)
                    for part_, bank in ((0, n % 2), (1, 2 + n % 2)):
                        for k in range(KD):
                            c = FS * part_ + P * fb
                            if n < 2 and k == 0 and part_ == 0:
                                pe.wait_ge(cols_ready, 8)
                            last = mm(ps[:, bank, :], w0["sgu"][:, k, c:c + P], xc[:, k, tok], k == 0, k == 1)
                    last.then_inc(sh_filled, 1)
                for fb in range(FS // P):
                    pe.wait_ge(sh_hid, 2 * half + fb + 1)
                    if half == 0 and fb == 0:
                        pe.wait_ge(comb_ready, 1)
                    for i in range(HT):
                        o = ps[:, 4 + 2 * half + i // 2, D * (i % 2):D * (i % 2) + D]
                        last = mm(o, hid[:, fb, P * i:P * i + P], w0["sdn"][:, fb, :], fb == 0 and i % 2 == 0,
                                  fb == FS // P - 1, skip_group_check=True)
                last.then_inc(sh_down, 1)
            pe.wait_ge(sh_added, T)
            with pe.Fori(0, E // 2) as it:
                NB = 2 * 2 * FB
                def hidden(s):
                    b, half, fb = s // (2 * FB), s // FB % 2, s % FB
                    if s % (2 * FB) == 0:
                        pe.wait_ge(gu_loaded[b], it * 32 + 32)
                    pe_free = s - 1
                    if s >= 2:
                        pe.wait_ge(hid_ready, it * NB + pe_free)
                    tok = slice(HALF * half, HALF * half + HALF)
                    for part_, bank in ((0, s % 2), (1, 2 + s % 2)):
                        for k in range(KD):
                            c = F * part_ + P * fb
                            last = mm(ps[:, bank, :], gu_w[:, b, k, c:c + P], xc[:, k, tok], k == 0, k == 1)
                    last.then_inc(gu_filled, 1)

                def down(s):
                    b, half, fb = s // (2 * FB), s // FB % 2, s % FB
                    pe.wait_ge(hid_ready, it * NB + (s + 1))
                    if fb == 0:
                        unit = s // FB
                        if unit >= 2:
                            pe.wait_ge(combined, it * 4 * HT + HT * (unit - 1))
                    for i in range(HT):
                        o = ps[:, 4 + 2 * half + i // 2, D * (i % 2):D * (i % 2) + D]
                        last = mm(o, hid[:, s % 2, P * i:P * i + P], dn_w[:, b, fb, :], fb == 0 and i % 2 == 0,
                                  fb == FB - 1, skip_group_check=True)
                    if fb == FB - 1:
                        last.then_inc(down_filled, 1)
                        if half == 1:
                            pe.wait_ge(down_filled, it * 4 + (s // FB + 1))
                            pe.sem_inc(expert_used, 1)

                for s in range(NB):
                    hidden(s)
                    if s >= 1:
                        down(s - 1)
                down(NB - 1)
                pe.wait_ge(combined, it * 4 * HT + 4 * HT)
            if stop < 3:
                return
            turn_cols(2)
            pe.wait_ge(w_ga, 16)
            pe.wait_ge(cols_ready, 12)
            for half in range(2):
                for k in range(KD):
                    last = mm(ps[0:48, 6 + half, :], ga["xproj"][:, k, :], xc[:, k, HALF * half:HALF * half + HALF], k == 0, k == 1)
                last.then_inc(xd_filled, 1)
            pe.wait_ge(xd_copied, 2)
            for dk in range(KD):
                for half in range(2):
                    mm(ps[:, 2 * dk + half, :], dtw[:, P * dk:P * dk + P], xd[0:DTR, HALF * half:HALF * half + HALF],
                       True, True).then_inc(dt_filled, 1)
            for t in range(T):
                if t >= 2:
                    pe.wait_ge(gv_done, t - 1)
                o = ps[:, 4 + t % 2, 0:D]
                for k in range(KD):
                    mm(o, xc[:, k, P * t:P * t + P], ga["v"][:, k, :], k == 0, False)
                mm(o, row["one"], row["v"], False, True).then_inc(gv_filled, 1)
            pe.wait_ge(gv_done, T)

            def sum_states(n):
                for dk in range(KD):
                    pe.wait_ge(c_used, KD * n + dk + 1)
                    for half in range(2):
                        last = mm(ps[:, 2 * dk + half, :], ident, hC[:, dk, HALF * half:HALF * half + HALF],
                                  n == 0, n == NS - 1, skip_group_check=True)
                    last.then_inc(y_summed, 1)

            for n in range(NS):
                for r, bank, used, full in ((DTR + n, 4, b_used, b_spread), (DTR + NS + n, 6, c_used, c_spread)):
                    if n >= 1:
                        pe.wait_ge(used, KD * n)
                    for half in range(2):
                        last = mm(ps[:, bank + half, :], ident[0:48, r:r + 1].to_broadcast([48, P]),
                                  xd[:, HALF * half:HALF * half + HALF], True, True)
                    last.then_inc(full, 1)
                if n == 0:
                    pe.wait_ge(dt_log, 1)
                    pe.wait_ge(dt_relu, 4)
                if n >= 1:
                    sum_states(n - 1)
            sum_states(NS - 1)
            pe.wait_ge(rot_ready, 2)
            mm(ps[:, 4, 0:P], rot_a, rot_b, True, True).then_inc(rot_filled, 1)
            pe.wait_ge(mx_ready, 1)
            for j in range(6):
                m, half = j // 2, j % 2
                if j >= 2:
                    pe.wait_ge(zr_done, j - 1)
                for k in range(KD):
                    last = mm(ps[:, 6 + j % 2, :], ga["mx"][:, k, D + P * m:D + P * m + P],
                              mxT[:, k, HALF * half:HALF * half + HALF], k == 0, k == 1)
                last.then_inc(zr_filled, 1)
            pe.wait_ge(gbias_ready, 1)
            for t in range(T):
                if t >= 2:
                    pe.wait_ge(u_done, t - 1)
                o = ps[:, 4 + t % 2, 0:D]
                for k in range(KD):
                    mm(o, mxT[:, k, P * t:P * t + P], ga["mx"][:, k, 0:D], k == 0, False)
                mm(o, row["one"], row["u"], False, True).then_inc(u_filled, 1)
            pe.wait_ge(qk_cols, 2)
            pe.wait_ge(zr_done, 6)
            pe.wait_ge(u_done, T)
            for i in range(T + 3):
                if i < T:
                    t = i
                    if t >= 2:
                        pe.wait_ge(g_shifted, t - 1)
                    mm(ps[:, t % 2, 0:P], zq[:, P * t:P * t + P], zk[:, P * t:P * t + P], True, True).then_inc(g_scored, 1)
                if 1 <= i <= T:
                    t = i - 1
                    pe.wait_ge(g_probs, t + 1)
                    if t >= 2:
                        pe.wait_ge(g_copied, t - 1)
                    nc.tensor.transpose(ps[:, 2 + t % 2, 0:P], gsc[:, t % 2, :], ident).then_inc(g_turned, 1)
                if 2 <= i <= T + 1:
                    t = i - 2
                    pe.wait_ge(g_copied, t + 1)
                    if t >= 2:
                        pe.wait_ge(g_gated, t - 1)
                    for k in range(KD):
                        last = mm(ps[:, 4 + t % 2, P * k:P * k + P], v[:, t, P * k:P * k + P], gpT[:, t % 2, :], True, True)
                    last.then_inc(g_mixed, 1)
                if i >= 3:
                    t = i - 3
                    if t >= 2:
                        pe.wait_ge(g_silu, t - 1)
                    o = ps[:, 6 + t % 2, 0:D]
                    for k in range(KD):
                        mm(o, mxT[:, k, P * t:P * t + P], ga["mx"][:, k, 640:896], k == 0, False)
                    mm(o, row["one"], row["hx"], False, False)
                    mm(o, row["one"], row["h"], False, False)
                    pe.wait_ge(g_gated, t + 1)
                    for k in range(KD):
                        last = mm(o, ghr[:, t % 2, k, :], ga["h"][:, k, :], False, k == 1)
                    last.then_inc(g_out, 1)
            if stop < 4:
                return
            pe.wait_ge(g_done, T)
            turn_cols(3)
            pe.wait_ge(w_l1, 16)
            project(1, w1, False)
            attend(1, w1, False)
            if stop < 5:
                return
            turn_cols(4)
            route(1, w1)
            pe.wait_ge(comb_ready, 2)
            for t in range(T):
                bank = 4 + t // 4
                last = nc.tensor.transpose(ps[0:E, bank, P * (t % 4):P * (t % 4) + P], comb[:, E * t:E * t + E], ident)
            last.then_inc(comb_turned, 1)
            pe.wait_ge(comb_copied, 2)
            for t in range(T):
                mm(ps[:, t // 2, D * (t % 2):D * (t % 2) + D], combT[0:E, t, :], eb2[0:E, :], True, True).then_inc(bias_filled, 1)
            pe.wait_ge(bias_added, T)
            with pe.Fori(0, E // 2) as it:
                NB = 2 * 2 * FB

                def hidden1(s):
                    b, half, fb = s // (2 * FB), s // FB % 2, s % FB
                    if s % (2 * FB) == 0:
                        pe.wait_ge(up_loaded[b], it * 32 + 32)
                    if s >= 2:
                        pe.wait_ge(gelued, it * NB + (s - 1))
                    tok = slice(HALF * half, HALF * half + HALF)
                    for k in range(KD):
                        last = mm(ps[:, s % 2, :], up_w[:, b, k, P * fb:P * fb + P], xc[:, k, tok], k == 0, k == 1)
                    last.then_inc(up_filled, 1)

                def down1(s):
                    b, half, fb = s // (2 * FB), s // FB % 2, s % FB
                    pe.wait_ge(gelued, it * NB + (s + 1))
                    if fb == 0:
                        unit = s // FB
                        if unit >= 2:
                            pe.wait_ge(combined1, it * 4 * HT + HT * (unit - 1))
                    for i in range(HT):
                        o = ps[:, 4 + 2 * half + i // 2, D * (i % 2):D * (i % 2) + D]
                        last = mm(o, hid[:, s % 2, P * i:P * i + P], dn_w[:, b, fb, :], fb == 0 and i % 2 == 0,
                                  fb == FB - 1, skip_group_check=True)
                    if fb == FB - 1:
                        last.then_inc(down1_filled, 1)
                        if half == 1:
                            pe.wait_ge(down1_filled, it * 4 + (s // FB + 1))
                            pe.sem_inc(up_used, 1)

                for s in range(NB):
                    hidden1(s)
                    if s >= 1:
                        down1(s - 1)
                down1(NB - 1)
                pe.wait_ge(combined1, it * 4 * HT + 4 * HT)

        @block.scalar
        def _(act):
            steps = [0]

            def link(ins):
                steps[0] += 1
                ins.then_inc(act_step, 1)
                act.wait_ge(act_step, steps[0])

            def take_cols(n):
                for half in range(2):
                    for k in range(KD):
                        act.wait_ge(turned, n * 4 + 2 * half + k + 1)
                        o = xc[:, k, HALF * half:HALF * half + HALF]
                        if n == 0:
                            a = nc.scalar.copy(o, ps[:, 2 * half + k, :])
                        else:
                            g, b = NORM_SCALE[n]
                            a = nc.scalar.activation(o, ps[:, 2 * half + k, :], ACT.Identity, scale=g[:, k:k + 1],
                                                     bias=0.0 if b is None else b[:, k:k + 1])
                        a.then_inc(cols_ready, 1)

            def attend(n, w, bias):
                b0 = n * T
                for j in range(2 * G):
                    half, m = j // G, j % G
                    act.wait_ge(k_filled, n * 8 + j + 1)
                    nc.scalar.activation(kc[:, m, HALF * half:HALF * half + HALF], ps[:, 6 + j % 2, :], ACT.Identity,
                                         bias=w["bk"][:, m:m + 1] if bias else 0.0).then_inc(k_taken, 1)
                for i in range(T + 2):
                    if i < T:
                        act.wait_ge(shifted, b0 + i + 1)
                        nc.scalar.activation(sc[:, i % 2], sc[:, i % 2], ACT.Exp).then_inc(exped, 1)
                    if 1 <= i <= T:
                        t = i - 1
                        act.wait_ge(mixed, b0 + t + 1)
                        nc.scalar.copy(ya[:, t, :], ps[:, 4 + t % 2, 0:D]).then_inc(mix_copied, 1)
                    if i >= 2:
                        t = i - 2
                        act.wait_ge(mix_turned, b0 + t + 1)
                        if t >= 2:
                            act.wait_ge(projected, b0 + t - 1)
                        nc.scalar.copy(oT[:, t % 2].rearrange("p k n -> p (k n)"), ps[:, 6, 0:D]).then_inc(mixT_copied, 1)

            def route(n):
                act.wait_ge(top_diff, n + 1)
                nc.scalar.activation(wgt[:, 0:T], wgt[:, 2 * T:3 * T], ACT.Exp).then_inc(top_exp, 1)

            for t in range(T + 1):
                if t < T:
                    for b in range(4):
                        act.wait_ge(xw_turned, 4 * t + b + 1)
                        if t >= 2 and b == 0:
                            act.wait_ge(tok_scored, t - 1)
                        nc.scalar.copy(xwT[:, t % 2, 4 * b:4 * b + 4].rearrange("p w n -> p (w n)"), ps[:, b, :]).then_inc(xw_copied, 1)
                if t >= 1:
                    i = t - 1
                    act.wait_ge(pool_turned, i + 1)
                    if i >= 2:
                        act.wait_ge(tok_out, i - 1)
                    nc.scalar.copy(plT[:, i % 2].rearrange("p k n -> p (k n)"), ps[:, 5, 0:D]).then_inc(pool_copied, 1)
                if t < T:
                    act.wait_ge(tok_shift, t + 1)
                    a = tsc[:, 32 * (t % 2):32 * (t % 2) + 32]
                    nc.scalar.activation(a, a, ACT.Exp, scale=1.0 / 16).then_inc(tok_exp, 1)
            if stop < 1:
                return
            take_cols(0)
            attend(0, w0, True)
            if stop < 2:
                return
            take_cols(1)
            route(0)
            for n in range(4):
                act.wait_ge(sh_clipped, n + 1)
                nc.scalar.activation(gact[:, n % 2], gclip[:, n % 2], ACT.Silu).then_inc(sh_act, 1)
            act.wait_ge(sh_hid, 4)
            with act.Fori(0, E // 2) as it:
                NB = 4 * FB
                for s in range(NB):
                    act.wait_ge(clipped, it * NB + (s + 1))
                    if s >= 2:
                        act.wait_ge(hid_ready, it * NB + (s - 1))
                    nc.scalar.activation(gact[:, s % 2], gclip[:, s % 2], ACT.Silu).then_inc(silued, 1)
                act.wait_ge(hid_ready, it * NB + NB)
            if stop < 3:
                return
            act.wait_ge(w_ga, 16)
            take_cols(2)
            for half in range(2):
                act.wait_ge(xd_filled, half + 1)
                nc.scalar.copy(xd[:, HALF * half:HALF * half + HALF], ps[0:48, 6 + half, :]).then_inc(xd_copied, 1)
            for j in range(4):
                act.wait_ge(dt_filled, j + 1)
                last = nc.scalar.activation(fm[:, HALF * j:HALF * j + HALF], ps[:, j, :], ACT.Abs, bias=ga["dtb"][:, j // 2:j // 2 + 1])
                last.then_inc(dt_abs, 1)
            act.wait_ge(dt_abs, 4)
            link(nc.scalar.activation(fm[:, 0:2 * TOK], fm[:, 0:2 * TOK], ACT.Exp, scale=-1.0))
            nc.scalar.activation(fm[:, 2 * TOK:4 * TOK], fm[:, 0:2 * TOK], ACT.Ln, bias=1.0).then_inc(dt_log, 1)
            nc.scalar.activation(avec[:, :], ga["A"], ACT.Exp).then_inc(a_exp, 1)
            for t in range(T):
                act.wait_ge(gv_filled, t + 1)
                nc.scalar.activation(v[:, t, :], ps[:, 4 + t % 2, 0:D], ACT.Silu).then_inc(gv_done, 1)
            act.wait_ge(a_ready, 1)
            act.wait_ge(dtu_ready, 1)
            for n in range(NS):
                for dk in range(KD):
                    if n >= 1:
                        act.wait_ge(scanned, KD * (n - 1) + dk + 1)
                    later = "p (b s) -> p b s"
                    nc.scalar.activation(dA[:, dk, :].rearrange(later, s=S)[:, :, 1:S], dt[:, dk, :].rearrange(later, s=S)[:, :, 1:S], ACT.Exp,
                                         scale=avec[:, NS * dk + n:NS * dk + n + 1]).then_inc(decay, 1)
            act.wait_ge(y_ready, 4)
            nc.scalar.activation(mxT.rearrange("p k n -> p (k n)"), ypre.rearrange("p k n -> p (k n)"), ACT.Silu).then_inc(mx_ready, 1)
            for j in range(6):
                m, half = j // 2, j % 2
                act.wait_ge(zr_filled, j + 1)
                tok = slice(HALF * half, HALF * half + HALF)
                o = zT[:, tok] if m == 0 else rT[:, m - 1, tok]
                nc.scalar.activation(o, ps[:, 6 + j % 2, :], ACT.Silu, bias=ga["mxb"][:, m:m + 1]).then_inc(zr_done, 1)
            for t in range(T):
                act.wait_ge(u_filled, t + 1)
                nc.scalar.activation(ub[:, t, :], ps[:, 4 + t % 2, 0:D], ACT.Sigmoid).then_inc(u_done, 1)
            for i in range(T + 3):
                if i < T:
                    act.wait_ge(g_shifted, i + 1)
                    nc.scalar.activation(gsc[:, i % 2], gsc[:, i % 2], ACT.Exp, bias=smx[:, i % 2:i % 2 + 1],
                                         accum_out=ssum[:, i % 2:i % 2 + 1]).then_inc(g_exped, 1)
                if 1 <= i <= T:
                    t = i - 1
                    act.wait_ge(g_turned, t + 1)
                    if t >= 2:
                        act.wait_ge(g_mixed, t - 1)
                    nc.scalar.copy(gpT[:, t % 2], ps[:, 2 + t % 2, 0:P]).then_inc(g_copied, 1)
                if i >= 3:
                    t = i - 3
                    act.wait_ge(g_out, t + 1)
                    if t >= 2:
                        act.wait_ge(g_done, t - 1)
                    nc.scalar.activation(ghh[:, t % 2], ps[:, 6 + t % 2, 0:D], ACT.Silu).then_inc(g_silu, 1)
            if stop < 4:
                return
            act.wait_ge(w_l1, 16)
            take_cols(3)
            attend(1, w1, False)
            if stop < 5:
                return
            take_cols(4)
            route(1)
            with act.Fori(0, E // 2) as it:
                NB = 4 * FB
                nc.scalar.copy(eb_now[:, :], w1["eb1"].rearrange("p e f -> p (e f)")[:, bass.ds(it * (2 * FB), 2 * FB)]).then_inc(eb_copied, 1)
                act.wait_ge(eb_copied, it + 1)
                for s in range(NB):
                    b, half, fb = s // (2 * FB), s // FB % 2, s % FB
                    act.wait_ge(up_filled, it * NB + (s + 1))
                    nc.scalar.activation(hid[:, s % 2], ps[:, s % 2, :], ACT.Gelu_apprx_tanh,
                                         bias=eb_now[:, b * FB + fb:b * FB + fb + 1]).then_inc(gelued, 1)
                act.wait_ge(gelued, it * NB + NB)

        @block.gpsimd
        def _(pool):
            nc.gpsimd.memset(neghalf[:, :], -0.5).then_inc(consts, 1)
            pool.wait_ge(consts, 1)
            for n in range(6 if stop >= 5 else (0, 2, 3, 4, 5)[stop]):
                pool.wait_ge(var_ready, n + 1)
                nc.gpsimd.tensor_tensor(rs[:, :], ve[:, :], neghalf[:, :], ALU.pow).then_inc(rstd_ready, 1)

        @block.vector
        def _(dve):
            steps = [0]

            def link(ins):
                steps[0] += 1
                ins.then_inc(dve_step, 1)
                dve.wait_ge(dve_step, steps[0])

            mv3 = mv[:, :].rearrange("p (t c) -> p t c", c=2)
            ve3 = ve[:, :].rearrange("p (c t) -> p c t", c=2)
            stat3 = stat[:, :].rearrange("p (t c) -> p t c", c=6)
            norms = [0]

            def rstd(src):
                for t in range(T):
                    last = nc.vector.bn_stats(stat3[:, t, :], src[:, t, :])
                link(last)
                for t in range(T):
                    last = nc.vector.bn_aggr(mv3[:, t, :], stat3[:, t, :])
                link(last)
                nc.vector.tensor_scalar(ve3[:, 0, :], mv3[:, :, 1], EPS, None, ALU.add)
                norms[0] += 1
                nc.vector.tensor_scalar(ve3[:, 1, :], mv3[:, :, 1], 1.0 + EPS, EPS * EPS, ALU.mult, ALU.add).then_inc(var_ready, 1)
                dve.wait_ge(rstd_ready, norms[0])

            def norm_to(o, src, which, signal=None):
                for t in range(T):
                    last = nc.vector.tensor_scalar(o[:, t, :], src[:, t, :], mv3[:, t, 0:1], rs[:, T * which + t:T * which + t + 1],
                                                   ALU.subtract, ALU.mult)
                    if signal:
                        last.then_inc(signal, 1)
                if not signal:
                    link(last)

            def attend(n, w, bias):
                b0 = n * T
                jd = n * 16
                scale = 1.0 / 16 if bias else HD ** -0.5
                for half in range(2):
                    for m in range(G):
                        dve.wait_ge(qv_filled, jd + 1)
                        nc.vector.tensor_scalar(qc[:, m, HALF * half:HALF * half + HALF], ps[:, 4 + jd % 2, :],
                                                w["bq"][:, m:m + 1] if bias else 0.0, scale, ALU.add, ALU.mult).then_inc(qv_taken, 1)
                        jd += 1
                    for t in range(HT * half, HT * half + HT):
                        dve.wait_ge(qv_filled, jd + 1)
                        nc.vector.tensor_copy(v[:, t, :], ps[:, 4 + jd % 2, 0:D]).then_inc(qv_taken, 1)
                        jd += 1
                if bias:
                    link(nc.vector.tensor_tensor(rel, rel, mask32[:, :].unsqueeze(1).to_broadcast([P, H, 32]), ALU.add))
                for i in range(T + 3):
                    if i < T:
                        t = i
                        dve.wait_ge(scored, b0 + t + 1)
                        add = (rel.rearrange("p (j m) c -> p j m c", j=G) if bias
                               else mask32[:, :].unsqueeze(1).unsqueeze(1).to_broadcast([P, G, G, 32]))
                        nc.vector.tensor_tensor(sc[:, t % 2].rearrange("p (j m) c -> p j m c", j=G),
                                                ps[:, 0:G, 0:P].rearrange("p j (m c) -> p j m c", m=G), add, ALU.add).then_inc(score_taken, 1)
                        dve.wait_ge(score_taken, b0 + t + 1)
                        mx = smx[:, H * (t % 2):H * (t % 2) + H]
                        link(nc.vector.tensor_reduce(mx, sc[:, t % 2], AX.X, ALU.max))
                        nc.vector.tensor_tensor(sc[:, t % 2], sc[:, t % 2], mx.unsqueeze(2).to_broadcast([P, H, 32]),
                                                ALU.subtract).then_inc(shifted, 1)
                    if 1 <= i <= T:
                        t = i - 1
                        dve.wait_ge(exped, b0 + t + 1)
                        sm = ssum[:, H * (t % 2):H * (t % 2) + H]
                        link(nc.vector.tensor_reduce(sm, sc[:, t % 2], AX.X, ALU.add))
                        link(nc.vector.reciprocal(sm, sm))
                        link(nc.vector.tensor_tensor(sc[:, t % 2], sc[:, t % 2], sm.unsqueeze(2).to_broadcast([P, H, 32]), ALU.mult))
                        if t >= 2:
                            dve.wait_ge(mixed, b0 + t - 1)
                        nc.vector.transpose(pT[:, t % 2].rearrange("p h c -> p (h c)"), sc[:, t % 2].rearrange("p h c -> p (h c)")).then_inc(probs_ready, 1)
                    if i >= 3:
                        t = i - 3
                        dve.wait_ge(projected, b0 + t + 1)
                        nc.vector.tensor_tensor(ub[:, t, :], ps[:, 7, 0:D], xh[:, t, :], ALU.add).then_inc(resid_ready, 1)
                dve.wait_ge(resid_ready, b0 + T)

            def route(n):
                dve.wait_ge(routed, n + 1)
                link(nc.vector.tensor_copy(lg[:, :], ps[:, 4, 0:T * E]))
                for t in range(T):
                    last = nc.vector.max(top[:, 8 * t:8 * t + 8], lg[:, E * t:E * t + E])
                link(last)
                for t in range(T):
                    last = nc.vector.max_index(idx[:, 8 * t:8 * t + 8], top[:, 8 * t:8 * t + 8], lg[:, E * t:E * t + E])
                link(last)
                top3 = top[:, :].rearrange("p (t c) -> p t c", c=8)
                idx3 = idx[:, :].rearrange("p (t c) -> p t c", c=8)
                id3 = idf[:, :].rearrange("p (c t) -> p c t", c=2)
                w3 = wgt[:, :].rearrange("p (c t) -> p c t", c=3)
                nc.vector.tensor_tensor(w3[:, 2, :], top3[:, :, 1], top3[:, :, 0], ALU.subtract).then_inc(top_diff, 1)
                nc.vector.tensor_copy(id3[:, 0, :], idx3[:, :, 0])
                link(nc.vector.tensor_copy(id3[:, 1, :], idx3[:, :, 1]))
                dve.wait_ge(top_exp, n + 1)
                link(nc.vector.tensor_scalar(w3[:, 1, :], w3[:, 0, :], 1.0, None, ALU.add))
                link(nc.vector.reciprocal(w3[:, 1, :], w3[:, 1, :]))
                link(nc.vector.tensor_tensor(w3[:, 2, :], w3[:, 0, :], w3[:, 1, :], ALU.mult))
                c3 = comb[:, :].rearrange("p (t e) -> p t e", e=E)
                d3 = comb2[:, :].rearrange("p (t e) -> p t e", e=E)
                io = iota[:, :].unsqueeze(1).to_broadcast([P, T, E])
                nc.vector.tensor_tensor(c3, io, id3[:, 0, :].unsqueeze(2).to_broadcast([P, T, E]), ALU.is_equal)
                link(nc.vector.tensor_tensor(d3, io, id3[:, 1, :].unsqueeze(2).to_broadcast([P, T, E]), ALU.is_equal))
                nc.vector.tensor_tensor(c3, c3, w3[:, 1, :].unsqueeze(2).to_broadcast([P, T, E]), ALU.mult)
                link(nc.vector.tensor_tensor(d3, d3, w3[:, 2, :].unsqueeze(2).to_broadcast([P, T, E]), ALU.mult))
                nc.vector.tensor_tensor(c3, c3, d3, ALU.add).then_inc(comb_ready, 1)
                dve.wait_ge(comb_ready, n + 1)

            dve.wait_ge(qk_sum, 1)
            nc.vector.tensor_copy(qk[:, :], ps[:, 7, 0:KD * POOL_HEADS]).then_inc(qk_ready, 1)
            for i in range(T + 1):
                if i >= 1:
                    t = i - 1
                    a = tsc[:, 32 * (t % 2):32 * (t % 2) + 32].rearrange("p (w h) -> p w h", w=WIN)
                    sm = tsum[:, 4 * (t % 2):4 * (t % 2) + 4]
                    wb = wbar[:, WIN * (t % 2):WIN * (t % 2) + WIN]
                    dve.wait_ge(tok_exp, t + 1)
                    link(nc.vector.tensor_reduce(sm, a.rearrange("p w h -> p h w"), AX.X, ALU.add))
                    link(nc.vector.reciprocal(sm, sm))
                    link(nc.vector.tensor_tensor(a, a, sm.unsqueeze(1).to_broadcast([P, WIN, POOL_HEADS]), ALU.mult))
                    link(nc.vector.tensor_reduce(wb, a, AX.X, ALU.add))
                    link(nc.vector.tensor_scalar(wb, wb, 1.0 / POOL_HEADS, None, ALU.mult))
                    dve.wait_ge(x_in[t], 16)
                    if t >= 2:
                        dve.wait_ge(pool_turned, t - 1)
                    o = pooled[:, t % 2, :]
                    link(nc.vector.tensor_scalar(o, frames[:, t, 0, :], wb[:, 0:1], None, ALU.mult))
                    for w in range(1, WIN):
                        last = nc.vector.scalar_tensor_tensor(o, frames[:, t, w, :], wb[:, w:w + 1], o, ALU.mult, ALU.add)
                        if w < WIN - 1:
                            link(last)
                    last.then_inc(tok_pooled, 1)
                if i < T:
                    t = i
                    a = tsc[:, 32 * (t % 2):32 * (t % 2) + 32].rearrange("p (w h) -> p w h", w=WIN)
                    s = ps[:, 4, 0:32].rearrange("p (w h) -> p w h", w=WIN)
                    mx = tmx[:, 4 * (t % 2):4 * (t % 2) + 4]
                    dve.wait_ge(tok_scored, t + 1)
                    link(nc.vector.tensor_reduce(mx, s.rearrange("p w h -> p h w"), AX.X, ALU.max))
                    nc.vector.tensor_tensor(a, s, mx.unsqueeze(1).to_broadcast([P, WIN, POOL_HEADS]), ALU.subtract).then_inc(tok_shift, 1)
                    dve.wait_ge(tok_shift, t + 1)
                    dve.sem_inc(tok_score_taken, 1)
                if i >= 1:
                    t = i - 1
                    dve.wait_ge(tok_out, t + 1)
                    nc.vector.tensor_copy(h[:, t, :], ps[:, 6, D * (t % 2):D * (t % 2) + D]).then_inc(h_ready, 1)
            if stop < 1:
                return
            dve.wait_ge(h_ready, T)
            dve.wait_ge(w_l0, 32)
            nc.vector.tensor_copy(mask32[:, :], w0["mask32"])
            link(nc.vector.tensor_copy(iota[:, :], w0["iota"]))
            rstd(h)
            norm_to(xh, h, 0, normed)
            attend(0, w0, True)
            rstd(ub)
            norm_to(ub, ub, 0)
            ln_g, ln_b = (w0[n].unsqueeze(1).to_broadcast([P, HT, D]) for n in ("ln_g", "ln_b"))
            for half in range(2):
                r = slice(HT * half, HT * half + HT)
                link(nc.vector.tensor_tensor(ub[:, r], ub[:, r], ln_g, ALU.mult))
                link(nc.vector.tensor_tensor(ub[:, r], ub[:, r], ln_b, ALU.add))
                nc.vector.tensor_tensor(h[:, r], h[:, r], ub[:, r], ALU.add).then_inc(h_ready, HT)
            if stop < 2:
                return
            dve.wait_ge(h_ready, 2 * T)
            rstd(h)
            norm_to(ya, h, 1, normed)
            route(0)

            def gate_times_up(n, filled, clip_, acted, ready):
                def clip():
                    nc.vector.tensor_scalar(gclip[:, n % 2], ps[:, n % 2, :], -10.0, 10.0, ALU.max, ALU.min).then_inc(clip_, 1)

                def mult():
                    nc.vector.tensor_tensor(hid[:, n % 2], gact[:, n % 2], ps[:, 2 + n % 2, :], ALU.mult).then_inc(ready, 1)
                return clip, mult

            for n in range(4):
                clip, mult = gate_times_up(n, sh_filled, sh_clipped, sh_act, sh_hid)
                dve.wait_ge(sh_filled, n + 1)
                clip()
                dve.wait_ge(sh_act, n + 1)
                if n >= 2:
                    dve.wait_ge(sh_down, 1)
                mult()
            for t in range(T):
                dve.wait_ge(sh_down, t // HT + 1)
                nc.vector.tensor_tensor(h[:, t, :], ps[:, 4 + t // 2, D * (t % 2):D * (t % 2) + D], h[:, t, :], ALU.add).then_inc(sh_added, 1)
            dve.wait_ge(sh_added, T)
            with dve.Fori(0, E // 2) as it:
                NB = 4 * FB

                def combine(unit):
                    b, half = unit // 2, unit % 2
                    dve.wait_ge(down_filled, it * 4 + (unit + 1))
                    for i in range(HT):
                        t = HT * half + i
                        if unit >= 2:
                            dve.wait_ge(combined, it * 4 * HT + HT * (unit - 1))
                        nc.vector.scalar_tensor_tensor(h[:, t, :], ps[:, 4 + t // 2, D * (t % 2):D * (t % 2) + D],
                                                       comb[:, bass.ds(it * 2 + (E * t + b), 1)], h[:, t, :],
                                                       ALU.mult, ALU.add).then_inc(combined, 1)

                for s in range(NB + 1):
                    if s < NB:
                        clip, mult = gate_times_up(s, gu_filled, clipped, silued, hid_ready)
                        dve.wait_ge(gu_filled, it * NB + (s + 1))
                        if s >= 2:
                            dve.wait_ge(silued, it * NB + (s - 1))
                        clip()
                    if s >= 1:
                        p = s - 1
                        _, mult = gate_times_up(p, gu_filled, clipped, silued, hid_ready)
                        dve.wait_ge(silued, it * NB + (p + 1))
                        mult()
                    if s >= FB and s % FB == 2:
                        combine(s // FB - 1)
                combine(3)
                dve.wait_ge(combined, it * 4 * HT + 4 * HT)
            if stop < 3:
                return
            rstd(h)
            norm_to(xh, h, 0)
            norm_to(ya, h, 1, normed)
            dve.wait_ge(w_ga, 16)
            for j, (a, b) in enumerate((("al", "als"), ("be", "bes"))):
                link(nc.vector.tensor_scalar(rot[:, 0:S], ga["cos"], ga[a], None, ALU.mult))
                link(nc.vector.scalar_tensor_tensor(rot[:, S:2 * S], ga["sin"], ga[b], rot[:, 0:S], ALU.mult, ALU.add))
                o = (rot_a, rot_b)[j].rearrange("p (b s) -> p b s", s=S)
                nc.vector.tensor_copy(o, rot[:, S:2 * S].unsqueeze(1).to_broadcast([P, P // S, S])).then_inc(rot_ready, 1)
                dve.wait_ge(rot_ready, j + 1)
            for j in range(4):
                dve.wait_ge(dt_abs, j + 1)
                nc.vector.tensor_scalar(dt[:, j // 2, HALF * (j % 2):HALF * (j % 2) + HALF], ps[:, j, :],
                                        ga["dtb"][:, j // 2:j // 2 + 1], 0.0, ALU.add, ALU.max).then_inc(dt_relu, 1)
            dve.wait_ge(dt_relu, 4)
            dve.wait_ge(dt_log, 1)
            dtf = dt.rearrange("p k n -> p (k n)")
            link(nc.vector.tensor_tensor(dtf, dtf, fm[:, 2 * TOK:4 * TOK], ALU.add))
            dve.wait_ge(cols_ready, 12)
            link(nc.vector.tensor_tensor(dtu.rearrange("p k n -> p (k n)"), dtf, xc.rearrange("p k n -> p (k n)"), ALU.mult))
            nc.vector.memset(dA.rearrange("p k (b s) -> p (k b) s", s=S)[:, :, 0:1], 0.0).then_inc(dtu_ready, 1)
            dve.wait_ge(a_exp, 1)
            nc.vector.tensor_scalar(avec[:, :], avec[:, :], -1.0, None, ALU.mult).then_inc(a_ready, 1)
            for n in range(NS):
                dve.wait_ge(b_spread, n + 1)
                for dk in range(KD):
                    nc.vector.tensor_tensor(dBu[:, dk, :], dtu[:, dk, :], ps[:, 4:6, :].rearrange("p b n -> p (b n)"), ALU.mult).then_inc(b_used, 1)
                for dk in range(KD):
                    dve.wait_ge(b_used, KD * n + dk + 1)
                    dve.wait_ge(decay, KD * n + dk + 1)
                    nc.vector.tensor_tensor_scan(hs[:, dk, :], dA[:, dk, :], dBu[:, dk, :], 0.0, ALU.mult, ALU.add).then_inc(scanned, 1)
                dve.wait_ge(c_spread, n + 1)
                for dk in range(KD):
                    dve.wait_ge(scanned, KD * n + dk + 1)
                    if n >= 1:
                        dve.wait_ge(y_summed, KD * (n - 1) + dk + 1)
                    nc.vector.tensor_tensor(hC[:, dk, :], hs[:, dk, :], ps[:, 6:8, :].rearrange("p b n -> p (b n)"), ALU.mult).then_inc(c_used, 1)
            for j in range(4):
                dk, tok = j // 2, slice(HALF * (j % 2), HALF * (j % 2) + HALF)
                dve.wait_ge(y_summed, KD * (NS - 1) + dk + 1)
                nc.vector.scalar_tensor_tensor(ypre[:, dk, tok], xc[:, dk, tok], ga["D"][:, dk:dk + 1], ps[:, j, :],
                                               ALU.mult, ALU.add).then_inc(y_ready, 1)
            dve.wait_ge(rot_filled, 1)
            nc.vector.tensor_tensor(gbias, ps[:, 4, 0:P], ga["mask"], ALU.add).then_inc(gbias_ready, 1)
            dve.wait_ge(zr_done, 2)
            for j, o in enumerate((zq, zk)):
                nc.vector.tensor_scalar(o, zT, ga["gamma"][:, j:j + 1], ga["beta"][:, j:j + 1], ALU.mult, ALU.add).then_inc(qk_cols, 1)
            dve.wait_ge(gbias_ready, 1)
            for i in range(T + 4):
                if i < T:
                    t = i
                    dve.wait_ge(g_scored, t + 1)
                    link(nc.vector.scalar_tensor_tensor(gsc[:, t % 2], ps[:, t % 2, 0:P], Z ** -0.5, gbias, ALU.mult, ALU.add))
                    nc.vector.tensor_reduce(smx[:, t % 2:t % 2 + 1], gsc[:, t % 2], AX.X, ALU.max, negate=True).then_inc(g_shifted, 1)
                if 1 <= i <= T:
                    t = i - 1
                    dve.wait_ge(g_exped, t + 1)
                    sm = ssum[:, t % 2:t % 2 + 1]
                    link(nc.vector.reciprocal(sm, sm))
                    nc.vector.tensor_scalar(gsc[:, t % 2], gsc[:, t % 2], sm, None, ALU.mult).then_inc(g_probs, 1)
                if 2 <= i <= T + 1:
                    t = i - 2
                    dve.wait_ge(g_mixed, t + 1)
                    nc.vector.tensor_tensor(ghr[:, t % 2], ps[:, 4 + t % 2, 0:D].rearrange("p (k n) -> p k n", k=KD),
                                            rT[:, :, P * t:P * t + P], ALU.mult).then_inc(g_gated, 1)
                if i >= 4:
                    t = i - 4
                    dve.wait_ge(g_silu, t + 1)
                    o = ya[:, t, :]
                    link(nc.vector.tensor_tensor(o, ghh[:, t % 2], xh[:, t, :], ALU.subtract))
                    link(nc.vector.tensor_tensor(o, o, ub[:, t, :], ALU.mult))
                    link(nc.vector.tensor_tensor(o, o, xh[:, t, :], ALU.add))
                    nc.vector.tensor_tensor(h[:, t, :], h[:, t, :], o, ALU.add).then_inc(g_done, 1)
            if stop < 4:
                return
            dve.wait_ge(g_done, T)
            rstd(h)
            norm_to(xh, h, 0)
            norm_to(ya, h, 1, normed)
            attend(1, w1, False)
            for t in range(T):
                nc.vector.tensor_tensor(h[:, t, :], h[:, t, :], ub[:, t, :], ALU.add).then_inc(h_ready, 1)
            if stop < 5:
                return
            dve.wait_ge(h_ready, 3 * T)
            rstd(ub)
            norm_to(ya, ub, 0, normed)
            route(1)
            dve.wait_ge(comb_turned, 1)
            for j in range(2):
                nc.vector.tensor_copy(combT[0:E, 4 * j:4 * j + 4].rearrange("p t n -> p (t n)"), ps[0:E, 4 + j, :]).then_inc(comb_copied, 1)
            for t in range(T):
                dve.wait_ge(bias_filled, t // 2 * 2 + 2)
                nc.vector.tensor_tensor(h[:, t, :], ps[:, t // 2, D * (t % 2):D * (t % 2) + D], h[:, t, :], ALU.add).then_inc(bias_added, 1)
            dve.wait_ge(bias_added, T)
            with dve.Fori(0, E // 2) as it:
                for unit in range(4):
                    b, half = unit // 2, unit % 2
                    dve.wait_ge(down1_filled, it * 4 + (unit + 1))
                    for i in range(HT):
                        t = HT * half + i
                        if unit >= 2:
                            dve.wait_ge(combined1, it * 4 * HT + HT * (unit - 1))
                        nc.vector.scalar_tensor_tensor(h[:, t, :], ps[:, 4 + t // 2, D * (t % 2):D * (t % 2) + D],
                                                       comb[:, bass.ds(it * 2 + (E * t + b), 1)], h[:, t, :],
                                                       ALU.mult, ALU.add).then_inc(combined1, 1)
                dve.wait_ge(combined1, it * 4 * HT + 4 * HT)


STOP = 99


def kernel(**inp):
    import concourse.bacc as _bacc
    from concourse.bass_utils import run_bass_kernel_spmd as _run

    a = {k: np.asarray(v_) for k, v_ in inp.items()}
    f32 = np.float32

    def blocks(w):
        k, n = w.shape
        return w.reshape(k // P, P, n).transpose(1, 0, 2).reshape(P, -1)

    def per_feature(b):
        return b.reshape(-1, P).T

    def everywhere(b):
        return np.broadcast_to(b, (P, b.shape[-1]))

    def padded_heads(w):
        w = w.reshape(w.shape[0], H, HD)
        out = np.zeros((w.shape[0], H, 32), f32)
        out[:, :, :HD] = w
        return out.reshape(w.shape[0], H * 32)

    def on_rows(w, rows=P):
        out = np.zeros((rows, w.shape[1]), f32)
        out[:w.shape[0]] = w
        return out

    def pack(parts, where, n, rows=P):
        out = np.zeros((rows, n), f32)
        for name, (s, e) in where.items():
            out[:, s:e] = parts[name]
        return out

    x = np.zeros((CLIPS, P, D), f32)
    x[:, :FRAMES] = a["x"]
    x = x.reshape(T, P, WIN * D)

    tok_w = pack({"wk": blocks(a["L0_tok_Wk"]), "q": blocks(a["L0_tok_q"].T), "wv": blocks(a["L0_tok_Wv"].T),
                  "ident": np.eye(P, dtype=f32)}, TOK_PACK, TOK_N)

    tok = np.arange(P)
    same = (tok[:, None] // S == tok[None, :] // S) & (tok[None, :] <= tok[:, None])
    mask128 = np.where(same, 0.0, NEG).astype(f32)
    mask32 = np.stack([mask128[p, 32 * (p // 32):32 * (p // 32) + 32] for p in range(P)])
    half = Z // 2
    freqs = np.exp(np.arange(half, dtype=f32) * f32(-np.log(10000.0) / half)).astype(f32)
    ang = (np.arange(S, dtype=f32)[:, None] * freqs[None, :]).astype(f32)
    cos = np.concatenate([np.cos(ang), np.cos(ang)], 1).T.astype(f32)
    sin = np.concatenate([-np.sin(ang), np.sin(ang)], 1).T.astype(f32)

    rpb = a["L0_attn_rpb"]
    pos = np.clip(np.arange(32)[None, :] % S - tok[:, None] % S, -S + 1, S - 1) + S - 1
    heads = [G * m + j for j in range(G) for m in range(G)]
    rel = rpb[pos][:, :, heads].transpose(0, 2, 1).reshape(P, H * 32)
    w = a["L0_attn_W_w"]
    bq, bk, bv = np.split(a["L0_attn_W_b"], 3)
    l0_w = pack({
        "wq": blocks(padded_heads(w[0:D].T)), "wk": blocks(padded_heads(w[D:2 * D].T)), "wv": blocks(w[2 * D:].T),
        "wo": blocks(a["L0_attn_proj_w"].T), "bq": per_feature(padded_heads(bq[None])[0]),
        "bk": per_feature(padded_heads(bk[None])[0]), "rel": rel, "mask32": mask32,
        "ln_g": everywhere(a["L0_attn_ln_g"]), "ln_b": everywhere(a["L0_attn_ln_b"]),
        "gamma": per_feature(a["L0_ffn_ln_gamma"]), "beta": per_feature(a["L0_ffn_ln_beta"]),
        "router": blocks(a["L0_ffn_router_w"]), "sgu": blocks(a["L0_ffn_shared_gate_up_w"]),
        "sdn": blocks(a["L0_ffn_shared_down_w"]), "iota": everywhere(np.arange(E, dtype=f32))}, L0_PACK, L0_N)

    mx_b = a["L1_attn_mx_b"]
    swap = np.r_[half:Z, 0:half]
    al, be = a["L1_attn_alpha_rb"][0], a["L1_attn_beta_rb"][0]
    ga_w = pack({
        "norm": per_feature(a["L1_attn_norm_w"]), "v": blocks(a["L1_attn_v_w"].T), "mx": blocks(a["L1_attn_mx_w"].T),
        "mxb": per_feature(mx_b[D:D + 3 * P]), "h": blocks(a["L1_attn_h_w"].T), "xproj": blocks(a["L1_attn_xproj_w"].T),
        "dt": on_rows(a["L1_attn_dt_w"].T), "A": blocks(a["L1_attn_A_log"]), "D": per_feature(a["L1_attn_D_p"]),
        "dtb": per_feature(a["L1_attn_dt_b"]), "gamma": a["L1_attn_gamma"].T, "beta": a["L1_attn_beta"].T,
        "cos": cos, "sin": sin, "al": al[:, None], "als": al[swap][:, None], "be": be[:, None],
        "bes": be[swap][:, None], "mask": mask128}, GA_PACK, GA_N)

    wq, wk, wv = np.split(a["L1_ffn_w_qkv"], 3, axis=1)
    l1_w = pack({
        "wq": blocks(padded_heads(wq)), "wk": blocks(padded_heads(wk)), "wv": blocks(wv), "wo": blocks(a["L1_ffn_w_o"]),
        "g1": per_feature(a["L1_ffn_ln1_g"]), "b1": per_feature(a["L1_ffn_ln1_b"]),
        "g2": per_feature(a["L1_ffn_ln2_g"]), "b2": per_feature(a["L1_ffn_ln2_b"]), "router": blocks(a["L1_ffn_w_gate"]),
        "eb1": a["L1_ffn_b1"].reshape(E, FB, P).transpose(2, 0, 1).reshape(P, E * FB),
        "eb2": on_rows(a["L1_ffn_b2"])}, L1_PACK, L1_N)

    first = np.zeros((32, P), f32)
    first[0] = 1.0
    rows_w = pack({
        "one": first, "wv": on_rows(bv[None], 32), "wo": on_rows(a["L0_attn_proj_b"][None], 32),
        "v": on_rows(a["L1_attn_v_b"][None], 32), "u": on_rows(mx_b[None, 0:D], 32),
        "hx": on_rows(mx_b[None, 640:896], 32), "h": on_rows(a["L1_attn_h_b"][None], 32)}, ROW_PACK, ROW_N, 32)

    def expert_blocks(w3):
        e, k, n = w3.shape
        return np.ascontiguousarray(w3.reshape(e, k // P, P, n).transpose(0, 2, 1, 3))

    arrays = {
        "x": x, "tok_w": tok_w, "l0_w": l0_w, "ga_w": ga_w, "l1_w": l1_w, "rows_w": rows_w,
        "moe0_gu": expert_blocks(a["L0_ffn_gate_up_w"]), "moe0_dn": expert_blocks(a["L0_ffn_down_w"]),
        "moe1_up": expert_blocks(a["L1_ffn_w1"]), "moe1_dn": expert_blocks(a["L1_ffn_w2"])}

    nc = _bacc.Bacc("TRN2", target_bir_lowering=False, num_devices=1)
    args = [nc.dram_tensor(n, v_.shape, F32, kind="ExternalInput").ap() for n, v_ in arrays.items()]
    out = nc.dram_tensor("out", (TOK, D), F32, kind="ExternalOutput").ap()
    tower(nc, *args, out, stop=STOP)
    r = _run(nc, [arrays], core_ids=[0])
    return r.results[0]["out"].reshape(CLIPS, S, D)
```

```python
from contextlib import ExitStack

import numpy as np

import concourse.bass as bass
from concourse import mybir

F32 = mybir.dt.float32
U32 = mybir.dt.uint32
I32 = mybir.dt.int32
ALU = mybir.AluOpType
ACT = mybir.ActivationFunctionType
AX = mybir.AxisListType

P = 128
D = 256
KD = D // P
CLIPS, FRAMES, WIN = 64, 125, 8
S = 16
TOK = CLIPS * S
T = TOK // P
HALF = TOK // 2
HT = T // 2
POOL_HEADS = 4
H, HD = 16, 16
G = 4
E = 8
F = 1024
FB = F // P
FS = 256
Z = 128
NS = 16
DTR = 16
EPS = 1e-5
NEG = -1e30
TOP = 2
STEPS = TOP * TOK // P + E - 1
assert STEPS % 2 == 1


def layout(sizes):
    at, out = 0, {}
    for name, n in sizes:
        out[name] = (at, at + n)
        at += n
    return out, at


TOK_PACK, TOK_N = layout([("wk", KD * D), ("q", KD * POOL_HEADS), ("wv", KD * D), ("ident", P), ("tri", P), ("ones", P), ("steps", STEPS)])
L0_PACK, L0_N = layout([
    ("wq", KD * 512), ("wk", KD * 512), ("wv", KD * D), ("wo", KD * D), ("bq", G), ("bk", G),
    ("rel", H * 32), ("mask32", 32), ("ln_g", D), ("ln_b", D), ("gamma", KD), ("beta", KD),
    ("router", KD * E), ("sgu", KD * 2 * FS), ("sdn", FS // P * D), ("iota", E)])
GA_PACK, GA_N = layout([
    ("norm", KD), ("v", KD * D), ("mx", KD * 896), ("mxb", 3), ("h", KD * D), ("xproj", KD * 48),
    ("dt", D), ("A", KD * NS), ("D", KD), ("dtb", KD), ("gamma", 2), ("beta", 2),
    ("cos", S), ("sin", S), ("al", 1), ("als", 1), ("be", 1), ("bes", 1), ("mask", P)])
L1_PACK, L1_N = layout([
    ("wq", KD * 512), ("wk", KD * 512), ("wv", KD * D), ("wo", KD * D), ("g1", KD), ("b1", KD),
    ("g2", KD), ("b2", KD), ("router", KD * E), ("eb1", E * FB), ("eb2", D)])
ROW_PACK, ROW_N = layout([
    ("one", P), ("wv", D), ("wo", D), ("v", D), ("u", D), ("hx", D), ("h", D)])


def tower(nc, x, tok_w, l0_w, ga_w, l1_w, rows_w, moe0_gu, moe0_dn, moe1_up, moe1_dn, out, sorted_x, sorted_y, stop=99):
    ctx = ExitStack()
    with ctx:
        def sb(name, cols, rows=P, dt=F32):
            return ctx.enter_context(nc.sbuf_tensor(name, [rows, cols], dt))

        def sem(name):
            return ctx.enter_context(nc.semaphore(name))

        big = sb("big", T * WIN * D)
        tok_c = sb("tok_c", TOK_N)
        l0_c = sb("l0_c", L0_N)
        ga_c = sb("ga_c", GA_N)
        row_c = sb("row_c", ROW_N, rows=32)
        h_ = sb("h_rows", T * D)
        rows_ = sb("rows", 4 * T * D)
        xc_ = sb("x_cols", KD * TOK)
        fm = sb("fm", 8 * TOK)
        stat = sb("stat", T * 6)
        mv = sb("mv", T * 2)
        ve = sb("ve", T * 2)
        rs = sb("rs", T * 2)
        neghalf = sb("neghalf", T * 2)
        smx = sb("smx", 2 * H)
        ssum = sb("ssum", 2 * H)
        tsc = sb("tsc", 2 * WIN * POOL_HEADS)
        tmx = sb("tmx", 2 * POOL_HEADS)
        tsum = sb("tsum", 2 * POOL_HEADS)
        wbar = sb("wbar", 2 * WIN)
        qk = sb("qk", KD * POOL_HEADS)
        lg = sb("lg", T * E)
        top = sb("top", T * 8)
        idx = sb("idx", T * 8, dt=U32)
        idf = sb("idf", T * 2)
        wgt = sb("wgt", T * 3)
        pick = sb("pick", 2 * T * E)
        both = sb("both", T * E)
        posn = sb("posn", T * E)
        comb = sb("comb", T * E)
        plan = sb("plan", 4 * E)
        plan_i = sb("plan_i", E, dt=I32)
        ends = sb("ends", E, dt=I32)
        step_e = sb("step_e", STEPS, dt=I32)
        step_b = sb("step_b", STEPS, dt=I32)
        step_f = sb("step_f", STEPS)
        step_c = sb("step_c", STEPS * E)
        slot_f = sb("slot_f", 2 * T)
        slot = sb("slot", 2 * T, dt=U32)
        zero = sb("zero", D)
        avec = sb("avec", KD * NS)
        eb_now = sb("eb_now", 2 * FB)
        rot = sb("rot", 4 * S)

        def rows3(a):
            return a[:, 0:T * D].rearrange("p (t d) -> p t d", t=T)

        h = rows3(h_)
        xh, ya, v, ub = (rows3(rows_[:, i * T * D:(i + 1) * T * D]) for i in range(4))
        y_all = rows_[:, 0:STEPS * D].rearrange("p (s d) -> p s d", d=D)
        xc = xc_[:, :].rearrange("p (k n) -> p k n", k=KD)
        frames = big[:, :].rearrange("p (t w d) -> p t w d", t=T, w=WIN)
        tail = 12288
        assert tail == 2 * (KD * 2 * F + FB * D)
        gu_w = big[:, 0:2 * KD * 2 * F].rearrange("p (b k f) -> p b k f", b=2, k=KD)
        up_w = big[:, 0:2 * KD * F].rearrange("p (b k f) -> p b k f", b=2, k=KD)
        dn_w = big[:, 2 * KD * 2 * F:tail].rearrange("p (b f d) -> p b f d", b=2, f=FB)
        gclip = big[:, tail:tail + 1024].rearrange("p (b n) -> p b n", b=2)
        gact = big[:, tail + 1024:tail + 2048].rearrange("p (b n) -> p b n", b=2)
        hid = big[:, tail + 2048:tail + 3072].rearrange("p (b n) -> p b n", b=2)
        sc = big[:, tail:tail + 1024].rearrange("p (b h c) -> p b h c", b=2, c=32)
        pT = big[:, tail + 1024:tail + 2048].rearrange("p (b h c) -> p b h c", b=2, c=32)
        oT = big[:, tail + 2048:tail + 2560].rearrange("p (b k n) -> p b k n", b=2, k=KD)
        gsc = big[:, tail:tail + 256].rearrange("p (b n) -> p b n", b=2)
        gpT = big[:, tail + 256:tail + 512].rearrange("p (b n) -> p b n", b=2)
        ghr = big[:, tail + 512:tail + 1024].rearrange("p (b k n) -> p b k n", b=2, k=KD)
        ghh = big[:, tail + 1024:tail + 1536].rearrange("p (b n) -> p b n", b=2)
        gbias = big[:, tail + 1536:tail + 1664]
        rot_a = big[:, tail + 1664:tail + 1792]
        rot_b = big[:, tail + 1792:tail + 1920]
        xg_now = big[:, tail + 3072:tail + 3584].rearrange("p (b d) -> p b d", b=2)
        xgT = big[:, tail + 3584:tail + 4096].rearrange("p (b k n) -> p b k n", b=2, k=KD)
        xg = fm[:, 0:(STEPS + 1) * D].rearrange("p (s d) -> p s d", d=D)
        hidT = fm[:, (STEPS + 1) * D:].rearrange("p (b f n) -> p b f n", b=2, f=FB)
        yg = fm[:, 0:2 * T * D].rearrange("p (c t d) -> p c t d", c=2, t=T)
        combT = big[:, tail + 3072:tail + 4096].rearrange("p (t n) -> p t n", t=T)
        qc = fm[:, 0:4 * TOK].rearrange("p (m n) -> p m n", m=4)
        kc = fm[:, 4 * TOK:].rearrange("p (m n) -> p m n", m=4)
        xwT = fm[:, 0:4096].rearrange("p (b w n) -> p b w n", b=2, w=2 * WIN)
        plT = fm[:, 4096:4608].rearrange("p (b k n) -> p b k n", b=2, k=KD)
        pooled = fm[:, 4608:5120].rearrange("p (b d) -> p b d", b=2)
        scan4 = fm[:, :].rearrange("p (a k n) -> p a k n", a=4, k=KD)
        dA, dBu, hs, hC = scan4[:, 0], scan4[:, 1], scan4[:, 2], scan4[:, 3]
        mxT = fm[:, 0:2048].rearrange("p (k n) -> p k n", k=KD)
        rT = fm[:, 2048:4096].rearrange("p (k n) -> p k n", k=KD)
        zT = fm[:, 4096:5120]
        zq = fm[:, 5120:6144]
        zk = fm[:, 6144:7168]
        ypre = xc
        dt = rows_[:, T * D:2 * T * D].rearrange("p (k n) -> p k n", k=KD)
        dtu = rows_[:, 3 * T * D:].rearrange("p (k n) -> p k n", k=KD)
        xd = sb("xd", TOK, rows=48)

        def part(tensor, where, name, k=None, rows=P):
            a, b = where[name]
            ap = tensor[0:rows, a:b]
            return ap.rearrange("p (k n) -> p k n", k=k) if k else ap

        ident = part(tok_c, TOK_PACK, "ident")
        w0 = {n: part(l0_c, L0_PACK, n, k) for n, k in (
            ("wq", KD), ("wk", KD), ("wv", KD), ("wo", KD), ("bq", None), ("bk", None), ("mask32", None),
            ("ln_g", None), ("ln_b", None), ("gamma", None), ("beta", None), ("router", KD), ("sgu", KD),
            ("sdn", FS // P), ("iota", None))}
        rel = part(l0_c, L0_PACK, "rel").rearrange("p (h c) -> p h c", c=32)
        w1 = {n: part(l0_c, L1_PACK, n, k) for n, k in (
            ("wq", KD), ("wk", KD), ("wv", KD), ("wo", KD), ("g1", None), ("b1", None), ("g2", None),
            ("b2", None), ("router", KD), ("eb1", E))}
        eb2 = part(l0_c, L1_PACK, "eb2", rows=32)
        ga = {n: part(ga_c, GA_PACK, n, k) for n, k in (
            ("norm", None), ("v", KD), ("mx", KD), ("mxb", None), ("h", KD), ("xproj", KD), ("A", None),
            ("D", None), ("dtb", None), ("gamma", None), ("beta", None), ("cos", None), ("sin", None),
            ("al", None), ("als", None), ("be", None), ("bes", None), ("mask", None))}
        dtw = part(ga_c, GA_PACK, "dt", rows=DTR)
        row = {n: part(row_c, ROW_PACK, n, rows=32) for n in ROW_PACK}
        mask32 = sb("mask32", 32)
        iota = sb("iota", E)

        ps = ctx.enter_context(nc.psum_tensor("ps", [P, 8, 512], F32))

        w_tok, w_l0, w_ga, w_l1 = sem("w_tok"), sem("w_l0"), sem("w_ga"), sem("w_l1")
        x_in = [sem(f"x_in{t}") for t in range(T)]
        out_done = sem("out_done")
        dve_step, act_step, pool_step = sem("dve_step"), sem("act_step"), sem("pool_step")
        consts = sem("consts")
        qk_sum, qk_ready = sem("qk_sum"), sem("qk_ready")
        xw_turned, xw_copied, tok_scored, tok_shift = (sem(n) for n in ("xw_turned", "xw_copied", "tok_scored", "tok_shift"))
        tok_exp, tok_pooled, pool_turned, pool_copied = (sem(n) for n in ("tok_exp", "tok_pooled", "pool_turned", "pool_copied"))
        tok_out, h_ready, tok_score_taken = sem("tok_out"), sem("h_ready"), sem("tok_score_taken")
        var_ready, rstd_ready, normed, turned, cols_ready = (sem(n) for n in ("var_ready", "rstd_ready", "normed", "turned", "cols_ready"))
        qv_filled, qv_taken, k_filled, k_taken = (sem(n) for n in ("qv_filled", "qv_taken", "k_filled", "k_taken"))
        scored, shifted, exped, probs_ready = (sem(n) for n in ("scored", "shifted", "exped", "probs_ready"))
        score_taken = sem("score_taken")
        mixed, mix_copied, mix_turned, mixT_copied, projected, resid_ready = (
            sem(n) for n in ("mixed", "mix_copied", "mix_turned", "mixT_copied", "projected", "resid_ready"))
        routed, top_diff, top_exp, comb_ready = (sem(n) for n in ("routed", "top_diff", "top_exp", "comb_ready"))
        sh_filled, sh_clipped, sh_act, sh_hid, sh_down, sh_added = (
            sem(n) for n in ("sh_filled", "sh_clipped", "sh_act", "sh_hid", "sh_down", "sh_added"))
        both_ready, ranked, slots_ready, zeroed, zero_ready = (
            sem(n) for n in ("both_ready", "ranked", "slots_ready", "zeroed", "zero_ready"))
        expert_in = [sem(f"expert_in{b}") for b in range(2)]
        moe = {k: sem(k) for k in (
            "expert_ready", "scattered", "xg_now_ready", "xg_turned", "xgT_ready", "gu_filled", "clipped",
            "silued", "hid_ready", "hid_turned", "hidT_ready", "bias_now_ready", "y_filled", "y_taken", "y_stored", "added")}
        xg_in = [sem(f"xg_in{c}") for c in range(3)]
        gathered = [sem(f"gathered{c}") for c in range(4)]
        comb_turned, comb_copied, bias_filled, bias_added = (
            sem(n) for n in ("comb_turned", "comb_copied", "bias_filled", "bias_added"))
        gv_filled, gv_done, xd_filled, xd_copied = (sem(n) for n in ("gv_filled", "gv_done", "xd_filled", "xd_copied"))
        dt_filled, dt_abs, dt_log, dt_relu, dtu_ready, a_exp, a_ready = (
            sem(n) for n in ("dt_filled", "dt_abs", "dt_log", "dt_relu", "dtu_ready", "a_exp", "a_ready"))
        b_spread, c_spread, decay, b_used, c_used, scanned, y_summed = (
            sem(n) for n in ("b_spread", "c_spread", "decay", "b_used", "c_used", "scanned", "y_summed"))
        y_ready, mx_ready, zr_filled, zr_done, qk_cols, u_filled, u_done = (
            sem(n) for n in ("y_ready", "mx_ready", "zr_filled", "zr_done", "qk_cols", "u_filled", "u_done"))
        rot_ready, rot_filled, gbias_ready = sem("rot_ready"), sem("rot_filled"), sem("gbias_ready")
        g_scored, g_shifted, g_exped, g_probs, g_turned, g_copied = (
            sem(n) for n in ("g_scored", "g_shifted", "g_exped", "g_probs", "g_turned", "g_copied"))
        g_mixed, g_gated, g_out, g_silu, g_done = (sem(n) for n in ("g_mixed", "g_gated", "g_out", "g_silu", "g_done"))

        block = ctx.enter_context(nc.Block())

        XG_PARTS = ((0, 2), (2, 8), (8, STEPS + 1))
        NORM_SCALE = {1: (w0["gamma"], w0["beta"]), 2: (ga["norm"], None), 3: (w1["g1"], w1["b1"]), 4: (w1["g2"], w1["b2"])}

        @block.sync
        def _(sp):
            W = ((gu_w, moe0_gu), (up_w, moe1_up))

            def load_expert(n, e, b):
                sbuf, dram = W[n]
                dn = (moe0_dn, moe1_dn)[n]
                ix = bass.ds(e, 1)
                sp.dma_start(sbuf[:, b], dram[ix].rearrange("o p k f -> p (o k) f")).then_inc(expert_in[b], 16)
                sp.dma_start(dn_w[:, b], dn[ix].rearrange("o p f d -> p (o f) d")).then_inc(expert_in[b], 16)

            def first_experts(n):
                if n == 1:
                    sp.wait_ge(moe["y_filled"], STEPS + 1)
                for b in range(2):
                    load_expert(n, b, b)
                    sp.wait_ge(expert_in[b], n * 16 * E + 32)
                    sp.sem_inc(moe["expert_ready"], 1)

            def serve_experts(n):
                sp.wait_ge(moe["scattered"], n * 16 * 2 * T + (16 * 2 * T))
                src = sorted_x[n].rearrange("(s p) d -> p s d", p=P)
                for c, (a, b) in enumerate(XG_PARTS):
                    sp.dma_start(xg[:, a:b], src[:, a:b]).then_inc(xg_in[c], 16)
                with sp.Fori(0, E // 2 - 1) as i:
                    for b in range(2):
                        end = sp.value_load(ends[0:1, bass.ds(i * 2 + b, 1)], min_val=0, max_val=STEPS)
                        sp.wait_ge(moe["y_filled"], n * (STEPS + 1) + (end + 1))
                        load_expert(n, i * 2 + (b + 2), b)
                        sp.wait_ge(expert_in[b], i * 32 + (n * 16 * E + 64))
                        sp.sem_inc(moe["expert_ready"], 1)

            sp.dma_start(tok_c[:, :], tok_w).then_inc(w_tok, 16)
            for t in range(T):
                sp.dma_start(frames[:, t], x[t].rearrange("p (w d) -> p w d", w=WIN)).then_inc(x_in[t], 16)
            if stop >= 1:
                sp.dma_start(l0_c[:, :], l0_w).then_inc(w_l0, 16)
                sp.dma_start(row_c[:, :], rows_w).then_inc(w_l0, 16)
                sp.dma_start(ga_c[:, :], ga_w).then_inc(w_ga, 16)
                sp.wait_ge(zero_ready, 1)
                for n in range(2):
                    sp.dma_start(sorted_x[n].rearrange("(s p) d -> p s d", p=P),
                                 zero[:, :].unsqueeze(1).to_broadcast([P, STEPS + 1, D])).then_inc(zeroed, 16)
            if stop >= 2:
                sp.wait_ge(tok_pooled, T)
                first_experts(0)
                serve_experts(0)
            if stop >= 4:
                sp.wait_ge(sh_added, T)
                sp.dma_start(l0_c[:, 0:L1_N], l1_w).then_inc(w_l1, 16)
            if stop >= 5:
                first_experts(1)
                serve_experts(1)
            done = {0: (h_ready, T), 1: (h_ready, 2 * T), 2: (moe["added"], 2 * T), 3: (g_done, T), 4: (h_ready, 3 * T), 5: (moe["added"], 4 * T)}[min(stop, 5)]
            sp.wait_ge(*done)
            sp.dma_start(out.rearrange("(t p) d -> p t d", p=P), h).then_inc(out_done, 16)
            sp.wait_ge(out_done, 16)

        @block.tensor
        def _(pe):
            def mm(o, a, b, start, stop_, **kw):
                return nc.tensor.matmul(o, a, b, start=start, stop=stop_, **kw)

            def turn_cols(n):
                src = xh if n == 0 else ya
                for half in range(2):
                    pe.wait_ge(normed, n * T + HT * (half + 1))
                    for k in range(KD):
                        for i in range(HT):
                            last = nc.tensor.transpose(ps[:, 2 * half + k, P * i:P * i + P],
                                                       src[:, HT * half + i, P * k:P * k + P], ident)
                        last.then_inc(turned, 1)

            def project(n, w, bias):
                jd, ja = n * 16, n * 8
                for half in range(2):
                    pe.wait_ge(cols_ready, (0, 3)[n] * 4 + 2 * half + 2)
                    tok = slice(HALF * half, HALF * half + HALF)
                    for m in range(G):
                        if jd - n * 16 >= 2:
                            pe.wait_ge(qv_taken, jd - 1)
                        for k in range(KD):
                            last = mm(ps[:, 4 + jd % 2, :], w["wq"][:, k, P * m:P * m + P], xc[:, k, tok], k == 0, k == 1)
                        last.then_inc(qv_filled, 1)
                        jd += 1
                        if ja - n * 8 >= 2:
                            pe.wait_ge(k_taken, ja - 1)
                        for k in range(KD):
                            last = mm(ps[:, 6 + ja % 2, :], w["wk"][:, k, P * m:P * m + P], xc[:, k, tok], k == 0, k == 1)
                        last.then_inc(k_filled, 1)
                        ja += 1
                    for t in range(HT * half, HT * half + HT):
                        pe.wait_ge(qv_taken, jd - 1)
                        o = ps[:, 4 + jd % 2, 0:D]
                        for k in range(KD):
                            last = mm(o, xc[:, k, P * t:P * t + P], w["wv"][:, k, :], k == 0, k == 1 and not bias)
                        if bias:
                            last = mm(o, row["one"], row["wv"], False, True)
                        last.then_inc(qv_filled, 1)
                        jd += 1

            def attend(n, w, bias):
                pe.wait_ge(qv_taken, 16 * (n + 1))
                pe.wait_ge(k_taken, 8 * (n + 1))
                b0 = n * T

                def scores(t):
                    if t >= 1:
                        pe.wait_ge(score_taken, b0 + t)
                    for m in range(G):
                        for g in range(G):
                            for j in range(G):
                                tok = slice(P * t + 32 * g, P * t + 32 * g + 32)
                                c = 32 * m
                                last = mm(ps[32 * g:32 * g + 32, j, c:c + 32], qc[32 * j:32 * j + 32, m, tok],
                                          kc[32 * j:32 * j + 32, m, tok], True, True)
                    last.then_inc(scored, 1)

                def mix(t):
                    pe.wait_ge(probs_ready, b0 + t + 1)
                    if t >= 2:
                        pe.wait_ge(mix_copied, b0 + t - 1)
                    for hh in range(H):
                        for g in range(G):
                            c = HD * hh
                            q = slice(32 * g, 32 * g + 32)
                            last = mm(ps[q, 4 + t % 2, c:c + HD], pT[q, t % 2, (hh % G) * G + hh // G, :],
                                      v[q, t, HD * hh:HD * hh + HD], True, True)
                    last.then_inc(mixed, 1)

                def turn_mix(t):
                    pe.wait_ge(mix_copied, b0 + t + 1)
                    if t >= 1:
                        pe.wait_ge(mixT_copied, b0 + t)
                    for k in range(KD):
                        last = nc.tensor.transpose(ps[:, 6, P * k:P * k + P], ya[:, t, P * k:P * k + P], ident)
                    last.then_inc(mix_turned, 1)

                def out_proj(t):
                    pe.wait_ge(mixT_copied, b0 + t + 1)
                    if t >= 1:
                        pe.wait_ge(resid_ready, b0 + t)
                    o = ps[:, 7, 0:D]
                    for k in range(KD):
                        last = mm(o, oT[:, t % 2, k, :], w["wo"][:, k, :], k == 0, k == 1 and not bias)
                    if bias:
                        last = mm(o, row["one"], row["wo"], False, True)
                    last.then_inc(projected, 1)

                for i in range(T + 3):
                    if i < T:
                        scores(i)
                    if 1 <= i <= T:
                        mix(i - 1)
                    if 2 <= i <= T + 1:
                        turn_mix(i - 2)
                    if i >= 3:
                        out_proj(i - 3)

            def route(n, w):
                pe.wait_ge(cols_ready, (1, 4)[n] * 4 + 4)
                for t in range(T):
                    for k in range(KD):
                        last = mm(ps[:, 4, E * t:E * t + E], xc[:, k, P * t:P * t + P], w["router"][:, k, :], k == 0, k == 1)
                last.then_inc(routed, 1)

            def rank(n):
                pe.wait_ge(both_ready, n + 1)
                o = ps[:, 5, 0:T * E]
                for j in range(1, T):
                    mm(o[:, j * E:], ones, both[:, 0:(T - j) * E], j == 1, False, skip_group_check=True)
                mm(o, part(tok_c, TOK_PACK, "tri"), both[:, :], False, True, skip_group_check=True)
                for t in range(T):
                    last = mm(ps[:, 6, 0:E], ones, both[:, t * E:(t + 1) * E], t == 0, t == T - 1)
                last.then_inc(ranked, 1)

            def experts(n):
                w_in = (gu_w, up_w)[n]

                def turn_x(s):
                    pe.wait_ge(moe["xg_now_ready"], n * (STEPS + 1) + (s + 1))
                    return s

                def turn_x_to(b):
                    for k in range(KD):
                        last = nc.tensor.transpose(ps[:, 6, P * k:P * k + P], xg_now[:, b, P * k:P * k + P], ident)
                    last.then_inc(moe["xg_turned"], 1)

                def hidden(s, b, first):
                    e = pe.value_load(step_e[0:1, bass.ds(s, 1)], min_val=0, max_val=E - 1)
                    buf = pe.value_load(step_b[0:1, bass.ds(s, 1)], min_val=0, max_val=1)
                    pe.wait_ge(moe["expert_ready"], n * E + (e + 1))
                    pe.wait_ge(moe["xgT_ready"], n * (STEPS + 1) + (s + 1))
                    w = w_in[:, bass.ds(buf, 1)]
                    for j in range(2):
                        if not first:
                            pe.wait_ge(moe["hid_ready"], n * 2 * STEPS + (s * 2 + (j - 1)))
                        for part_ in range(2 - n):
                            for k in range(KD):
                                c = F * part_ + 512 * j
                                last = mm(ps[:, 2 * part_ + j, :], xgT[:, b, k, :],
                                          w[:, :, k, c:c + 512].rearrange("p o c -> p (o c)"), k == 0, k == 1)
                        last.then_inc(moe["gu_filled"], 1)

                def turn_hidden(s, j, first):
                    pe.wait_ge(moe["hid_ready"], n * 2 * STEPS + (s * 2 + (j + 1)))
                    if not first:
                        pe.wait_ge(moe["hidT_ready"], n * 2 * STEPS + (s * 2 + (j - 1)))
                    for i in range(4):
                        last = nc.tensor.transpose(ps[:, 4 + j, P * i:P * i + P], hid[:, j, P * i:P * i + P], ident)
                    last.then_inc(moe["hid_turned"], 1)

                def down(s, b):
                    buf = pe.value_load(step_b[0:1, bass.ds(s, 1)], min_val=0, max_val=1)
                    pe.wait_ge(moe["hidT_ready"], n * 2 * STEPS + (s * 2 + 2))
                    pe.wait_ge(moe["y_taken"], n * (STEPS + 1) + (s + 1))
                    w = dn_w[:, bass.ds(buf, 1)]
                    for f in range(FB):
                        last = mm(ps[:, 7, 0:D], hidT[:, b, f, :], w[:, :, f, :].rearrange("p o d -> p (o d)"), f == 0, f == FB - 1)
                    last.then_inc(moe["y_filled"], 1)

                pe.wait_ge(slots_ready, n + 1)
                pe.sem_inc(moe["y_filled"], 1)
                turn_x(0)
                turn_x_to(0)
                hidden(0, 0, True)
                turn_hidden(0, 0, True)
                pe.wait_ge(moe["xgT_ready"], n * (STEPS + 1) + (1))
                turn_x(1)
                turn_x_to(1)
                turn_hidden(0, 1, True)
                with pe.Fori(0, STEPS // 2) as it:
                    for u in range(2):
                        s, b = it * 2 + (u + 1), (u + 1) % 2
                        hidden(s, b, False)
                        turn_hidden(s, 0, False)
                        down(it * 2 + u, 1 - b)
                        pe.wait_ge(moe["xgT_ready"], n * (STEPS + 1) + (s + 1))
                        turn_x(s + 1)
                        turn_x_to(1 - b)
                        turn_hidden(s, 1, False)
                down(STEPS - 1, (STEPS - 1) % 2)

            pe.wait_ge(w_tok, 16)
            ones = part(tok_c, TOK_PACK, "ones")
            wk = part(tok_c, TOK_PACK, "wk", KD)
            qh = part(tok_c, TOK_PACK, "q", KD)
            wv = part(tok_c, TOK_PACK, "wv", KD)
            for m in range(KD):
                for k in range(KD):
                    last = mm(ps[:, 7, POOL_HEADS * m:POOL_HEADS * m + POOL_HEADS], wk[:, k, P * m:P * m + P], qh[:, k, :], k == 0, k == 1)
            last.then_inc(qk_sum, 1)
            for i in range(T + 1):
                if i < T:
                    pe.wait_ge(x_in[i], 16)
                    for b in range(4):
                        if i >= 1:
                            pe.wait_ge(xw_copied, 4 * (i - 1) + b + 1)
                        for c in range(4):
                            w, k = 2 * b + c // 2, c % 2
                            last = nc.tensor.transpose(ps[:, b, P * c:P * c + P], frames[:, i, w, P * k:P * k + P], ident)
                        last.then_inc(xw_turned, 1)
                if i >= 1:
                    t = i - 1
                    pe.wait_ge(tok_pooled, t + 1)
                    if t >= 1:
                        pe.wait_ge(pool_copied, t)
                    for k in range(KD):
                        last = nc.tensor.transpose(ps[:, 5, P * k:P * k + P], pooled[:, t % 2, P * k:P * k + P], ident)
                    last.then_inc(pool_turned, 1)
                if i < T:
                    if i == 0:
                        pe.wait_ge(qk_ready, 1)
                    pe.wait_ge(xw_copied, 4 * (i + 1))
                    if i >= 1:
                        pe.wait_ge(tok_score_taken, i)
                    for w in range(WIN):
                        for k in range(KD):
                            last = mm(ps[:, 4, POOL_HEADS * w:POOL_HEADS * w + POOL_HEADS], xwT[:, i % 2, 2 * w + k, :],
                                      qk[:, POOL_HEADS * k:POOL_HEADS * k + POOL_HEADS], k == 0, k == 1)
                    last.then_inc(tok_scored, 1)
                if i >= 1:
                    t = i - 1
                    pe.wait_ge(pool_copied, t + 1)
                    if t >= 2:
                        pe.wait_ge(h_ready, t - 1)
                    for k in range(KD):
                        last = mm(ps[:, 6, D * (t % 2):D * (t % 2) + D], plT[:, t % 2, k, :], wv[:, k, :], k == 0, k == 1)
                    last.then_inc(tok_out, 1)
            if stop < 1:
                return
            pe.wait_ge(w_l0, 32)
            turn_cols(0)
            project(0, w0, True)
            attend(0, w0, True)
            if stop < 2:
                return
            turn_cols(1)
            route(0, w0)
            rank(0)
            for half in range(2):
                tok = slice(HALF * half, HALF * half + HALF)
                for fb in range(FS // P):
                    n = 2 * half + fb
                    if n >= 2:
                        pe.wait_ge(sh_hid, n - 1)
                    for part_, bank in ((0, n % 2), (1, 2 + n % 2)):
                        for k in range(KD):
                            c = FS * part_ + P * fb
                            if n < 2 and k == 0 and part_ == 0:
                                pe.wait_ge(cols_ready, 8)
                            last = mm(ps[:, bank, :], w0["sgu"][:, k, c:c + P], xc[:, k, tok], k == 0, k == 1)
                    last.then_inc(sh_filled, 1)
                for fb in range(FS // P):
                    pe.wait_ge(sh_hid, 2 * half + fb + 1)
                    if half == 0 and fb == 0:
                        pe.wait_ge(slots_ready, 1)
                    for i in range(HT):
                        o = ps[:, 4 + 2 * half + i // 2, D * (i % 2):D * (i % 2) + D]
                        last = mm(o, hid[:, fb, P * i:P * i + P], w0["sdn"][:, fb, :], fb == 0 and i % 2 == 0,
                                  fb == FS // P - 1, skip_group_check=True)
                last.then_inc(sh_down, 1)
            pe.wait_ge(sh_added, T)
            experts(0)
            if stop < 3:
                return
            turn_cols(2)
            pe.wait_ge(w_ga, 16)
            pe.wait_ge(cols_ready, 12)
            for half in range(2):
                for k in range(KD):
                    last = mm(ps[0:48, 6 + half, :], ga["xproj"][:, k, :], xc[:, k, HALF * half:HALF * half + HALF], k == 0, k == 1)
                last.then_inc(xd_filled, 1)
            pe.wait_ge(xd_copied, 2)
            for dk in range(KD):
                for half in range(2):
                    mm(ps[:, 2 * dk + half, :], dtw[:, P * dk:P * dk + P], xd[0:DTR, HALF * half:HALF * half + HALF],
                       True, True).then_inc(dt_filled, 1)
            for t in range(T):
                if t >= 2:
                    pe.wait_ge(gv_done, t - 1)
                o = ps[:, 4 + t % 2, 0:D]
                for k in range(KD):
                    mm(o, xc[:, k, P * t:P * t + P], ga["v"][:, k, :], k == 0, False)
                mm(o, row["one"], row["v"], False, True).then_inc(gv_filled, 1)
            pe.wait_ge(gv_done, T)

            def sum_states(n):
                for dk in range(KD):
                    pe.wait_ge(c_used, KD * n + dk + 1)
                    for half in range(2):
                        last = mm(ps[:, 2 * dk + half, :], ident, hC[:, dk, HALF * half:HALF * half + HALF],
                                  n == 0, n == NS - 1, skip_group_check=True)
                    last.then_inc(y_summed, 1)

            for n in range(NS):
                for r, bank, used, full in ((DTR + n, 4, b_used, b_spread), (DTR + NS + n, 6, c_used, c_spread)):
                    if n >= 1:
                        pe.wait_ge(used, KD * n)
                    for half in range(2):
                        last = mm(ps[:, bank + half, :], ident[0:48, r:r + 1].to_broadcast([48, P]),
                                  xd[:, HALF * half:HALF * half + HALF], True, True)
                    last.then_inc(full, 1)
                if n == 0:
                    pe.wait_ge(dt_log, 1)
                    pe.wait_ge(dt_relu, 4)
                if n >= 1:
                    sum_states(n - 1)
            sum_states(NS - 1)
            pe.wait_ge(rot_ready, 2)
            mm(ps[:, 4, 0:P], rot_a, rot_b, True, True).then_inc(rot_filled, 1)
            pe.wait_ge(mx_ready, 1)
            for j in range(6):
                m, half = j // 2, j % 2
                if j >= 2:
                    pe.wait_ge(zr_done, j - 1)
                for k in range(KD):
                    last = mm(ps[:, 6 + j % 2, :], ga["mx"][:, k, D + P * m:D + P * m + P],
                              mxT[:, k, HALF * half:HALF * half + HALF], k == 0, k == 1)
                last.then_inc(zr_filled, 1)
            pe.wait_ge(gbias_ready, 1)
            for t in range(T):
                if t >= 2:
                    pe.wait_ge(u_done, t - 1)
                o = ps[:, 4 + t % 2, 0:D]
                for k in range(KD):
                    mm(o, mxT[:, k, P * t:P * t + P], ga["mx"][:, k, 0:D], k == 0, False)
                mm(o, row["one"], row["u"], False, True).then_inc(u_filled, 1)
            pe.wait_ge(qk_cols, 2)
            pe.wait_ge(zr_done, 6)
            pe.wait_ge(u_done, T)
            for i in range(T + 3):
                if i < T:
                    t = i
                    if t >= 2:
                        pe.wait_ge(g_shifted, t - 1)
                    mm(ps[:, t % 2, 0:P], zq[:, P * t:P * t + P], zk[:, P * t:P * t + P], True, True).then_inc(g_scored, 1)
                if 1 <= i <= T:
                    t = i - 1
                    pe.wait_ge(g_probs, t + 1)
                    if t >= 2:
                        pe.wait_ge(g_copied, t - 1)
                    nc.tensor.transpose(ps[:, 2 + t % 2, 0:P], gsc[:, t % 2, :], ident).then_inc(g_turned, 1)
                if 2 <= i <= T + 1:
                    t = i - 2
                    pe.wait_ge(g_copied, t + 1)
                    if t >= 2:
                        pe.wait_ge(g_gated, t - 1)
                    for k in range(KD):
                        last = mm(ps[:, 4 + t % 2, P * k:P * k + P], v[:, t, P * k:P * k + P], gpT[:, t % 2, :], True, True)
                    last.then_inc(g_mixed, 1)
                if i >= 3:
                    t = i - 3
                    if t >= 2:
                        pe.wait_ge(g_silu, t - 1)
                    o = ps[:, 6 + t % 2, 0:D]
                    for k in range(KD):
                        mm(o, mxT[:, k, P * t:P * t + P], ga["mx"][:, k, 640:896], k == 0, False)
                    mm(o, row["one"], row["hx"], False, False)
                    mm(o, row["one"], row["h"], False, False)
                    pe.wait_ge(g_gated, t + 1)
                    for k in range(KD):
                        last = mm(o, ghr[:, t % 2, k, :], ga["h"][:, k, :], False, k == 1)
                    last.then_inc(g_out, 1)
            if stop < 4:
                return
            pe.wait_ge(g_done, T)
            turn_cols(3)
            pe.wait_ge(w_l1, 16)
            project(1, w1, False)
            attend(1, w1, False)
            if stop < 5:
                return
            turn_cols(4)
            route(1, w1)
            rank(1)
            pe.wait_ge(comb_ready, 1)
            for t in range(T):
                bank = 4 + t // 4
                last = nc.tensor.transpose(ps[0:E, bank, P * (t % 4):P * (t % 4) + P], comb[:, E * t:E * t + E], ident)
            last.then_inc(comb_turned, 1)
            pe.wait_ge(comb_copied, 2)
            for t in range(T):
                mm(ps[:, t // 2, D * (t % 2):D * (t % 2) + D], combT[0:E, t, :], eb2[0:E, :], True, True).then_inc(bias_filled, 1)
            pe.wait_ge(bias_added, T)
            experts(1)

        @block.scalar
        def _(act):
            steps = [0]

            def link(ins):
                steps[0] += 1
                ins.then_inc(act_step, 1)
                act.wait_ge(act_step, steps[0])

            def take_cols(n):
                for half in range(2):
                    for k in range(KD):
                        act.wait_ge(turned, n * 4 + 2 * half + k + 1)
                        o = xc[:, k, HALF * half:HALF * half + HALF]
                        if n == 0:
                            a = nc.scalar.copy(o, ps[:, 2 * half + k, :])
                        else:
                            g, b = NORM_SCALE[n]
                            a = nc.scalar.activation(o, ps[:, 2 * half + k, :], ACT.Identity, scale=g[:, k:k + 1],
                                                     bias=0.0 if b is None else b[:, k:k + 1])
                        a.then_inc(cols_ready, 1)

            def attend(n, w, bias):
                b0 = n * T
                for j in range(2 * G):
                    half, m = j // G, j % G
                    act.wait_ge(k_filled, n * 8 + j + 1)
                    nc.scalar.activation(kc[:, m, HALF * half:HALF * half + HALF], ps[:, 6 + j % 2, :], ACT.Identity,
                                         bias=w["bk"][:, m:m + 1] if bias else 0.0).then_inc(k_taken, 1)
                for i in range(T + 2):
                    if i < T:
                        act.wait_ge(shifted, b0 + i + 1)
                        nc.scalar.activation(sc[:, i % 2], sc[:, i % 2], ACT.Exp).then_inc(exped, 1)
                    if 1 <= i <= T:
                        t = i - 1
                        act.wait_ge(mixed, b0 + t + 1)
                        nc.scalar.copy(ya[:, t, :], ps[:, 4 + t % 2, 0:D]).then_inc(mix_copied, 1)
                    if i >= 2:
                        t = i - 2
                        act.wait_ge(mix_turned, b0 + t + 1)
                        if t >= 2:
                            act.wait_ge(projected, b0 + t - 1)
                        nc.scalar.copy(oT[:, t % 2].rearrange("p k n -> p (k n)"), ps[:, 6, 0:D]).then_inc(mixT_copied, 1)

            def route(n):
                act.wait_ge(top_diff, n + 1)
                nc.scalar.activation(wgt[:, 0:T], wgt[:, 2 * T:3 * T], ACT.Exp).then_inc(top_exp, 1)

            def experts(n):

                def take_x(s, b, first):
                    act.wait_ge(moe["xg_turned"], n * (STEPS + 1) + (s + 1))
                    if not first:
                        act.wait_ge(moe["gu_filled"], n * 2 * STEPS + (s * 2 - 2))
                    g, shift = NORM_SCALE[(1, 4)[n]]
                    for k in range(KD):
                        last = nc.scalar.activation(xgT[:, b, k, :], ps[:, 6, P * k:P * k + P], ACT.Identity,
                                                    scale=g[:, k:k + 1], bias=shift[:, k:k + 1])
                    last.then_inc(moe["xgT_ready"], 1)

                def bias_now(s, b):
                    e = act.value_load(step_e[0:1, bass.ds(s, 1)], min_val=0, max_val=E - 1)
                    nc.scalar.copy(eb_now[:, b * FB:b * FB + FB], w1["eb1"].rearrange("p e f -> p (e f)")[:, bass.ds(e * FB, FB)]).then_inc(moe["bias_now_ready"], 1)

                def act_on(s, j, first):
                    act.wait_ge(moe["clipped"], s * 2 + (j + 1))
                    if not first:
                        act.wait_ge(moe["hid_ready"], n * 2 * STEPS + (s * 2 + (j - 1)))
                    nc.scalar.activation(gact[:, j], gclip[:, j], ACT.Silu).then_inc(moe["silued"], 1)

                def take_hidden(s, j, b, first):
                    act.wait_ge(moe["hid_turned"], n * 2 * STEPS + (s * 2 + (j + 1)))
                    if not first:
                        act.wait_ge(moe["y_filled"], n * (STEPS + 1) + (s))
                    if n == 0:
                        nc.scalar.copy(hidT[:, b, 4 * j:4 * j + 4].rearrange("p f n -> p (f n)"), ps[:, 4 + j, :]).then_inc(moe["hidT_ready"], 1)
                        return
                    if j == 0:
                        act.wait_ge(moe["bias_now_ready"], s + 1)
                    for i in range(4):
                        last = nc.scalar.activation(hidT[:, b, 4 * j + i, :], ps[:, 4 + j, P * i:P * i + P], ACT.Gelu_apprx_tanh,
                                                    bias=eb_now[:, b * FB + 4 * j + i:b * FB + 4 * j + i + 1])
                    last.then_inc(moe["hidT_ready"], 1)

                def store(s):
                    act.wait_ge(moe["y_taken"], n * (STEPS + 1) + (s + 2))
                    act.dma_start(sorted_y[n].rearrange("(s p) d -> p s d", p=P)[:, bass.ds(s, 1), :],
                                  y_all[:, bass.ds(s, 1), :]).then_inc(moe["y_stored"], 16)

                take_x(0, 0, True)
                if n == 1:
                    bias_now(0, 0)
                for j in range(2):
                    if n == 0:
                        act_on(0, j, True)
                take_hidden(0, 0, 0, True)
                take_x(1, 1, True)
                take_hidden(0, 1, 0, True)
                with act.Fori(0, STEPS // 2) as it:
                    for u in range(2):
                        s, b = it * 2 + (u + 1), (u + 1) % 2
                        if n == 1:
                            bias_now(s, b)
                        for j in range(2):
                            if n == 0:
                                act_on(s, j, False)
                        take_hidden(s, 0, b, False)
                        take_x(s + 1, 1 - b, False)
                        take_hidden(s, 1, b, False)
                        store(it * 2 + u)
                store(STEPS - 1)

            for t in range(T + 1):
                if t < T:
                    for b in range(4):
                        act.wait_ge(xw_turned, 4 * t + b + 1)
                        if t >= 2 and b == 0:
                            act.wait_ge(tok_scored, t - 1)
                        nc.scalar.copy(xwT[:, t % 2, 4 * b:4 * b + 4].rearrange("p w n -> p (w n)"), ps[:, b, :]).then_inc(xw_copied, 1)
                if t >= 1:
                    i = t - 1
                    act.wait_ge(pool_turned, i + 1)
                    if i >= 2:
                        act.wait_ge(tok_out, i - 1)
                    nc.scalar.copy(plT[:, i % 2].rearrange("p k n -> p (k n)"), ps[:, 5, 0:D]).then_inc(pool_copied, 1)
                if t < T:
                    act.wait_ge(tok_shift, t + 1)
                    a = tsc[:, 32 * (t % 2):32 * (t % 2) + 32]
                    nc.scalar.activation(a, a, ACT.Exp, scale=1.0 / 16).then_inc(tok_exp, 1)
            if stop < 1:
                return
            take_cols(0)
            attend(0, w0, True)
            if stop < 2:
                return
            take_cols(1)
            route(0)
            for n in range(4):
                act.wait_ge(sh_clipped, n + 1)
                nc.scalar.activation(gact[:, n % 2], gclip[:, n % 2], ACT.Silu).then_inc(sh_act, 1)
            act.wait_ge(sh_hid, 4)
            experts(0)
            if stop < 3:
                return
            act.wait_ge(w_ga, 16)
            take_cols(2)
            for half in range(2):
                act.wait_ge(xd_filled, half + 1)
                nc.scalar.copy(xd[:, HALF * half:HALF * half + HALF], ps[0:48, 6 + half, :]).then_inc(xd_copied, 1)
            for j in range(4):
                act.wait_ge(dt_filled, j + 1)
                last = nc.scalar.activation(fm[:, HALF * j:HALF * j + HALF], ps[:, j, :], ACT.Abs, bias=ga["dtb"][:, j // 2:j // 2 + 1])
                last.then_inc(dt_abs, 1)
            act.wait_ge(dt_abs, 4)
            link(nc.scalar.activation(fm[:, 0:2 * TOK], fm[:, 0:2 * TOK], ACT.Exp, scale=-1.0))
            nc.scalar.activation(fm[:, 2 * TOK:4 * TOK], fm[:, 0:2 * TOK], ACT.Ln, bias=1.0).then_inc(dt_log, 1)
            nc.scalar.activation(avec[:, :], ga["A"], ACT.Exp).then_inc(a_exp, 1)
            for t in range(T):
                act.wait_ge(gv_filled, t + 1)
                nc.scalar.activation(v[:, t, :], ps[:, 4 + t % 2, 0:D], ACT.Silu).then_inc(gv_done, 1)
            act.wait_ge(a_ready, 1)
            act.wait_ge(dtu_ready, 1)
            for n in range(NS):
                for dk in range(KD):
                    if n >= 1:
                        act.wait_ge(scanned, KD * (n - 1) + dk + 1)
                    later = "p (b s) -> p b s"
                    nc.scalar.activation(dA[:, dk, :].rearrange(later, s=S)[:, :, 1:S], dt[:, dk, :].rearrange(later, s=S)[:, :, 1:S], ACT.Exp,
                                         scale=avec[:, NS * dk + n:NS * dk + n + 1]).then_inc(decay, 1)
            act.wait_ge(y_ready, 4)
            nc.scalar.activation(mxT.rearrange("p k n -> p (k n)"), ypre.rearrange("p k n -> p (k n)"), ACT.Silu).then_inc(mx_ready, 1)
            for j in range(6):
                m, half = j // 2, j % 2
                act.wait_ge(zr_filled, j + 1)
                tok = slice(HALF * half, HALF * half + HALF)
                o = zT[:, tok] if m == 0 else rT[:, m - 1, tok]
                nc.scalar.activation(o, ps[:, 6 + j % 2, :], ACT.Silu, bias=ga["mxb"][:, m:m + 1]).then_inc(zr_done, 1)
            for t in range(T):
                act.wait_ge(u_filled, t + 1)
                nc.scalar.activation(ub[:, t, :], ps[:, 4 + t % 2, 0:D], ACT.Sigmoid).then_inc(u_done, 1)
            for i in range(T + 3):
                if i < T:
                    act.wait_ge(g_shifted, i + 1)
                    nc.scalar.activation(gsc[:, i % 2], gsc[:, i % 2], ACT.Exp, bias=smx[:, i % 2:i % 2 + 1],
                                         accum_out=ssum[:, i % 2:i % 2 + 1]).then_inc(g_exped, 1)
                if 1 <= i <= T:
                    t = i - 1
                    act.wait_ge(g_turned, t + 1)
                    if t >= 2:
                        act.wait_ge(g_mixed, t - 1)
                    nc.scalar.copy(gpT[:, t % 2], ps[:, 2 + t % 2, 0:P]).then_inc(g_copied, 1)
                if i >= 3:
                    t = i - 3
                    act.wait_ge(g_out, t + 1)
                    if t >= 2:
                        act.wait_ge(g_done, t - 1)
                    nc.scalar.activation(ghh[:, t % 2], ps[:, 6 + t % 2, 0:D], ACT.Silu).then_inc(g_silu, 1)
            if stop < 4:
                return
            act.wait_ge(w_l1, 16)
            take_cols(3)
            attend(1, w1, False)
            if stop < 5:
                return
            take_cols(4)
            route(1)
            experts(1)

        @block.gpsimd
        def _(pool):
            nc.gpsimd.memset(neghalf[:, :], -0.5).then_inc(consts, 1)
            nc.gpsimd.memset(zero[:, :], 0.0).then_inc(zero_ready, 1)
            pool.wait_ge(consts, 1)
            norms = [0]

            def rstd(count):
                for _ in range(count):
                    norms[0] += 1
                    pool.wait_ge(var_ready, norms[0])
                    nc.gpsimd.tensor_tensor(rs[:, :], ve[:, :], neghalf[:, :], ALU.pow).then_inc(rstd_ready, 1)

            def dispatch(n):
                pool.wait_ge(zeroed, 32)
                pool.wait_ge(slots_ready, n + 1)
                for t in range(T):
                    for c in range(TOP):
                        pool.indirect_dma_start(sorted_x[n], bass.IndirectOffsetOnAxis(slot[:, c * T + t:c * T + t + 1], 0),
                                                ya[:, t, :], None).then_inc(moe["scattered"], 16)
                pool.wait_ge(moe["y_stored"], n * 16 * STEPS + (16 * STEPS))
                for t in range(T):
                    for c in range(TOP):
                        pool.indirect_dma_start(yg[:, c, t, :], None, sorted_y[n],
                                                bass.IndirectOffsetOnAxis(slot[:, c * T + t:c * T + t + 1], 0)).then_inc(gathered[t // 2], 16)

            if stop >= 1:
                rstd(2)
            if stop >= 2:
                rstd(1)
                dispatch(0)
            if stop >= 3:
                rstd(1)
            if stop >= 4:
                rstd(1)
            if stop >= 5:
                rstd(1)
                dispatch(1)

        @block.vector
        def _(dve):
            steps = [0]

            def link(ins):
                steps[0] += 1
                ins.then_inc(dve_step, 1)
                dve.wait_ge(dve_step, steps[0])

            mv3 = mv[:, :].rearrange("p (t c) -> p t c", c=2)
            ve3 = ve[:, :].rearrange("p (c t) -> p c t", c=2)
            stat3 = stat[:, :].rearrange("p (t c) -> p t c", c=6)
            norms = [0]

            def rstd(src):
                for t in range(T):
                    last = nc.vector.bn_stats(stat3[:, t, :], src[:, t, :])
                link(last)
                for t in range(T):
                    last = nc.vector.bn_aggr(mv3[:, t, :], stat3[:, t, :])
                link(last)
                nc.vector.tensor_scalar(ve3[:, 0, :], mv3[:, :, 1], EPS, None, ALU.add)
                norms[0] += 1
                nc.vector.tensor_scalar(ve3[:, 1, :], mv3[:, :, 1], 1.0 + EPS, EPS * EPS, ALU.mult, ALU.add).then_inc(var_ready, 1)
                dve.wait_ge(rstd_ready, norms[0])

            def norm_to(o, src, which, signal=None):
                for t in range(T):
                    last = nc.vector.tensor_scalar(o[:, t, :], src[:, t, :], mv3[:, t, 0:1], rs[:, T * which + t:T * which + t + 1],
                                                   ALU.subtract, ALU.mult)
                    if signal:
                        last.then_inc(signal, 1)
                if not signal:
                    link(last)

            def attend(n, w, bias):
                b0 = n * T
                jd = n * 16
                scale = 1.0 / 16 if bias else HD ** -0.5
                for half in range(2):
                    for m in range(G):
                        dve.wait_ge(qv_filled, jd + 1)
                        nc.vector.tensor_scalar(qc[:, m, HALF * half:HALF * half + HALF], ps[:, 4 + jd % 2, :],
                                                w["bq"][:, m:m + 1] if bias else 0.0, scale, ALU.add, ALU.mult).then_inc(qv_taken, 1)
                        jd += 1
                    for t in range(HT * half, HT * half + HT):
                        dve.wait_ge(qv_filled, jd + 1)
                        nc.vector.tensor_copy(v[:, t, :], ps[:, 4 + jd % 2, 0:D]).then_inc(qv_taken, 1)
                        jd += 1
                if bias:
                    link(nc.vector.tensor_tensor(rel, rel, mask32[:, :].unsqueeze(1).to_broadcast([P, H, 32]), ALU.add))
                for i in range(T + 3):
                    if i < T:
                        t = i
                        dve.wait_ge(scored, b0 + t + 1)
                        add = (rel.rearrange("p (j m) c -> p j m c", j=G) if bias
                               else mask32[:, :].unsqueeze(1).unsqueeze(1).to_broadcast([P, G, G, 32]))
                        nc.vector.tensor_tensor(sc[:, t % 2].rearrange("p (j m) c -> p j m c", j=G),
                                                ps[:, 0:G, 0:P].rearrange("p j (m c) -> p j m c", m=G), add, ALU.add).then_inc(score_taken, 1)
                        dve.wait_ge(score_taken, b0 + t + 1)
                        mx = smx[:, H * (t % 2):H * (t % 2) + H]
                        link(nc.vector.tensor_reduce(mx, sc[:, t % 2], AX.X, ALU.max))
                        nc.vector.tensor_tensor(sc[:, t % 2], sc[:, t % 2], mx.unsqueeze(2).to_broadcast([P, H, 32]),
                                                ALU.subtract).then_inc(shifted, 1)
                    if 1 <= i <= T:
                        t = i - 1
                        dve.wait_ge(exped, b0 + t + 1)
                        sm = ssum[:, H * (t % 2):H * (t % 2) + H]
                        link(nc.vector.tensor_reduce(sm, sc[:, t % 2], AX.X, ALU.add))
                        link(nc.vector.reciprocal(sm, sm))
                        link(nc.vector.tensor_tensor(sc[:, t % 2], sc[:, t % 2], sm.unsqueeze(2).to_broadcast([P, H, 32]), ALU.mult))
                        if t >= 2:
                            dve.wait_ge(mixed, b0 + t - 1)
                        nc.vector.transpose(pT[:, t % 2].rearrange("p h c -> p (h c)"), sc[:, t % 2].rearrange("p h c -> p (h c)")).then_inc(probs_ready, 1)
                    if i >= 3:
                        t = i - 3
                        dve.wait_ge(projected, b0 + t + 1)
                        nc.vector.tensor_tensor(ub[:, t, :], ps[:, 7, 0:D], xh[:, t, :], ALU.add).then_inc(resid_ready, 1)
                dve.wait_ge(resid_ready, b0 + T)

            def route(n):
                dve.wait_ge(routed, n + 1)
                link(nc.vector.tensor_copy(lg[:, :], ps[:, 4, 0:T * E]))
                for t in range(T):
                    last = nc.vector.max(top[:, 8 * t:8 * t + 8], lg[:, E * t:E * t + E])
                link(last)
                for t in range(T):
                    last = nc.vector.max_index(idx[:, 8 * t:8 * t + 8], top[:, 8 * t:8 * t + 8], lg[:, E * t:E * t + E])
                link(last)
                top3 = top[:, :].rearrange("p (t c) -> p t c", c=8)
                idx3 = idx[:, :].rearrange("p (t c) -> p t c", c=8)
                id3 = idf[:, :].rearrange("p (c t) -> p c t", c=2)
                w3 = wgt[:, :].rearrange("p (c t) -> p c t", c=3)
                nc.vector.tensor_tensor(w3[:, 2, :], top3[:, :, 1], top3[:, :, 0], ALU.subtract).then_inc(top_diff, 1)
                nc.vector.tensor_copy(id3[:, 0, :], idx3[:, :, 0])
                link(nc.vector.tensor_copy(id3[:, 1, :], idx3[:, :, 1]))
                p4 = pick[:, :].rearrange("p (c t e) -> p c t e", c=2, e=E)
                io = iota[:, :].unsqueeze(1).to_broadcast([P, T, E])
                for c in range(TOP):
                    last = nc.vector.tensor_tensor(p4[:, c], io, id3[:, c, :].unsqueeze(2).to_broadcast([P, T, E]), ALU.is_equal)
                link(last)
                both3 = both[:, :].rearrange("p (t e) -> p t e", e=E)
                nc.vector.tensor_tensor(both3, p4[:, 0], p4[:, 1], ALU.add).then_inc(both_ready, 1)
                dve.wait_ge(top_exp, n + 1)
                link(nc.vector.tensor_scalar(w3[:, 1, :], w3[:, 0, :], 1.0, None, ALU.add))
                link(nc.vector.reciprocal(w3[:, 1, :], w3[:, 1, :]))
                link(nc.vector.tensor_tensor(w3[:, 2, :], w3[:, 0, :], w3[:, 1, :], ALU.mult))
                pl = plan[:, :].rearrange("p (c e) -> p c e", c=4)
                dve.wait_ge(ranked, n + 1)
                link(nc.vector.tensor_scalar(pl[:, 0, :], ps[:, 6, 0:E], float(P - 1), None, ALU.add))
                link(nc.vector.tensor_copy(plan_i[:, :], pl[:, 0, :]))
                link(nc.vector.tensor_scalar(plan_i[:, :], plan_i[:, :], 7, None, ALU.arith_shift_right))
                link(nc.vector.tensor_copy(pl[:, 1, :], plan_i[:, :]))
                link(nc.vector.tensor_tensor_scan(pl[:, 2, :], ones[:, 0:E], pl[:, 1, :], 0.0, ALU.mult, ALU.add))
                nc.vector.tensor_copy(ends[:, :], pl[:, 2, :])
                link(nc.vector.tensor_tensor(pl[:, 3, :], pl[:, 2, :], pl[:, 1, :], ALU.subtract))
                link(nc.vector.tensor_scalar(pl[:, 3, :], pl[:, 3, :], float(P), None, ALU.mult))
                q3 = posn[:, :].rearrange("p (t e) -> p t e", e=E)
                link(nc.vector.tensor_tensor(q3, ps[:, 5, 0:T * E].rearrange("p (t e) -> p t e", e=E),
                                             pl[:, 3, :].unsqueeze(1).to_broadcast([P, T, E]), ALU.add))
                s3 = step_c[:, :].rearrange("p (s e) -> p s e", e=E)
                steps_ = part(tok_c, TOK_PACK, "steps")
                link(nc.vector.tensor_tensor(s3, pl[:, 2, :].unsqueeze(1).to_broadcast([P, STEPS, E]),
                                             steps_.unsqueeze(2).to_broadcast([P, STEPS, E]), ALU.is_le))
                link(nc.vector.tensor_reduce(step_f[:, :], s3, AX.X, ALU.add))
                link(nc.vector.tensor_scalar(step_f[:, :], step_f[:, :], float(E - 1), None, ALU.min))
                link(nc.vector.tensor_copy(step_e[:, :], step_f[:, :]))
                link(nc.vector.tensor_scalar(step_b[:, :], step_e[:, :], 1, None, ALU.bitwise_and))
                c3 = comb[:, :].rearrange("p (t e) -> p t e", e=E)
                for c in range(TOP):
                    link(nc.vector.tensor_tensor(c3, p4[:, c], q3, ALU.mult))
                    link(nc.vector.tensor_reduce(slot_f[:, c * T:c * T + T], c3, AX.X, ALU.add))
                nc.vector.tensor_copy(slot[:, :], slot_f[:, :]).then_inc(slots_ready, 1)
                dve.wait_ge(slots_ready, n + 1)
                if n == 1:
                    for c in range(TOP):
                        last = nc.vector.tensor_tensor(p4[:, c], p4[:, c], w3[:, 1 + c, :].unsqueeze(2).to_broadcast([P, T, E]), ALU.mult)
                    link(last)
                    nc.vector.tensor_tensor(c3, p4[:, 0], p4[:, 1], ALU.add).then_inc(comb_ready, 1)

            def experts(n):

                def x_now(s, b):
                    nc.vector.tensor_scalar(xg_now[:, b, :], xg[:, bass.ds(s, 1), :].rearrange("p o d -> p (o d)"), 1.0, None,
                                            ALU.mult).then_inc(moe["xg_now_ready"], 1)

                def elementwise(s, j, first):
                    dve.wait_ge(moe["gu_filled"], n * 2 * STEPS + (s * 2 + (j + 1)))
                    if n == 0:
                        if not first:
                            dve.wait_ge(moe["silued"], s * 2 + (j - 1))
                        nc.vector.tensor_scalar(gclip[:, j], ps[:, j, :], -10.0, 10.0, ALU.max, ALU.min).then_inc(moe["clipped"], 1)
                        dve.wait_ge(moe["silued"], s * 2 + (j + 1))
                    if not first:
                        dve.wait_ge(moe["hid_turned"], n * 2 * STEPS + (s * 2 + (j - 1)))
                    if n == 0:
                        nc.vector.tensor_tensor(hid[:, j], gact[:, j], ps[:, 2 + j, :], ALU.mult).then_inc(moe["hid_ready"], 1)
                    else:
                        nc.vector.tensor_copy(hid[:, j], ps[:, j, :]).then_inc(moe["hid_ready"], 1)

                def take_y(s):
                    dve.wait_ge(moe["y_filled"], n * (STEPS + 1) + (s + 2))
                    nc.vector.tensor_scalar(y_all[:, bass.ds(s, 1), :].rearrange("p o d -> p (o d)"), ps[:, 7, 0:D], 1.0, None,
                                            ALU.mult).then_inc(moe["y_taken"], 1)

                dve.sem_inc(moe["y_taken"], 1)
                dve.wait_ge(xg_in[0], 16 * (n + 1))
                x_now(0, 0)
                x_now(1, 1)
                for c in range(1, len(XG_PARTS)):
                    dve.wait_ge(xg_in[c], 16 * (n + 1))
                elementwise(0, 0, True)
                elementwise(0, 1, True)
                with dve.Fori(0, STEPS // 2) as it:
                    for u in range(2):
                        s, b = it * 2 + (u + 1), (u + 1) % 2
                        dve.wait_ge(moe["xg_turned"], n * (STEPS + 1) + (s))
                        x_now(s + 1, 1 - b)
                        elementwise(s, 0, False)
                        elementwise(s, 1, False)
                        take_y(it * 2 + u)
                take_y(STEPS - 1)
                w3 = wgt[:, :].rearrange("p (c t) -> p c t", c=3)
                for t in range(T):
                    if t % 2 == 0:
                        dve.wait_ge(gathered[t // 2], 16 * 2 * TOP * (n + 1))
                    for c in range(TOP):
                        if c:
                            dve.wait_ge(moe["added"], n * TOP * T + (TOP * t + c))
                        nc.vector.scalar_tensor_tensor(h[:, t, :], yg[:, c, t, :], w3[:, 1 + c, t:t + 1], h[:, t, :],
                                                       ALU.mult, ALU.add).then_inc(moe["added"], 1)
                dve.wait_ge(moe["added"], n * TOP * T + (TOP * T))

            ones = part(tok_c, TOK_PACK, "ones")
            dve.wait_ge(qk_sum, 1)
            nc.vector.tensor_copy(qk[:, :], ps[:, 7, 0:KD * POOL_HEADS]).then_inc(qk_ready, 1)
            for i in range(T + 1):
                if i >= 1:
                    t = i - 1
                    a = tsc[:, 32 * (t % 2):32 * (t % 2) + 32].rearrange("p (w h) -> p w h", w=WIN)
                    sm = tsum[:, 4 * (t % 2):4 * (t % 2) + 4]
                    wb = wbar[:, WIN * (t % 2):WIN * (t % 2) + WIN]
                    dve.wait_ge(tok_exp, t + 1)
                    link(nc.vector.tensor_reduce(sm, a.rearrange("p w h -> p h w"), AX.X, ALU.add))
                    link(nc.vector.reciprocal(sm, sm))
                    link(nc.vector.tensor_tensor(a, a, sm.unsqueeze(1).to_broadcast([P, WIN, POOL_HEADS]), ALU.mult))
                    link(nc.vector.tensor_reduce(wb, a, AX.X, ALU.add))
                    link(nc.vector.tensor_scalar(wb, wb, 1.0 / POOL_HEADS, None, ALU.mult))
                    dve.wait_ge(x_in[t], 16)
                    if t >= 2:
                        dve.wait_ge(pool_turned, t - 1)
                    o = pooled[:, t % 2, :]
                    link(nc.vector.tensor_scalar(o, frames[:, t, 0, :], wb[:, 0:1], None, ALU.mult))
                    for w in range(1, WIN):
                        last = nc.vector.scalar_tensor_tensor(o, frames[:, t, w, :], wb[:, w:w + 1], o, ALU.mult, ALU.add)
                        if w < WIN - 1:
                            link(last)
                    last.then_inc(tok_pooled, 1)
                if i < T:
                    t = i
                    a = tsc[:, 32 * (t % 2):32 * (t % 2) + 32].rearrange("p (w h) -> p w h", w=WIN)
                    s = ps[:, 4, 0:32].rearrange("p (w h) -> p w h", w=WIN)
                    mx = tmx[:, 4 * (t % 2):4 * (t % 2) + 4]
                    dve.wait_ge(tok_scored, t + 1)
                    link(nc.vector.tensor_reduce(mx, s.rearrange("p w h -> p h w"), AX.X, ALU.max))
                    nc.vector.tensor_tensor(a, s, mx.unsqueeze(1).to_broadcast([P, WIN, POOL_HEADS]), ALU.subtract).then_inc(tok_shift, 1)
                    dve.wait_ge(tok_shift, t + 1)
                    dve.sem_inc(tok_score_taken, 1)
                if i >= 1:
                    t = i - 1
                    dve.wait_ge(tok_out, t + 1)
                    nc.vector.tensor_copy(h[:, t, :], ps[:, 6, D * (t % 2):D * (t % 2) + D]).then_inc(h_ready, 1)
            if stop < 1:
                return
            dve.wait_ge(h_ready, T)
            dve.wait_ge(w_l0, 32)
            nc.vector.tensor_copy(mask32[:, :], w0["mask32"])
            link(nc.vector.tensor_copy(iota[:, :], w0["iota"]))
            rstd(h)
            norm_to(xh, h, 0, normed)
            attend(0, w0, True)
            rstd(ub)
            norm_to(ub, ub, 0)
            ln_g, ln_b = (w0[n].unsqueeze(1).to_broadcast([P, HT, D]) for n in ("ln_g", "ln_b"))
            for half in range(2):
                r = slice(HT * half, HT * half + HT)
                link(nc.vector.tensor_tensor(ub[:, r], ub[:, r], ln_g, ALU.mult))
                link(nc.vector.tensor_tensor(ub[:, r], ub[:, r], ln_b, ALU.add))
                nc.vector.tensor_tensor(h[:, r], h[:, r], ub[:, r], ALU.add).then_inc(h_ready, HT)
            if stop < 2:
                return
            dve.wait_ge(h_ready, 2 * T)
            rstd(h)
            norm_to(ya, h, 1, normed)
            route(0)

            def gate_times_up(n, filled, clip_, acted, ready):
                def clip():
                    nc.vector.tensor_scalar(gclip[:, n % 2], ps[:, n % 2, :], -10.0, 10.0, ALU.max, ALU.min).then_inc(clip_, 1)

                def mult():
                    nc.vector.tensor_tensor(hid[:, n % 2], gact[:, n % 2], ps[:, 2 + n % 2, :], ALU.mult).then_inc(ready, 1)
                return clip, mult

            for n in range(4):
                clip, mult = gate_times_up(n, sh_filled, sh_clipped, sh_act, sh_hid)
                dve.wait_ge(sh_filled, n + 1)
                clip()
                dve.wait_ge(sh_act, n + 1)
                if n >= 2:
                    dve.wait_ge(sh_down, 1)
                mult()
            for t in range(T):
                dve.wait_ge(sh_down, t // HT + 1)
                nc.vector.tensor_tensor(h[:, t, :], ps[:, 4 + t // 2, D * (t % 2):D * (t % 2) + D], h[:, t, :], ALU.add).then_inc(sh_added, 1)
            dve.wait_ge(sh_added, T)
            experts(0)
            if stop < 3:
                return
            rstd(h)
            norm_to(xh, h, 0)
            norm_to(ya, h, 1, normed)
            dve.wait_ge(w_ga, 16)
            for j, (a, b) in enumerate((("al", "als"), ("be", "bes"))):
                link(nc.vector.tensor_scalar(rot[:, 0:S], ga["cos"], ga[a], None, ALU.mult))
                link(nc.vector.scalar_tensor_tensor(rot[:, S:2 * S], ga["sin"], ga[b], rot[:, 0:S], ALU.mult, ALU.add))
                o = (rot_a, rot_b)[j].rearrange("p (b s) -> p b s", s=S)
                nc.vector.tensor_copy(o, rot[:, S:2 * S].unsqueeze(1).to_broadcast([P, P // S, S])).then_inc(rot_ready, 1)
                dve.wait_ge(rot_ready, j + 1)
            for j in range(4):
                dve.wait_ge(dt_abs, j + 1)
                nc.vector.tensor_scalar(dt[:, j // 2, HALF * (j % 2):HALF * (j % 2) + HALF], ps[:, j, :],
                                        ga["dtb"][:, j // 2:j // 2 + 1], 0.0, ALU.add, ALU.max).then_inc(dt_relu, 1)
            dve.wait_ge(dt_relu, 4)
            dve.wait_ge(dt_log, 1)
            dtf = dt.rearrange("p k n -> p (k n)")
            link(nc.vector.tensor_tensor(dtf, dtf, fm[:, 2 * TOK:4 * TOK], ALU.add))
            dve.wait_ge(cols_ready, 12)
            link(nc.vector.tensor_tensor(dtu.rearrange("p k n -> p (k n)"), dtf, xc.rearrange("p k n -> p (k n)"), ALU.mult))
            nc.vector.memset(dA.rearrange("p k (b s) -> p (k b) s", s=S)[:, :, 0:1], 0.0).then_inc(dtu_ready, 1)
            dve.wait_ge(a_exp, 1)
            nc.vector.tensor_scalar(avec[:, :], avec[:, :], -1.0, None, ALU.mult).then_inc(a_ready, 1)
            for n in range(NS):
                dve.wait_ge(b_spread, n + 1)
                for dk in range(KD):
                    nc.vector.tensor_tensor(dBu[:, dk, :], dtu[:, dk, :], ps[:, 4:6, :].rearrange("p b n -> p (b n)"), ALU.mult).then_inc(b_used, 1)
                for dk in range(KD):
                    dve.wait_ge(b_used, KD * n + dk + 1)
                    dve.wait_ge(decay, KD * n + dk + 1)
                    nc.vector.tensor_tensor_scan(hs[:, dk, :], dA[:, dk, :], dBu[:, dk, :], 0.0, ALU.mult, ALU.add).then_inc(scanned, 1)
                dve.wait_ge(c_spread, n + 1)
                for dk in range(KD):
                    dve.wait_ge(scanned, KD * n + dk + 1)
                    if n >= 1:
                        dve.wait_ge(y_summed, KD * (n - 1) + dk + 1)
                    nc.vector.tensor_tensor(hC[:, dk, :], hs[:, dk, :], ps[:, 6:8, :].rearrange("p b n -> p (b n)"), ALU.mult).then_inc(c_used, 1)
            for j in range(4):
                dk, tok = j // 2, slice(HALF * (j % 2), HALF * (j % 2) + HALF)
                dve.wait_ge(y_summed, KD * (NS - 1) + dk + 1)
                nc.vector.scalar_tensor_tensor(ypre[:, dk, tok], xc[:, dk, tok], ga["D"][:, dk:dk + 1], ps[:, j, :],
                                               ALU.mult, ALU.add).then_inc(y_ready, 1)
            dve.wait_ge(rot_filled, 1)
            nc.vector.tensor_tensor(gbias, ps[:, 4, 0:P], ga["mask"], ALU.add).then_inc(gbias_ready, 1)
            dve.wait_ge(zr_done, 2)
            for j, o in enumerate((zq, zk)):
                nc.vector.tensor_scalar(o, zT, ga["gamma"][:, j:j + 1], ga["beta"][:, j:j + 1], ALU.mult, ALU.add).then_inc(qk_cols, 1)
            dve.wait_ge(gbias_ready, 1)
            for i in range(T + 4):
                if i < T:
                    t = i
                    dve.wait_ge(g_scored, t + 1)
                    link(nc.vector.scalar_tensor_tensor(gsc[:, t % 2], ps[:, t % 2, 0:P], Z ** -0.5, gbias, ALU.mult, ALU.add))
                    nc.vector.tensor_reduce(smx[:, t % 2:t % 2 + 1], gsc[:, t % 2], AX.X, ALU.max, negate=True).then_inc(g_shifted, 1)
                if 1 <= i <= T:
                    t = i - 1
                    dve.wait_ge(g_exped, t + 1)
                    sm = ssum[:, t % 2:t % 2 + 1]
                    link(nc.vector.reciprocal(sm, sm))
                    nc.vector.tensor_scalar(gsc[:, t % 2], gsc[:, t % 2], sm, None, ALU.mult).then_inc(g_probs, 1)
                if 2 <= i <= T + 1:
                    t = i - 2
                    dve.wait_ge(g_mixed, t + 1)
                    nc.vector.tensor_tensor(ghr[:, t % 2], ps[:, 4 + t % 2, 0:D].rearrange("p (k n) -> p k n", k=KD),
                                            rT[:, :, P * t:P * t + P], ALU.mult).then_inc(g_gated, 1)
                if i >= 4:
                    t = i - 4
                    dve.wait_ge(g_silu, t + 1)
                    o = ya[:, t, :]
                    link(nc.vector.tensor_tensor(o, ghh[:, t % 2], xh[:, t, :], ALU.subtract))
                    link(nc.vector.tensor_tensor(o, o, ub[:, t, :], ALU.mult))
                    link(nc.vector.tensor_tensor(o, o, xh[:, t, :], ALU.add))
                    nc.vector.tensor_tensor(h[:, t, :], h[:, t, :], o, ALU.add).then_inc(g_done, 1)
            if stop < 4:
                return
            dve.wait_ge(g_done, T)
            rstd(h)
            norm_to(xh, h, 0)
            norm_to(ya, h, 1, normed)
            attend(1, w1, False)
            for t in range(T):
                nc.vector.tensor_tensor(h[:, t, :], h[:, t, :], ub[:, t, :], ALU.add).then_inc(h_ready, 1)
            if stop < 5:
                return
            dve.wait_ge(h_ready, 3 * T)
            rstd(ub)
            norm_to(ya, ub, 0, normed)
            route(1)
            dve.wait_ge(comb_turned, 1)
            for j in range(2):
                nc.vector.tensor_copy(combT[0:E, 4 * j:4 * j + 4].rearrange("p t n -> p (t n)"), ps[0:E, 4 + j, :]).then_inc(comb_copied, 1)
            for t in range(T):
                dve.wait_ge(bias_filled, t // 2 * 2 + 2)
                nc.vector.tensor_tensor(h[:, t, :], ps[:, t // 2, D * (t % 2):D * (t % 2) + D], h[:, t, :], ALU.add).then_inc(bias_added, 1)
            dve.wait_ge(bias_added, T)
            experts(1)


STOP = 99


def kernel(**inp):
    import concourse.bacc as _bacc
    from concourse.bass_utils import run_bass_kernel_spmd as _run

    a = {k: np.asarray(v_) for k, v_ in inp.items()}
    f32 = np.float32

    def blocks(w):
        k, n = w.shape
        return w.reshape(k // P, P, n).transpose(1, 0, 2).reshape(P, -1)

    def per_feature(b):
        return b.reshape(-1, P).T

    def everywhere(b):
        return np.broadcast_to(b, (P, b.shape[-1]))

    def padded_heads(w):
        w = w.reshape(w.shape[0], H, HD)
        out = np.zeros((w.shape[0], H, 32), f32)
        out[:, :, :HD] = w
        return out.reshape(w.shape[0], H * 32)

    def on_rows(w, rows=P):
        out = np.zeros((rows, w.shape[1]), f32)
        out[:w.shape[0]] = w
        return out

    def pack(parts, where, n, rows=P):
        out = np.zeros((rows, n), f32)
        for name, (s, e) in where.items():
            out[:, s:e] = parts[name]
        return out

    x = np.zeros((CLIPS, P, D), f32)
    x[:, :FRAMES] = a["x"]
    x = x.reshape(T, P, WIN * D)

    tok_w = pack({"wk": blocks(a["L0_tok_Wk"]), "q": blocks(a["L0_tok_q"].T), "wv": blocks(a["L0_tok_Wv"].T),
                  "ident": np.eye(P, dtype=f32), "tri": np.triu(np.ones((P, P), f32), 1), "ones": np.ones((P, P), f32),
                  "steps": everywhere(np.arange(STEPS, dtype=f32))}, TOK_PACK, TOK_N)

    tok = np.arange(P)
    same = (tok[:, None] // S == tok[None, :] // S) & (tok[None, :] <= tok[:, None])
    mask128 = np.where(same, 0.0, NEG).astype(f32)
    mask32 = np.stack([mask128[p, 32 * (p // 32):32 * (p // 32) + 32] for p in range(P)])
    half = Z // 2
    freqs = np.exp(np.arange(half, dtype=f32) * f32(-np.log(10000.0) / half)).astype(f32)
    ang = (np.arange(S, dtype=f32)[:, None] * freqs[None, :]).astype(f32)
    cos = np.concatenate([np.cos(ang), np.cos(ang)], 1).T.astype(f32)
    sin = np.concatenate([-np.sin(ang), np.sin(ang)], 1).T.astype(f32)

    rpb = a["L0_attn_rpb"]
    pos = np.clip(np.arange(32)[None, :] % S - tok[:, None] % S, -S + 1, S - 1) + S - 1
    heads = [G * m + j for j in range(G) for m in range(G)]
    rel = rpb[pos][:, :, heads].transpose(0, 2, 1).reshape(P, H * 32)
    w = a["L0_attn_W_w"]
    bq, bk, bv = np.split(a["L0_attn_W_b"], 3)
    l0_w = pack({
        "wq": blocks(padded_heads(w[0:D].T)), "wk": blocks(padded_heads(w[D:2 * D].T)), "wv": blocks(w[2 * D:].T),
        "wo": blocks(a["L0_attn_proj_w"].T), "bq": per_feature(padded_heads(bq[None])[0]),
        "bk": per_feature(padded_heads(bk[None])[0]), "rel": rel, "mask32": mask32,
        "ln_g": everywhere(a["L0_attn_ln_g"]), "ln_b": everywhere(a["L0_attn_ln_b"]),
        "gamma": per_feature(a["L0_ffn_ln_gamma"]), "beta": per_feature(a["L0_ffn_ln_beta"]),
        "router": blocks(a["L0_ffn_router_w"]), "sgu": blocks(a["L0_ffn_shared_gate_up_w"]),
        "sdn": blocks(a["L0_ffn_shared_down_w"]), "iota": everywhere(np.arange(E, dtype=f32))}, L0_PACK, L0_N)

    mx_b = a["L1_attn_mx_b"]
    swap = np.r_[half:Z, 0:half]
    al, be = a["L1_attn_alpha_rb"][0], a["L1_attn_beta_rb"][0]
    ga_w = pack({
        "norm": per_feature(a["L1_attn_norm_w"]), "v": blocks(a["L1_attn_v_w"].T), "mx": blocks(a["L1_attn_mx_w"].T),
        "mxb": per_feature(mx_b[D:D + 3 * P]), "h": blocks(a["L1_attn_h_w"].T), "xproj": blocks(a["L1_attn_xproj_w"].T),
        "dt": on_rows(a["L1_attn_dt_w"].T), "A": blocks(a["L1_attn_A_log"]), "D": per_feature(a["L1_attn_D_p"]),
        "dtb": per_feature(a["L1_attn_dt_b"]), "gamma": a["L1_attn_gamma"].T, "beta": a["L1_attn_beta"].T,
        "cos": cos, "sin": sin, "al": al[:, None], "als": al[swap][:, None], "be": be[:, None],
        "bes": be[swap][:, None], "mask": mask128}, GA_PACK, GA_N)

    wq, wk, wv = np.split(a["L1_ffn_w_qkv"], 3, axis=1)
    l1_w = pack({
        "wq": blocks(padded_heads(wq)), "wk": blocks(padded_heads(wk)), "wv": blocks(wv), "wo": blocks(a["L1_ffn_w_o"]),
        "g1": per_feature(a["L1_ffn_ln1_g"]), "b1": per_feature(a["L1_ffn_ln1_b"]),
        "g2": per_feature(a["L1_ffn_ln2_g"]), "b2": per_feature(a["L1_ffn_ln2_b"]), "router": blocks(a["L1_ffn_w_gate"]),
        "eb1": a["L1_ffn_b1"].reshape(E, FB, P).transpose(2, 0, 1).reshape(P, E * FB),
        "eb2": on_rows(a["L1_ffn_b2"])}, L1_PACK, L1_N)

    first = np.zeros((32, P), f32)
    first[0] = 1.0
    rows_w = pack({
        "one": first, "wv": on_rows(bv[None], 32), "wo": on_rows(a["L0_attn_proj_b"][None], 32),
        "v": on_rows(a["L1_attn_v_b"][None], 32), "u": on_rows(mx_b[None, 0:D], 32),
        "hx": on_rows(mx_b[None, 640:896], 32), "h": on_rows(a["L1_attn_h_b"][None], 32)}, ROW_PACK, ROW_N, 32)

    def expert_blocks(w3):
        e, k, n = w3.shape
        return np.ascontiguousarray(w3.reshape(e, k // P, P, n).transpose(0, 2, 1, 3))

    arrays = {
        "x": x, "tok_w": tok_w, "l0_w": l0_w, "ga_w": ga_w, "l1_w": l1_w, "rows_w": rows_w,
        "moe0_gu": expert_blocks(a["L0_ffn_gate_up_w"]), "moe0_dn": expert_blocks(a["L0_ffn_down_w"]),
        "moe1_up": expert_blocks(a["L1_ffn_w1"]), "moe1_dn": expert_blocks(a["L1_ffn_w2"])}

    nc = _bacc.Bacc("TRN2", target_bir_lowering=False, num_devices=1)
    args = [nc.dram_tensor(n, v_.shape, F32, kind="ExternalInput").ap() for n, v_ in arrays.items()]
    out = nc.dram_tensor("out", (TOK, D), F32, kind="ExternalOutput").ap()
    scratch = [[nc.dram_tensor(f"{n}{i}", (rows, D), F32, kind="Internal").ap() for i in range(2)]
               for n, rows in (("sorted_x", (STEPS + 1) * P), ("sorted_y", STEPS * P))]
    tower(nc, *args, out, *scratch, stop=STOP)
    r = _run(nc, [arrays], core_ids=[0])
    return r.results[0]["out"].reshape(CLIPS, S, D)
```

```python
from contextlib import ExitStack

import numpy as np

import concourse.bass as bass
from concourse import mybir

F32 = mybir.dt.float32
BF16 = mybir.dt.bfloat16
U32 = mybir.dt.uint32
I32 = mybir.dt.int32
ALU = mybir.AluOpType
ACT = mybir.ActivationFunctionType
AX = mybir.AxisListType

P = 128
D = 256
KD = D // P
CLIPS, FRAMES, WIN = 64, 125, 8
S = 16
TOK = CLIPS * S
T = TOK // P
HALF = TOK // 2
HT = T // 2
POOL_HEADS = 4
H, HD = 16, 16
G = 4
E = 8
F = 1024
FB = F // P
FS = 256
Z = 128
NS = 16
DTR = 16
EPS = 1e-5
NEG = -1e30
TOP = 2
STEPS = TOP * TOK // P + E - 1
assert STEPS % 2 == 1


def layout(sizes):
    at, out = 0, {}
    for name, n in sizes:
        out[name] = (at, at + n)
        at += n
    return out, at


TOK_PACK, TOK_N = layout([
    ("wk", KD * D), ("q", KD * POOL_HEADS), ("wv", KD * D), ("ident", P), ("tri", P), ("ones", P), ("steps", STEPS),
    ("reset", E * T), ("home", TOP * T + STEPS + 1)])
L0_PACK, L0_N = layout([
    ("wq", KD * 512), ("wk", KD * 512), ("wv", KD * D), ("wo", KD * D), ("bq", G), ("bk", G),
    ("bv", D), ("bo", D), ("rel", H * 32), ("mask32", 32), ("ln_g", D), ("ln_b", D), ("gamma", KD), ("beta", KD),
    ("router", KD * E), ("sgu", KD * 2 * FS), ("sdn", FS // P * D), ("iota", E)])
GA_PACK, GA_N = layout([
    ("norm", KD), ("v", KD * D), ("vb", D), ("mx", KD * 896), ("mxb", 3), ("h", KD * D), ("xproj", KD * P), ("sel", 2 * NS),
    ("dt", D), ("A", KD * NS), ("D", KD), ("dtb", KD), ("gamma", 2), ("beta", 2),
    ("cos", S), ("sin", S), ("al", 1), ("als", 1), ("be", 1), ("bes", 1), ("mask", P)])
L1_PACK, L1_N = layout([
    ("wq", KD * 512), ("wk", KD * 512), ("wv", KD * D), ("wo", KD * D), ("g1", KD), ("b1", KD),
    ("g2", KD), ("b2", KD), ("router", KD * E), ("eb1", E * FB), ("eb2", D)])
ROW_PACK, ROW_N = layout([
    ("one", P), ("u", D), ("h", D)])


def tower(nc, x, tok_w, l0_w, ga_w, l1_w, rows_w, moe0_gu, moe0_dn, moe1_up, moe1_dn, out, sorted_x, slot_home, token_y):
    ctx = ExitStack()
    with ctx:
        def sb(name, cols, rows=P, dt=F32):
            return ctx.enter_context(nc.sbuf_tensor(name, [rows, cols], dt))

        def sem(name):
            return ctx.enter_context(nc.semaphore(name))

        big = sb("big", T * WIN * D)
        tok_c = sb("tok_c", TOK_N)
        l0_c = sb("l0_c", L0_N)
        ga_c = sb("ga_c", GA_N)
        row_c = sb("row_c", ROW_N, rows=32)
        h_ = sb("h_rows", T * D)
        rows_ = sb("rows", 4 * T * D)
        xc_ = sb("x_cols", KD * TOK)
        fm = sb("fm", 8 * TOK)
        stat = sb("stat", T * 6)
        mv = sb("mv", T * 2)
        ve = sb("ve", T * 2)
        rs = sb("rs", T * 2)
        neghalf = sb("neghalf", T * 2)
        smx = sb("smx", 2 * H)
        ssum = sb("ssum", 2 * H)
        tsc = sb("tsc", 2 * WIN * POOL_HEADS)
        tmx = sb("tmx", 2 * POOL_HEADS)
        tsum = sb("tsum", 2 * POOL_HEADS)
        wbar = sb("wbar", 2 * WIN)
        qk = sb("qk", KD * POOL_HEADS)
        lg = sb("lg", T * E)
        top = sb("top", T * 8)
        idx = sb("idx", T * 8, dt=U32)
        idf = sb("idf", T * 2)
        wgt = sb("wgt", T * 3)
        pick = sb("pick", 2 * T * E)
        both = sb("both", T * E)
        posn = sb("posn", T * E)
        upto_ = sb("upto", E * T)
        own_ = sb("own", 2 * T * E)
        comb = sb("comb", T * E)
        plan = sb("plan", 4 * E)
        plan_i = sb("plan_i", E, dt=I32)
        ends = sb("ends", E, dt=I32)
        step_e = sb("step_e", STEPS, dt=I32)
        step_b = sb("step_b", STEPS, dt=I32)
        step_f = sb("step_f", STEPS)
        step_c = sb("step_c", STEPS * E)
        slot_f = sb("slot_f", 2 * T)
        slot = sb("slot", 2 * T, dt=U32)
        zero = sb("zero", D)
        home = sb("home", TOP * T + STEPS + 1, dt=U32)
        dest = sb("dest", STEPS, dt=U32)
        avec = sb("avec", KD * NS)
        eb_now = sb("eb_now", 2 * FB)
        rot = sb("rot", 4 * S)

        def rows3(a):
            return a[:, 0:T * D].rearrange("p (t d) -> p t d", t=T)

        h = rows3(h_)
        xh, ya, v, ub = (rows3(rows_[:, i * T * D:(i + 1) * T * D]) for i in range(4))
        y_now = rows_[:, 0:2 * D].rearrange("p (b d) -> p b d", b=2)
        xc = xc_[:, :].rearrange("p (k n) -> p k n", k=KD)
        frames = big[:, :].rearrange("p (t w d) -> p t w d", t=T, w=WIN)
        tail = 12288
        BUFS = (2, 3)
        assert tail == BUFS[0] * (KD * 2 * F + FB * D) == BUFS[1] * (KD * F + FB * D)
        gu_w = big[:, 0:2 * KD * 2 * F].rearrange("p (b k f) -> p b k f", b=2, k=KD)
        up_w = big[:, 0:BUFS[1] * KD * F].rearrange("p (b k f) -> p b k f", b=BUFS[1], k=KD)
        dn_w = [big[:, tail - b * FB * D:tail].rearrange("p (b f d) -> p b f d", b=b, f=FB) for b in BUFS]
        gclip = big[:, tail:tail + 1024].rearrange("p (b n) -> p b n", b=2)
        gact = big[:, tail + 1024:tail + 2048].rearrange("p (b n) -> p b n", b=2)
        hid = big[:, tail + 2048:tail + 3072].rearrange("p (b n) -> p b n", b=2)
        sc = big[:, tail:tail + 1024].rearrange("p (b h c) -> p b h c", b=2, c=32)
        pT = big[:, tail + 1024:tail + 2048].rearrange("p (b h c) -> p b h c", b=2, c=32)
        oT = big[:, tail + 2048:tail + 2560].rearrange("p (b k n) -> p b k n", b=2, k=KD)
        gsc = big[:, tail:tail + 256].rearrange("p (b n) -> p b n", b=2)
        gpT = big[:, tail + 256:tail + 512].rearrange("p (b n) -> p b n", b=2)
        ghr = big[:, tail + 512:tail + 1024].rearrange("p (b k n) -> p b k n", b=2, k=KD)
        ghh = big[:, tail + 1024:tail + 1536].rearrange("p (b n) -> p b n", b=2)
        gbias = big[:, tail + 1536:tail + 1664]
        rot_a = big[:, tail + 1664:tail + 1792]
        rot_b = big[:, tail + 1792:tail + 1920]
        xg_now = big[:, tail + 3072:tail + 3584].rearrange("p (b d) -> p b d", b=2)
        xgT = big[:, tail + 3584:tail + 4096].rearrange("p (b k n) -> p b k n", b=2, k=KD)
        xg = fm[:, 0:(STEPS + 1) * D].rearrange("p (s d) -> p s d", d=D)
        hidT = fm[:, (STEPS + 1) * D:].rearrange("p (b f n) -> p b f n", b=2, f=FB)
        yg = fm[:, 0:2 * T * D].rearrange("p (c t d) -> p c t d", c=2, t=T)
        combT = big[:, tail + 3072:tail + 4096].rearrange("p (t n) -> p t n", t=T)
        qc = fm[:, 0:4 * TOK].rearrange("p (m n) -> p m n", m=4)
        kc = fm[:, 4 * TOK:].rearrange("p (m n) -> p m n", m=4)
        xwT = fm[:, 0:4096].rearrange("p (b w n) -> p b w n", b=2, w=2 * WIN)
        plT = fm[:, 4096:4608].rearrange("p (b k n) -> p b k n", b=2, k=KD)
        scoresT = fm[0:POOL_HEADS, 5120:5120 + WIN * P]
        pool_odd = fm[:, 6144:6144 + D]
        pooled = fm[:, 4608:5120].rearrange("p (b d) -> p b d", b=2)
        scan4 = fm[:, :].rearrange("p (a k n) -> p a k n", a=4, k=KD)
        dA, dBu, hs, hC = scan4[:, 0], scan4[:, 1], scan4[:, 2], scan4[:, 3]
        mxT = fm[:, 0:2048].rearrange("p (k n) -> p k n", k=KD)
        rT = fm[:, 2048:4096].rearrange("p (k n) -> p k n", k=KD)
        zT = fm[:, 4096:5120]
        zq = fm[:, 5120:6144]
        zk = fm[:, 6144:7168]
        ypre = xc
        dt = rows_[:, T * D:2 * T * D].rearrange("p (k n) -> p k n", k=KD)
        dtu = rows_[:, 3 * T * D:].rearrange("p (k n) -> p k n", k=KD)
        xd = sb("xd", TOK)
        xd_parts = sb("xd_parts", TOK, dt=BF16)
        sel = sb("sel", 2 * NS, dt=BF16)
        b_all = [big[:, tail + c:tail + c + TOK] for c in (0, 1920)]
        rest = big[:, tail + 1920 + TOK:tail + 1920 + 2 * TOK]

        def part(tensor, where, name, k=None, rows=P):
            a, b = where[name]
            ap = tensor[0:rows, a:b]
            return ap.rearrange("p (k n) -> p k n", k=k) if k else ap

        ident = part(tok_c, TOK_PACK, "ident")
        w0 = {n: part(l0_c, L0_PACK, n, k) for n, k in (
            ("wq", KD), ("wk", KD), ("wv", KD), ("wo", KD), ("bq", None), ("bk", None), ("bv", None), ("bo", None), ("mask32", None),
            ("ln_g", None), ("ln_b", None), ("gamma", None), ("beta", None), ("router", KD), ("sgu", KD),
            ("sdn", FS // P), ("iota", None))}
        rel = part(l0_c, L0_PACK, "rel").rearrange("p (h c) -> p h c", c=32)
        w1 = {n: part(l0_c, L1_PACK, n, k) for n, k in (
            ("wq", KD), ("wk", KD), ("wv", KD), ("wo", KD), ("g1", None), ("b1", None), ("g2", None),
            ("b2", None), ("router", KD), ("eb1", E))}
        eb2 = part(l0_c, L1_PACK, "eb2", rows=32)
        ga = {n: part(ga_c, GA_PACK, n, k) for n, k in (
            ("norm", None), ("v", KD), ("vb", None), ("mx", KD), ("mxb", None), ("h", KD), ("xproj", KD), ("sel", None), ("A", None),
            ("D", None), ("dtb", None), ("gamma", None), ("beta", None), ("cos", None), ("sin", None),
            ("al", None), ("als", None), ("be", None), ("bes", None), ("mask", None))}
        dtw = part(ga_c, GA_PACK, "dt", rows=DTR)
        row = {n: part(row_c, ROW_PACK, n, rows=32) for n in ROW_PACK}
        mask32 = sb("mask32", 32)
        iota = sb("iota", E)

        ps = ctx.enter_context(nc.psum_tensor("ps", [P, 8, 512], F32))

        w_tok, w_l0, w_ga, w_l1 = sem("w_tok"), sem("w_l0"), sem("w_ga"), sem("w_l1")
        x_in = [sem(f"x_in{t}") for t in range(T)]
        out_done = sem("out_done")
        dve_step, act_step, stats_done = sem("dve_step"), sem("act_step"), sem("stats_done")
        consts = sem("consts")
        qk_sum, qk_ready = sem("qk_sum"), sem("qk_ready")
        xw_turned, xw_copied, tok_scored, tok_shift = (sem(n) for n in ("xw_turned", "xw_copied", "tok_scored", "tok_shift"))
        tok_exp, tok_pooled, pool_turned, pool_copied = (sem(n) for n in ("tok_exp", "tok_pooled", "pool_turned", "pool_copied"))
        tok_out, h_ready, h_shifted, resid_bias, tok_turned, tok_scores_copied = (
            sem(n) for n in ("tok_out", "h_ready", "h_shifted", "resid_bias", "tok_turned", "tok_scores_copied"))
        var_ready, rstd_ready, normed, turned, cols_ready = (sem(n) for n in ("var_ready", "rstd_ready", "normed", "turned", "cols_ready"))
        qv_filled, qv_taken, k_filled, k_taken = (sem(n) for n in ("qv_filled", "qv_taken", "k_filled", "k_taken"))
        scored, shifted, exped, probs_ready = (sem(n) for n in ("scored", "shifted", "exped", "probs_ready"))
        score_taken = sem("score_taken")
        mixed, mix_copied, mix_turned, mixT_copied, projected, resid_ready = (
            sem(n) for n in ("mixed", "mix_copied", "mix_turned", "mixT_copied", "projected", "resid_ready"))
        routed, top_diff, top_exp, comb_ready = (sem(n) for n in ("routed", "top_diff", "top_exp", "comb_ready"))
        sh_filled, sh_clipped, sh_act, sh_hid, sh_down, sh_added = (
            sem(n) for n in ("sh_filled", "sh_clipped", "sh_act", "sh_hid", "sh_down", "sh_added"))
        both_ready, ranked, slots_ready, steps_ready, zeroed, zero_ready = (
            sem(n) for n in ("both_ready", "ranked", "slots_ready", "steps_ready", "zeroed", "zero_ready"))
        expert_in = [sem(f"expert_in{b}") for b in range(max(BUFS))]
        moe = {k: sem(k) for k in (
            "in_ready", "out_ready", "scattered", "xg_now_ready", "xg_turned", "xgT_ready", "gu_filled", "clipped",
            "silued", "hid_ready", "hid_turned", "hidT_ready", "bias_now_ready", "y_filled", "y_taken", "y_free", "home_scattered", "dest_in", "added")}
        y_out = [sem(f"y_out{b}") for b in range(2)]
        xg_in = [sem(f"xg_in{c}") for c in range(3)]
        token_y_in = [[sem(f"token_y_in{half}_{c}") for c in range(TOP)] for half in range(2)]
        comb_turned, comb_copied, bias_filled, bias_added = (
            sem(n) for n in ("comb_turned", "comb_copied", "bias_filled", "bias_added"))
        gv_filled, gv_done, xd_filled, xd_copied = (sem(n) for n in ("gv_filled", "gv_done", "xd_filled", "xd_copied"))
        dt_filled, dt_abs, dt_log, dt_relu, dtu_ready, a_exp, a_ready = (
            sem(n) for n in ("dt_filled", "dt_abs", "dt_log", "dt_relu", "dtu_ready", "a_exp", "a_ready"))
        xd_split, b_spread, b_copied, c_spread, decay, b_used, c_used, scanned, y_summed = (
            sem(n) for n in ("xd_split", "b_spread", "b_copied", "c_spread", "decay", "b_used", "c_used", "scanned", "y_summed"))
        y_ready, mx_ready, zr_filled, zr_done, qk_cols, u_filled, u_done = (
            sem(n) for n in ("y_ready", "mx_ready", "zr_filled", "zr_done", "qk_cols", "u_filled", "u_done"))
        rot_ready, rot_filled, gbias_ready = sem("rot_ready"), sem("rot_filled"), sem("gbias_ready")
        g_scored, g_shifted, g_exped, g_probs, g_turned, g_copied = (
            sem(n) for n in ("g_scored", "g_shifted", "g_exped", "g_probs", "g_turned", "g_copied"))
        g_mixed, g_gated, g_out, g_silu, g_less, g_delta, g_done, v_ready, h_plus_x = (
            sem(n) for n in ("g_mixed", "g_gated", "g_out", "g_silu", "g_less", "g_delta", "g_done", "v_ready", "h_plus_x"))

        block = ctx.enter_context(nc.Block())

        OUT_PARTS = ((0, HT), (HT, T - 1), (T - 1, T))

        def added_count(tiles):
            return TOP * tiles if tiles % HT == 0 else TOP * HT * (tiles // HT) + HT + tiles % HT

        def out_count(n, b, count):
            return 16 * (n * ((STEPS + 1 - b) // 2) + count)

        XG_PARTS = ((0, 2), (2, 8), (8, STEPS + 1))
        NORM_SCALE = {1: (w0["gamma"], w0["beta"]), 2: (ga["norm"], None), 3: (w1["g1"], w1["b1"]), 4: (w1["g2"], w1["b2"])}

        @block.sync
        def _(sp):
            W = ((gu_w, moe0_gu), (up_w, moe1_up))

            def load_in(n, e, b):
                sbuf, dram = W[n]
                sp.dma_start(sbuf[:, b], dram[bass.ds(e, 1)].rearrange("o p k f -> p (o k) f")).then_inc(expert_in[b], 16)

            def load_out(n, e, b):
                dn = (moe0_dn, moe1_dn)[n]
                sp.dma_start(dn_w[n][:, b], dn[bass.ds(e, 1)].rearrange("o p f d -> p (o f) d")).then_inc(expert_in[b], 16)

            def landed(n, b, count, ready):
                sp.wait_ge(expert_in[b], count * 16 + (E // BUFS[0] * 32 if n and b < BUFS[0] else 0))
                sp.sem_inc(moe[ready], 1)

            def first_experts(n):
                if n == 1:
                    sp.wait_ge(moe["added"], TOP * T)
                for b in range(BUFS[n]):
                    load_in(n, b, b)
                for b in range(BUFS[n]):
                    landed(n, b, 1, "in_ready")
                    load_out(n, b, b)
                for b in range(BUFS[n]):
                    landed(n, b, 2, "out_ready")

            def serve_experts(n):
                sp.wait_ge(moe["scattered"], n * 16 * 2 * T + (16 * 2 * T))
                src = sorted_x[n].rearrange("(s p) d -> p s d", p=P)
                for c, (a, b) in enumerate(XG_PARTS):
                    sp.dma_start(xg[:, a:b], src[:, a:b]).then_inc(xg_in[c], 16)

                def follow(e, b, count):
                    end = sp.value_load(ends[0:1, bass.ds(e, 1)], min_val=0, max_val=STEPS)
                    sp.wait_ge(moe["gu_filled"], end * 2 + (n * (2 * STEPS + 1) + 1))
                    load_in(n, e + BUFS[n], b)
                    landed(n, b, count * 2 + 1, "in_ready")
                    sp.wait_ge(moe["y_filled"], end + (n * (STEPS + 1) + 1))
                    load_out(n, e + BUFS[n], b)
                    landed(n, b, count * 2 + 2, "out_ready")

                rounds = E // BUFS[n] - 1
                with sp.Fori(0, rounds) as i:
                    for b in range(BUFS[n]):
                        follow(i * BUFS[n] + b, b, i + 1)
                for b in range(E % BUFS[n]):
                    follow(rounds * BUFS[n] + b, b, rounds + 1)
                if n == 0:
                    sp.wait_ge(sh_added, T)
                    sp.dma_start(l0_c[:, 0:L1_N], l1_w).then_inc(w_l1, 16)
                for b in range(2):
                    sp.wait_ge(y_out[b], out_count(n, b, (STEPS + 1 - b) // 2))
                src = token_y[n][0:TOP * TOK].rearrange("(c t p) d -> p c t d", c=TOP, p=P)
                for half in range(2):
                    r = slice(HT * half, HT * half + HT)
                    for c in range(TOP):
                        sp.dma_start(yg[:, c, r], src[:, c, r]).then_inc(token_y_in[half][c], 16)

            sp.dma_start(tok_c[:, :], tok_w).then_inc(w_tok, 16)
            for t in range(T):
                sp.dma_start(frames[:, t], x[t].rearrange("p (w d) -> p w d", w=WIN)).then_inc(x_in[t], 16)
            sp.dma_start(l0_c[:, :], l0_w).then_inc(w_l0, 16)
            sp.dma_start(row_c[:, :], rows_w).then_inc(w_l0, 16)
            sp.dma_start(ga_c[:, :], ga_w).then_inc(w_ga, 16)
            sp.wait_ge(zero_ready, 2)
            for n in range(2):
                sp.dma_start(sorted_x[n].rearrange("(s p) d -> p s d", p=P),
                             zero[:, :].unsqueeze(1).to_broadcast([P, STEPS + 1, D])).then_inc(zeroed, 16)
                sp.dma_start(slot_home[n].rearrange("(s p) o -> p s o", p=P), home[:, TOP * T:].unsqueeze(2), allow_slow_non_contiguous=True).then_inc(zeroed, 16)
            sp.wait_ge(tok_pooled, T)
            first_experts(0)
            serve_experts(0)
            first_experts(1)
            serve_experts(1)
            for a, b in OUT_PARTS:
                sp.wait_ge(moe["added"], TOP * T + added_count(b))
                sp.dma_start(out.rearrange("(t p) d -> p t d", p=P)[:, a:b], h[:, a:b]).then_inc(out_done, 16)
            sp.wait_ge(out_done, 16 * len(OUT_PARTS))

        @block.tensor
        def _(pe):
            def mm(o, a, b, start, stop_, **kw):
                return nc.tensor.matmul(o, a, b, start=start, stop=stop_, **kw)

            def turn_half(n, half):
                src = xh if n == 0 else ya
                pe.wait_ge(normed, n * T + HT * (half + 1))
                for k in range(KD):
                    for i in range(HT):
                        last = nc.tensor.transpose(ps[:, 2 * half + k, P * i:P * i + P],
                                                   src[:, HT * half + i, P * k:P * k + P], ident)
                    last.then_inc(turned, 1)

            def turn_cols(n):
                for half in range(2):
                    turn_half(n, half)

            def project(n, w):
                jd, ja = n * 16, n * 8
                for half in range(2):
                    pe.wait_ge(cols_ready, (0, 3)[n] * 4 + 2 * half + 2)
                    tok = slice(HALF * half, HALF * half + HALF)
                    for m in range(G):
                        if jd - n * 16 >= 2:
                            pe.wait_ge(qv_taken, jd - 1)
                        for k in range(KD):
                            last = mm(ps[:, 4 + jd % 2, :], w["wq"][:, k, P * m:P * m + P], xc[:, k, tok], k == 0, k == 1)
                        last.then_inc(qv_filled, 1)
                        jd += 1
                        if ja - n * 8 >= 2:
                            pe.wait_ge(k_taken, ja - 1)
                        for k in range(KD):
                            last = mm(ps[:, 6 + ja % 2, :], w["wk"][:, k, P * m:P * m + P], xc[:, k, tok], k == 0, k == 1)
                        last.then_inc(k_filled, 1)
                        ja += 1
                    for t in range(HT * half, HT * half + HT):
                        pe.wait_ge(qv_taken, jd - 1)
                        o = ps[:, 4 + jd % 2, 0:D]
                        for k in range(KD):
                            last = mm(o, xc[:, k, P * t:P * t + P], w["wv"][:, k, :], k == 0, k == 1)
                        last.then_inc(qv_filled, 1)
                        jd += 1

            def attend(n, w):
                pe.wait_ge(qv_taken, 16 * (n + 1))
                pe.wait_ge(k_taken, 8 * (n + 1))
                b0 = n * T

                def scores(t):
                    if t >= 1:
                        pe.wait_ge(score_taken, b0 + t)
                    for m in range(G):
                        for g in range(G):
                            for j in range(G):
                                tok = slice(P * t + 32 * g, P * t + 32 * g + 32)
                                c = 32 * m
                                last = mm(ps[32 * g:32 * g + 32, j, c:c + 32], qc[32 * j:32 * j + 32, m, tok],
                                          kc[32 * j:32 * j + 32, m, tok], True, True)
                    last.then_inc(scored, 1)

                def mix(t):
                    pe.wait_ge(probs_ready, b0 + t + 1)
                    if t >= 2:
                        pe.wait_ge(mix_copied, b0 + t - 1)
                    for hh in range(H):
                        for g in range(G):
                            c = HD * hh
                            q = slice(32 * g, 32 * g + 32)
                            last = mm(ps[q, 4 + t % 2, c:c + HD], pT[q, t % 2, (hh % G) * G + hh // G, :],
                                      v[q, t, HD * hh:HD * hh + HD], True, True)
                    last.then_inc(mixed, 1)

                def turn_mix(t):
                    pe.wait_ge(mix_copied, b0 + t + 1)
                    if t >= 1:
                        pe.wait_ge(mixT_copied, b0 + t)
                    for k in range(KD):
                        last = nc.tensor.transpose(ps[:, 6, P * k:P * k + P], ya[:, t, P * k:P * k + P], ident)
                    last.then_inc(mix_turned, 1)

                def out_proj(t):
                    pe.wait_ge(mixT_copied, b0 + t + 1)
                    if t >= 1:
                        pe.wait_ge(resid_ready, b0 + t)
                    o = ps[:, 7, 0:D]
                    for k in range(KD):
                        last = mm(o, oT[:, t % 2, k, :], w["wo"][:, k, :], k == 0, k == 1)
                    last.then_inc(projected, 1)

                for i in range(T + 4):
                    if i < T:
                        scores(i)
                    if 2 <= i <= T + 1:
                        mix(i - 2)
                    if 3 <= i <= T + 2:
                        turn_mix(i - 3)
                    if i >= 4:
                        out_proj(i - 4)

            def turn_and_route(n, turning, w):
                def logits(half):
                    pe.wait_ge(cols_ready, (1, 4)[n] * 4 + 2 * half + 2)
                    for t in range(HT * half, HT * half + HT):
                        for k in range(KD):
                            last = mm(ps[:, 4, E * t:E * t + E], xc[:, k, P * t:P * t + P], w["router"][:, k, :], k == 0, k == 1)
                    return last

                turn_half(turning, 0)
                logits(0)
                turn_half(turning, 1)
                logits(1).then_inc(routed, 1)

            def rank(n):
                pe.wait_ge(both_ready, n + 1)
                mm(ps[:, 6, 0:T * E].rearrange("p (e t) -> p e t", t=T), ones, both[:, :].rearrange("p (t e) -> p e t", e=E), True, True)
                mm(ps[:, 5, 0:T * E], part(tok_c, TOK_PACK, "tri"), both[:, :], True, True).then_inc(ranked, 1)

            def experts(n):
                w_in = (gu_w, up_w)[n]

                def turn_x(s, b):
                    pe.wait_ge(moe["xg_now_ready"], n * (STEPS + 1) + (s + 1))
                    for k in range(KD):
                        last = nc.tensor.transpose(ps[:, 6, P * k:P * k + P], xg_now[:, b, P * k:P * k + P], ident)
                    last.then_inc(moe["xg_turned"], 1)

                def expert_of(s):
                    e = pe.value_load(step_e[0:1, bass.ds(s, 1)], min_val=0, max_val=E - 1)
                    buf = pe.value_load(step_b[0:1, bass.ds(s, 1)], min_val=0, max_val=BUFS[n] - 1)
                    return e, buf

                def hidden(s, b, expert, first):
                    e, buf = expert
                    pe.wait_ge(moe["in_ready"], n * E + (e + 1))
                    pe.wait_ge(moe["xgT_ready"], n * (STEPS + 1) + (s + 1))
                    w = w_in[:, bass.ds(buf, 1)]
                    for j in range(2):
                        if not first:
                            pe.wait_ge(moe["hid_ready"], n * 2 * STEPS + (s * 2 + (j - 1)))
                        for part_ in range(2 - n):
                            for k in range(KD):
                                c = F * part_ + 512 * j
                                last = mm(ps[:, 2 * part_ + j, :], xgT[:, b, k, :],
                                          w[:, :, k, c:c + 512].rearrange("p o c -> p (o c)"), k == 0, k == 1)
                        last.then_inc(moe["gu_filled"], 1)

                def turn_hidden(s, j, first):
                    pe.wait_ge(moe["hid_ready"], n * 2 * STEPS + (s * 2 + (j + 1)))
                    if not first:
                        pe.wait_ge(moe["hidT_ready"], n * 2 * STEPS + (s * 2 + (j - 1)))
                    for i in range(4):
                        last = nc.tensor.transpose(ps[:, 4 + j, P * i:P * i + P], hid[:, j, P * i:P * i + P], ident)
                    last.then_inc(moe["hid_turned"], 1)

                def down(s, b, expert):
                    e, buf = expert
                    pe.wait_ge(moe["out_ready"], n * E + (e + 1))
                    pe.wait_ge(moe["hidT_ready"], n * 2 * STEPS + (s * 2 + 2))
                    pe.wait_ge(moe["y_taken"], n * (STEPS + 1) + (s + 1))
                    w = dn_w[n][:, bass.ds(buf, 1)]
                    for f in range(FB):
                        last = mm(ps[:, 7, 0:D], hidT[:, b, f, :], w[:, :, f, :].rearrange("p o d -> p (o d)"), f == 0, f == FB - 1)
                    last.then_inc(moe["y_filled"], 1)

                pe.wait_ge(steps_ready, n + 1)
                pe.sem_inc(moe["y_filled"], 1)
                pe.sem_inc(moe["gu_filled"], 1)
                turn_x(0, 0)
                hidden(0, 0, expert_of(0), True)
                turn_hidden(0, 0, True)
                turn_x(1, 1)
                turn_hidden(0, 1, True)
                with pe.Fori(0, STEPS // 2) as it:
                    for u in range(2):
                        s, b = it * 2 + (u + 1), (u + 1) % 2
                        expert = expert_of(s)
                        hidden(s, b, expert, False)
                        if u == 0:
                            before = expert_of(it * 2)
                        turn_hidden(s, 0, False)
                        turn_x(s + 1, 1 - b)
                        down(it * 2 + u, 1 - b, before)
                        turn_hidden(s, 1, False)
                        before = expert
                down(STEPS - 1, (STEPS - 1) % 2, expert_of(STEPS - 1))

            pe.wait_ge(w_tok, 16)
            ones = part(tok_c, TOK_PACK, "ones")
            wk = part(tok_c, TOK_PACK, "wk", KD)
            qh = part(tok_c, TOK_PACK, "q", KD)
            wv = part(tok_c, TOK_PACK, "wv", KD)
            for m in range(KD):
                for k in range(KD):
                    last = mm(ps[:, 7, POOL_HEADS * m:POOL_HEADS * m + POOL_HEADS], wk[:, k, P * m:P * m + P], qh[:, k, :], k == 0, k == 1)
            last.then_inc(qk_sum, 1)
            for i in range(T + 3):
                if i < T:
                    pe.wait_ge(x_in[i], 16)
                    for b in range(4):
                        if i >= 1:
                            pe.wait_ge(xw_copied, 4 * (i - 1) + b + 1)
                        for c in range(4):
                            w, k = 2 * b + c // 2, c % 2
                            last = nc.tensor.transpose(ps[:, b, P * c:P * c + P], frames[:, i, w, P * k:P * k + P], ident)
                        last.then_inc(xw_turned, 1)
                if i >= 3:
                    t = i - 3
                    pe.wait_ge(tok_pooled, t + 1)
                    if t >= 1:
                        pe.wait_ge(h_ready, t)
                    for k in range(KD):
                        last = nc.tensor.transpose(ps[:, 5, P * k:P * k + P], pooled[:, t % 2, P * k:P * k + P], ident)
                    last.then_inc(pool_turned, 1)
                if 1 <= i <= T:
                    pe.wait_ge(tok_scores_copied, i)
                    if i >= 2:
                        pe.wait_ge(tok_shift, i - 1)
                    for w in range(WIN):
                        last = nc.tensor.transpose(ps[:, 4, POOL_HEADS * w:POOL_HEADS * w + POOL_HEADS], scoresT[:, P * w:P * w + P],
                                                   ident[0:POOL_HEADS, 0:POOL_HEADS])
                    last.then_inc(tok_turned, 1)
                if i < T:
                    if i == 0:
                        pe.wait_ge(qk_ready, 1)
                    pe.wait_ge(xw_copied, 4 * (i + 1))
                    if i >= 1:
                        pe.wait_ge(tok_scores_copied, i)
                    xw = xwT[:, i % 2].rearrange("p (w k) n -> p w k n", k=KD)
                    for half in range(2):
                        for k in range(KD):
                            last = mm(ps[0:POOL_HEADS, 6 + half, :].rearrange("p (w n) -> p w n", n=P), qk[:, POOL_HEADS * k:POOL_HEADS * k + POOL_HEADS],
                                      xw[:, 4 * half:4 * half + 4, k, :], k == 0, k == 1)
                    last.then_inc(tok_scored, 1)
                if i >= 3:
                    t = i - 3
                    pe.wait_ge(pool_copied, t + 1)
                    for k in range(KD):
                        last = mm(ps[:, 5, D:2 * D], plT[:, t % 2, k, :], wv[:, k, :], k == 0, k == 1)
                    last.then_inc(tok_out, 1)
            pe.wait_ge(w_l0, 32)
            turn_cols(0)
            project(0, w0)
            attend(0, w0)
            turn_and_route(0, 1, w0)
            rank(0)
            for half in range(2):
                tok = slice(HALF * half, HALF * half + HALF)
                for fb in range(FS // P):
                    n = 2 * half + fb
                    if n >= 2:
                        pe.wait_ge(sh_hid, n - 1)
                    for part_, bank in ((0, n % 2), (1, 2 + n % 2)):
                        for k in range(KD):
                            c = FS * part_ + P * fb
                            if n < 2 and k == 0 and part_ == 0:
                                pe.wait_ge(cols_ready, 8)
                            last = mm(ps[:, bank, :], w0["sgu"][:, k, c:c + P], xc[:, k, tok], k == 0, k == 1)
                    last.then_inc(sh_filled, 1)
                for fb in range(FS // P):
                    pe.wait_ge(sh_hid, 2 * half + fb + 1)
                    if half == 0 and fb == 0:
                        pe.wait_ge(slots_ready, 1)
                    for i in range(HT):
                        o = ps[:, 4 + 2 * half + i // 2, D * (i % 2):D * (i % 2) + D]
                        last = mm(o, hid[:, fb, P * i:P * i + P], w0["sdn"][:, fb, :], fb == 0 and i % 2 == 0,
                                  fb == FS // P - 1, skip_group_check=True)
                last.then_inc(sh_down, 1)
            pe.wait_ge(sh_added, T)
            experts(0)
            for half in range(2):
                turn_half(2, half)
                if half == 0:
                    pe.wait_ge(w_ga, 16)
                pe.wait_ge(cols_ready, 8 + 2 * half + 2)
                for k in range(KD):
                    last = mm(ps[:, 6 + half, :], ga["xproj"][:, k, :], xc[:, k, HALF * half:HALF * half + HALF], k == 0, k == 1)
                last.then_inc(xd_filled, 1)
            pe.wait_ge(xd_copied, 2)
            for dk in range(KD):
                for half in range(2):
                    mm(ps[:, 2 * dk + half, :], dtw[:, P * dk:P * dk + P], xd[0:DTR, HALF * half:HALF * half + HALF],
                       True, True).then_inc(dt_filled, 1)

            def value_rows(t):
                if t >= 2:
                    pe.wait_ge(gv_done, t - 1)
                for k in range(KD):
                    last = mm(ps[:, 6 + t % 2, 0:D], xc[:, k, P * t:P * t + P], ga["v"][:, k, :], k == 0, k == 1)
                last.then_inc(gv_filled, 1)

            def sum_states(n, dk):
                pe.wait_ge(c_used, KD * n + dk + 1)
                for half in range(2):
                    last = mm(ps[:, 2 * dk + half, :], ident, hC[:, dk, HALF * half:HALF * half + HALF],
                              n == 0, n == NS - 1, skip_group_check=True)
                last.then_inc(y_summed, 1)

            def spread(r, bank, free, count, full):
                if count:
                    pe.wait_ge(free, count)
                for half in range(2):
                    last = mm(ps[:, bank + half, :], sel[:, r:r + 1].to_broadcast([P, P]),
                              xd_parts[:, HALF * half:HALF * half + HALF], True, True)
                last.then_inc(full, 1)

            for t in range(HT):
                value_rows(t)
            pe.wait_ge(xd_split, 1)
            spread(0, 4, b_copied, 0, b_spread)
            for t in range(HT, T):
                value_rows(t)
            pe.wait_ge(gv_done, T)
            for n in range(NS):
                if n + 1 < NS:
                    spread(n + 1, 4, b_copied, n + 1, b_spread)
                if n >= 1:
                    sum_states(n - 1, 0)
                spread(NS + n, 6, c_used, KD * n, c_spread)
                if n == 0:
                    pe.wait_ge(dt_log, 1)
                    pe.wait_ge(dt_relu, 4)
                if n >= 1:
                    sum_states(n - 1, 1)
            for dk in range(KD):
                sum_states(NS - 1, dk)
            pe.wait_ge(rot_ready, 2)
            pe.wait_ge(b_copied, NS)
            mm(ps[:, 4, 0:P], rot_a, rot_b, True, True).then_inc(rot_filled, 1)
            pe.wait_ge(mx_ready, 1)
            for j in range(6):
                m, half = j // 2, j % 2
                if j >= 2:
                    pe.wait_ge(zr_done, j - 1)
                for k in range(KD):
                    last = mm(ps[:, 6 + j % 2, :], ga["mx"][:, k, D + P * m:D + P * m + P],
                              mxT[:, k, HALF * half:HALF * half + HALF], k == 0, k == 1)
                last.then_inc(zr_filled, 1)
            pe.wait_ge(gbias_ready, 1)
            for t in range(T):
                if t >= 2:
                    pe.wait_ge(u_done, t - 1)
                o = ps[:, 4 + t % 2, 0:D]
                for k in range(KD):
                    mm(o, mxT[:, k, P * t:P * t + P], ga["mx"][:, k, 0:D], k == 0, False)
                mm(o, row["one"], row["u"], False, True).then_inc(u_filled, 1)
            pe.wait_ge(qk_cols, 2)
            pe.wait_ge(v_ready, 1)
            pe.wait_ge(zr_done, 6)
            pe.wait_ge(u_done, T)
            for i in range(T + 3):
                if i < T:
                    t = i
                    if t >= 2:
                        pe.wait_ge(g_shifted, t - 1)
                    mm(ps[:, t % 2, 0:P], zq[:, P * t:P * t + P], zk[:, P * t:P * t + P], True, True).then_inc(g_scored, 1)
                if i >= 3:
                    t = i - 3
                    if t >= 2:
                        pe.wait_ge(g_silu, t - 1)
                    o = ps[:, 6 + t % 2, 0:D]
                    for k in range(KD):
                        mm(o, mxT[:, k, P * t:P * t + P], ga["mx"][:, k, 640:896], k == 0, False)
                    mm(o, row["one"], row["h"], False, False)
                    pe.wait_ge(g_gated, t + 1)
                    for k in range(KD):
                        last = mm(o, ghr[:, t % 2, k, :], ga["h"][:, k, :], False, k == 1)
                    last.then_inc(g_out, 1)
                if 2 <= i <= T + 1:
                    t = i - 2
                    pe.wait_ge(g_copied, t + 1)
                    if t >= 2:
                        pe.wait_ge(g_gated, t - 1)
                    for k in range(KD):
                        last = mm(ps[:, 4 + t % 2, P * k:P * k + P], v[:, t, P * k:P * k + P], gpT[:, t % 2, :], True, True)
                    last.then_inc(g_mixed, 1)
                if 1 <= i <= T:
                    t = i - 1
                    pe.wait_ge(g_probs, t + 1)
                    if t >= 2:
                        pe.wait_ge(g_copied, t - 1)
                    nc.tensor.transpose(ps[:, 2 + t % 2, 0:P], gsc[:, t % 2, :], ident).then_inc(g_turned, 1)
            pe.wait_ge(g_done, T)
            turn_cols(3)
            pe.wait_ge(w_l1, 16)
            project(1, w1)
            attend(1, w1)
            turn_and_route(1, 4, w1)
            rank(1)
            pe.wait_ge(comb_ready, 1)
            for t in range(T):
                bank = 4 + t // 4
                last = nc.tensor.transpose(ps[0:E, bank, P * (t % 4):P * (t % 4) + P], comb[:, E * t:E * t + E], ident)
            last.then_inc(comb_turned, 1)
            pe.wait_ge(comb_copied, 2)
            for t in range(T):
                mm(ps[:, t // 2, D * (t % 2):D * (t % 2) + D], combT[0:E, t, :], eb2[0:E, :], True, True).then_inc(bias_filled, 1)
            pe.wait_ge(bias_added, T)
            experts(1)

        @block.scalar
        def _(act):
            steps = [0]

            def link(ins):
                steps[0] += 1
                ins.then_inc(act_step, 1)
                act.wait_ge(act_step, steps[0])

            def take_cols(n):
                for half in range(2):
                    for k in range(KD):
                        act.wait_ge(turned, n * 4 + 2 * half + k + 1)
                        o = xc[:, k, HALF * half:HALF * half + HALF]
                        if n == 0:
                            a = nc.scalar.copy(o, ps[:, 2 * half + k, :])
                        else:
                            g, b = NORM_SCALE[n]
                            a = nc.scalar.activation(o, ps[:, 2 * half + k, :], ACT.Identity, scale=g[:, k:k + 1],
                                                     bias=0.0 if b is None else b[:, k:k + 1])
                        a.then_inc(cols_ready, 1)

            def attend(n, w, bias):
                b0 = n * T
                for j in range(2 * G):
                    half, m = j // G, j % G
                    act.wait_ge(k_filled, n * 8 + j + 1)
                    nc.scalar.activation(kc[:, m, HALF * half:HALF * half + HALF], ps[:, 6 + j % 2, :], ACT.Identity,
                                         bias=w["bk"][:, m:m + 1] if bias else 0.0).then_inc(k_taken, 1)
                for i in range(T + 3):
                    if i < T:
                        act.wait_ge(shifted, b0 + i + 1)
                        nc.scalar.activation(sc[:, i % 2], sc[:, i % 2], ACT.Exp).then_inc(exped, 1)
                    if 2 <= i <= T + 1:
                        t = i - 2
                        act.wait_ge(mixed, b0 + t + 1)
                        nc.scalar.copy(ya[:, t, :], ps[:, 4 + t % 2, 0:D]).then_inc(mix_copied, 1)
                    if i >= 3:
                        t = i - 3
                        act.wait_ge(mix_turned, b0 + t + 1)
                        if t >= 2:
                            act.wait_ge(projected, b0 + t - 1)
                        nc.scalar.copy(oT[:, t % 2].rearrange("p k n -> p (k n)"), ps[:, 6, 0:D]).then_inc(mixT_copied, 1)

            def route(n):
                act.wait_ge(top_diff, n + 1)
                nc.scalar.activation(wgt[:, 0:T], wgt[:, 2 * T:3 * T], ACT.Exp).then_inc(top_exp, 1)

            def experts(n):

                def take_x(s, b, first):
                    act.wait_ge(moe["xg_turned"], n * (STEPS + 1) + (s + 1))
                    if not first:
                        act.wait_ge(moe["gu_filled"], n * (2 * STEPS + 1) + (s * 2 - 1))
                    g, shift = NORM_SCALE[(1, 4)[n]]
                    for k in range(KD):
                        last = nc.scalar.activation(xgT[:, b, k, :], ps[:, 6, P * k:P * k + P], ACT.Identity,
                                                    scale=g[:, k:k + 1], bias=shift[:, k:k + 1])
                    last.then_inc(moe["xgT_ready"], 1)

                def bias_now(s, b):
                    e = act.value_load(step_e[0:1, bass.ds(s, 1)], min_val=0, max_val=E - 1)
                    nc.scalar.copy(eb_now[:, b * FB:b * FB + FB], w1["eb1"].rearrange("p e f -> p (e f)")[:, bass.ds(e * FB, FB)]).then_inc(moe["bias_now_ready"], 1)

                def act_on(s, j, first):
                    act.wait_ge(moe["clipped"], s * 2 + (j + 1))
                    if not first:
                        act.wait_ge(moe["hid_ready"], n * 2 * STEPS + (s * 2 + (j - 1)))
                    nc.scalar.activation(gact[:, j], gclip[:, j], ACT.Silu).then_inc(moe["silued"], 1)

                def take_hidden(s, j, b, first):
                    act.wait_ge(moe["hid_turned"], n * 2 * STEPS + (s * 2 + (j + 1)))
                    if not first:
                        act.wait_ge(moe["y_filled"], n * (STEPS + 1) + (s))
                    if n == 0:
                        nc.scalar.copy(hidT[:, b, 4 * j:4 * j + 4].rearrange("p f n -> p (f n)"), ps[:, 4 + j, :]).then_inc(moe["hidT_ready"], 1)
                        return
                    if j == 0:
                        act.wait_ge(moe["bias_now_ready"], s + 1)
                    for i in range(4):
                        last = nc.scalar.activation(hidT[:, b, 4 * j + i, :], ps[:, 4 + j, P * i:P * i + P], ACT.Gelu_apprx_tanh,
                                                    bias=eb_now[:, b * FB + 4 * j + i:b * FB + 4 * j + i + 1])
                    last.then_inc(moe["hidT_ready"], 1)

                take_x(0, 0, True)
                if n == 1:
                    bias_now(0, 0)
                for j in range(2):
                    if n == 0:
                        act_on(0, j, True)
                take_hidden(0, 0, 0, True)
                take_x(1, 1, True)
                take_hidden(0, 1, 0, True)
                with act.Fori(0, STEPS // 2) as it:
                    for u in range(2):
                        s, b = it * 2 + (u + 1), (u + 1) % 2
                        if n == 1:
                            bias_now(s, b)
                        for j in range(2):
                            if n == 0:
                                act_on(s, j, False)
                        take_hidden(s, 0, b, False)
                        take_x(s + 1, 1 - b, False)
                        take_hidden(s, 1, b, False)

            for i in range(T + 3):
                if i < T:
                    for b in range(4):
                        act.wait_ge(xw_turned, 4 * i + b + 1)
                        if i >= 2 and b == 0:
                            act.wait_ge(tok_scored, i - 1)
                        nc.scalar.copy(xwT[:, i % 2, 4 * b:4 * b + 4].rearrange("p w n -> p (w n)"), ps[:, b, :]).then_inc(xw_copied, 1)
                if i >= 3:
                    t = i - 3
                    act.wait_ge(pool_turned, t + 1)
                    if t >= 2:
                        act.wait_ge(tok_out, t - 1)
                    nc.scalar.copy(plT[:, t % 2].rearrange("p k n -> p (k n)"), ps[:, 5, 0:D]).then_inc(pool_copied, 1)
                if 1 <= i <= T:
                    act.wait_ge(tok_shift, i)
                    a = tsc[:, 32 * ((i - 1) % 2):32 * ((i - 1) % 2) + 32]
                    nc.scalar.activation(a, a, ACT.Exp, scale=1.0 / 16).then_inc(tok_exp, 1)
                if i < T:
                    act.wait_ge(tok_scored, i + 1)
                    nc.scalar.copy(scoresT, ps[0:POOL_HEADS, 6:8, :].rearrange("p b n -> p (b n)")).then_inc(tok_scores_copied, 1)
            take_cols(0)
            attend(0, w0, True)
            take_cols(1)
            route(0)
            for n in range(4):
                act.wait_ge(sh_clipped, n + 1)
                nc.scalar.activation(gact[:, n % 2], gclip[:, n % 2], ACT.Silu).then_inc(sh_act, 1)
            act.wait_ge(sh_hid, 4)
            experts(0)
            act.wait_ge(w_ga, 16)
            take_cols(2)
            for half in range(2):
                act.wait_ge(xd_filled, half + 1)
                nc.scalar.copy(xd[:, HALF * half:HALF * half + HALF], ps[:, 6 + half, :]).then_inc(xd_copied, 1)
            for j in range(4):
                act.wait_ge(dt_filled, j + 1)
                last = nc.scalar.activation(fm[:, HALF * j:HALF * j + HALF], ps[:, j, :], ACT.Abs, bias=ga["dtb"][:, j // 2:j // 2 + 1])
                last.then_inc(dt_abs, 1)
            act.wait_ge(dt_abs, 4)
            link(nc.scalar.activation(fm[:, 0:2 * TOK], fm[:, 0:2 * TOK], ACT.Exp, scale=-1.0))
            nc.scalar.activation(avec[:, :], ga["A"], ACT.Exp).then_inc(a_exp, 1)
            nc.scalar.activation(fm[:, 2 * TOK:4 * TOK], fm[:, 0:2 * TOK], ACT.Ln, bias=1.0).then_inc(dt_log, 1)
            act.wait_ge(a_ready, 1)
            act.wait_ge(dtu_ready, 1)
            for n in range(NS):
                act.wait_ge(b_spread, n + 1)
                if n >= 2:
                    act.wait_ge(b_used, KD * (n - 1))
                nc.scalar.copy(b_all[n % 2], ps[:, 4:6, :].rearrange("p b n -> p (b n)")).then_inc(b_copied, 1)
                for dk in range(KD):
                    if n >= 1:
                        act.wait_ge(scanned, KD * (n - 1) + dk + 1)
                    later = "p (b s) -> p b s"
                    nc.scalar.activation(dA[:, dk, :].rearrange(later, s=S)[:, :, 1:S], dt[:, dk, :].rearrange(later, s=S)[:, :, 1:S], ACT.Exp,
                                         scale=avec[:, NS * dk + n:NS * dk + n + 1]).then_inc(decay, 1)
            act.wait_ge(gv_done, T)
            v_flat = v.rearrange("p t d -> p (t d)")
            nc.scalar.activation(v_flat, v_flat, ACT.Silu).then_inc(v_ready, 1)
            act.wait_ge(y_ready, 4)
            nc.scalar.activation(mxT.rearrange("p k n -> p (k n)"), ypre.rearrange("p k n -> p (k n)"), ACT.Silu).then_inc(mx_ready, 1)
            for j in range(6):
                m, half = j // 2, j % 2
                act.wait_ge(zr_filled, j + 1)
                tok = slice(HALF * half, HALF * half + HALF)
                o = zT[:, tok] if m == 0 else rT[:, m - 1, tok]
                nc.scalar.activation(o, ps[:, 6 + j % 2, :], ACT.Silu, bias=ga["mxb"][:, m:m + 1]).then_inc(zr_done, 1)
            for t in range(T):
                act.wait_ge(u_filled, t + 1)
                nc.scalar.activation(ub[:, t, :], ps[:, 4 + t % 2, 0:D], ACT.Sigmoid).then_inc(u_done, 1)
            for i in range(T + 3):
                if i < T:
                    act.wait_ge(g_shifted, i + 1)
                    nc.scalar.activation(gsc[:, i % 2], gsc[:, i % 2], ACT.Exp, bias=smx[:, i % 2:i % 2 + 1],
                                         accum_out=ssum[:, i % 2:i % 2 + 1]).then_inc(g_exped, 1)
                if 1 <= i <= T:
                    t = i - 1
                    act.wait_ge(g_turned, t + 1)
                    if t >= 2:
                        act.wait_ge(g_mixed, t - 1)
                    nc.scalar.copy(gpT[:, t % 2], ps[:, 2 + t % 2, 0:P]).then_inc(g_copied, 1)
                if i >= 3:
                    t = i - 3
                    act.wait_ge(g_out, t + 1)
                    if t >= 2:
                        act.wait_ge(g_delta, t - 1)
                    nc.scalar.activation(ghh[:, t % 2], ps[:, 6 + t % 2, 0:D], ACT.Silu).then_inc(g_silu, 1)
            act.wait_ge(w_l1, 16)
            take_cols(3)
            attend(1, w1, False)
            take_cols(4)
            route(1)
            experts(1)

        @block.gpsimd
        def _(pool):
            nc.gpsimd.memset(neghalf[:, :], -0.5).then_inc(consts, 1)
            nc.gpsimd.memset(zero[:, :], 0.0).then_inc(zero_ready, 1)
            pool.wait_ge(w_tok, 16)
            nc.gpsimd.tensor_copy(home[:, :], part(tok_c, TOK_PACK, "home")).then_inc(zero_ready, 1)
            pool.wait_ge(consts, 1)
            norms = [0]

            def rstd(*halves):
                ve3, rs3, half3 = (a[:, :].rearrange("p (c t) -> p c t", c=2) for a in (ve, rs, neghalf))
                for half in halves:
                    r = slice(HT * half, HT * half + HT)
                    norms[0] += 1
                    pool.wait_ge(var_ready, norms[0])
                    nc.gpsimd.tensor_tensor(rs3[:, :, r], ve3[:, :, r], half3[:, :, r], ALU.pow).then_inc(rstd_ready, 1)

            def dispatch(n):
                pool.wait_ge(zeroed, 64)
                pool.wait_ge(slots_ready, n + 1)
                to = lambda c, t: bass.IndirectOffsetOnAxis(slot[:, c * T + t:c * T + t + 1], 0)
                for t in range(T):
                    for c in range(TOP):
                        pool.indirect_dma_start(sorted_x[n], to(c, t), ya[:, t, :], None).then_inc(moe["scattered"], 16)
                pool.sem_inc(moe["y_free"], 2)
                for c in range(TOP):
                    for t in range(T):
                        pool.indirect_dma_start(slot_home[n], to(c, t), home[:, c * T + t:c * T + t + 1],
                                                None).then_inc(moe["home_scattered"], 16)
                pool.wait_ge(moe["home_scattered"], 16 * TOP * T * (n + 1))
                pool.dma_start(dest[:, :].unsqueeze(2), slot_home[n][0:STEPS * P].rearrange("(s p) o -> p s o", p=P), allow_slow_non_contiguous=True).then_inc(moe["dest_in"], 16)
                pool.wait_ge(moe["dest_in"], 16 * (n + 1))
                for s in range(STEPS):
                    if s >= 2:
                        pool.wait_ge(y_out[s % 2], out_count(n, s % 2, s // 2))
                        pool.sem_inc(moe["y_free"], 1)
                    pool.wait_ge(moe["y_taken"], n * (STEPS + 1) + s + 2)
                    pool.indirect_dma_start(token_y[n], bass.IndirectOffsetOnAxis(dest[:, s:s + 1], 0),
                                            y_now[:, s % 2], None).then_inc(y_out[s % 2], 16)

            rstd(0, 1)
            pool.wait_ge(normed, T)
            pool.wait_ge(w_l0, 32)
            for t in range(T):
                nc.gpsimd.tensor_tensor(h[:, t, :], h[:, t, :], w0["ln_b"], ALU.add).then_inc(h_shifted, 1)
            pool.wait_ge(turned, 4)
            for t in range(T):
                nc.gpsimd.tensor_tensor(xh[:, t, :], xh[:, t, :], w0["bo"], ALU.add).then_inc(resid_bias, 1)
            rstd(0, 0, 1, 1)
            dispatch(0)
            rstd(0, 1)
            pool.wait_ge(dtu_ready, 1)
            for n in range(NS):
                pool.wait_ge(b_copied, n + 1)
                for dk in range(KD):
                    if n >= 1:
                        pool.wait_ge(scanned, KD * (n - 1) + dk + 1)
                    nc.gpsimd.tensor_tensor(dBu[:, dk, :], dtu[:, dk, :], b_all[n % 2], ALU.mult).then_inc(b_used, 1)
            for t in range(T):
                nc.gpsimd.tensor_tensor(h[:, t, :], h[:, t, :], xh[:, t, :], ALU.add).then_inc(h_plus_x, 1)
            for t in range(T):
                pool.wait_ge(g_silu, t + 1)
                nc.gpsimd.tensor_tensor(ghh[:, t % 2], ghh[:, t % 2], xh[:, t, :], ALU.subtract).then_inc(g_less, 1)
                pool.wait_ge(g_less, t + 1)
                nc.gpsimd.tensor_tensor(ub[:, t, :], ub[:, t, :], ghh[:, t % 2], ALU.mult).then_inc(g_delta, 1)
                if t == HT - 1:
                    rstd(0)
            rstd(1)
            rstd(0, 1)
            dispatch(1)

        @block.vector
        def _(dve):
            steps = [0]

            def link(ins):
                steps[0] += 1
                ins.then_inc(dve_step, 1)
                dve.wait_ge(dve_step, steps[0])

            mv3 = mv[:, :].rearrange("p (t c) -> p t c", c=2)
            ve3 = ve[:, :].rearrange("p (c t) -> p c t", c=2)
            stat3 = stat[:, :].rearrange("p (t c) -> p t c", c=6)
            norms = [0]

            def row_stats(src, t):
                nc.vector.bn_stats(stat3[:, t, :], src[:, t, :]).then_inc(stats_done, 1)

            def rstd_begin(half):
                r = slice(HT * half, HT * half + HT)
                norms[0] += 1
                dve.wait_ge(stats_done, HT * norms[0])
                for t in range(HT * half, HT * half + HT):
                    last = nc.vector.bn_aggr(mv3[:, t, :], stat3[:, t, :])
                link(last)
                nc.vector.tensor_scalar(ve3[:, 0, r], mv3[:, r, 1], EPS, None, ALU.add)
                nc.vector.tensor_scalar(ve3[:, 1, r], mv3[:, r, 1], 1.0 + EPS, EPS * EPS, ALU.mult, ALU.add).then_inc(var_ready, 1)

            def rstd(half):
                rstd_begin(half)
                dve.wait_ge(rstd_ready, norms[0])

            def norm_to(o, src, which, half, signal=None):
                for t in range(HT * half, HT * half + HT):
                    last = nc.vector.tensor_scalar(o[:, t, :], src[:, t, :], mv3[:, t, 0:1], rs[:, T * which + t:T * which + t + 1],
                                                   ALU.subtract, ALU.mult)
                    if signal:
                        last.then_inc(signal, 1)

            def attend(n, w, bias, finish):
                b0 = n * T
                jd = n * 16
                scale = 1.0 / 16 if bias else HD ** -0.5
                for half in range(2):
                    for m in range(G):
                        dve.wait_ge(qv_filled, jd + 1)
                        nc.vector.tensor_scalar(qc[:, m, HALF * half:HALF * half + HALF], ps[:, 4 + jd % 2, :],
                                                w["bq"][:, m:m + 1] if bias else 0.0, scale, ALU.add, ALU.mult).then_inc(qv_taken, 1)
                        jd += 1
                    for t in range(HT * half, HT * half + HT):
                        dve.wait_ge(qv_filled, jd + 1)
                        if bias:
                            nc.vector.tensor_tensor(v[:, t, :], ps[:, 4 + jd % 2, 0:D], w["bv"], ALU.add).then_inc(qv_taken, 1)
                        else:
                            nc.vector.tensor_copy(v[:, t, :], ps[:, 4 + jd % 2, 0:D]).then_inc(qv_taken, 1)
                        jd += 1
                if bias:
                    link(nc.vector.tensor_tensor(rel, rel, mask32[:, :].unsqueeze(1).to_broadcast([P, H, 32]), ALU.add))
                for i in range(T + 5):
                    if i >= 5:
                        t = i - 5
                        dve.wait_ge(projected, b0 + t + 1)
                        if bias and t == 0:
                            dve.wait_ge(resid_bias, T)
                        nc.vector.tensor_tensor(ub[:, t, :], ps[:, 7, 0:D], xh[:, t, :], ALU.add).then_inc(resid_ready, 1)
                        dve.wait_ge(resid_ready, b0 + t + 1)
                        row_stats(ub, t)
                    if i < T:
                        t = i
                        dve.wait_ge(scored, b0 + t + 1)
                        if t >= 2:
                            dve.wait_ge(probs_ready, b0 + t - 1)
                        add = (rel.rearrange("p (j m) c -> p j m c", j=G) if bias
                               else mask32[:, :].unsqueeze(1).unsqueeze(1).to_broadcast([P, G, G, 32]))
                        nc.vector.tensor_tensor(sc[:, t % 2].rearrange("p (j m) c -> p j m c", j=G),
                                                ps[:, 0:G, 0:P].rearrange("p j (m c) -> p j m c", m=G), add, ALU.add).then_inc(score_taken, 1)
                        dve.wait_ge(score_taken, b0 + t + 1)
                        mx = smx[:, H * (t % 2):H * (t % 2) + H]
                        link(nc.vector.tensor_reduce(mx, sc[:, t % 2], AX.X, ALU.max))
                        nc.vector.tensor_tensor(sc[:, t % 2], sc[:, t % 2], mx.unsqueeze(2).to_broadcast([P, H, 32]),
                                                ALU.subtract).then_inc(shifted, 1)
                    if 1 <= i <= T:
                        t = i - 1
                        dve.wait_ge(exped, b0 + t + 1)
                        sm = ssum[:, H * (t % 2):H * (t % 2) + H]
                        link(nc.vector.tensor_reduce(sm, sc[:, t % 2], AX.X, ALU.add))
                        link(nc.vector.reciprocal(sm, sm))
                        link(nc.vector.tensor_tensor(sc[:, t % 2], sc[:, t % 2], sm.unsqueeze(2).to_broadcast([P, H, 32]), ALU.mult))
                        if t >= 2:
                            dve.wait_ge(mixed, b0 + t - 1)
                        nc.vector.transpose(pT[:, t % 2].rearrange("p h c -> p (h c)"), sc[:, t % 2].rearrange("p h c -> p (h c)")).then_inc(probs_ready, 1)
                    if i == T:
                        finish(0)
                finish(1)

            def route(n):
                dve.wait_ge(routed, n + 1)
                link(nc.vector.tensor_copy(lg[:, :], ps[:, 4, 0:T * E]))
                for t in range(T):
                    last = nc.vector.max(top[:, 8 * t:8 * t + 8], lg[:, E * t:E * t + E])
                link(last)
                for t in range(T):
                    last = nc.vector.max_index(idx[:, 8 * t:8 * t + 8], top[:, 8 * t:8 * t + 8], lg[:, E * t:E * t + E])
                link(last)
                top3 = top[:, :].rearrange("p (t c) -> p t c", c=8)
                idx3 = idx[:, :].rearrange("p (t c) -> p t c", c=8)
                id3 = idf[:, :].rearrange("p (c t) -> p c t", c=2)
                w3 = wgt[:, :].rearrange("p (c t) -> p c t", c=3)
                nc.vector.tensor_tensor(w3[:, 2, :], top3[:, :, 1], top3[:, :, 0], ALU.subtract).then_inc(top_diff, 1)
                nc.vector.tensor_copy(id3[:, 0, :], idx3[:, :, 0])
                link(nc.vector.tensor_copy(id3[:, 1, :], idx3[:, :, 1]))
                p4 = pick[:, :].rearrange("p (c t e) -> p c t e", c=2, e=E)
                io = iota[:, :].unsqueeze(1).to_broadcast([P, T, E])
                for c in range(TOP):
                    last = nc.vector.tensor_tensor(p4[:, c], io, id3[:, c, :].unsqueeze(2).to_broadcast([P, T, E]), ALU.is_equal)
                link(last)
                both3 = both[:, :].rearrange("p (t e) -> p t e", e=E)
                nc.vector.tensor_tensor(both3, p4[:, 0], p4[:, 1], ALU.add).then_inc(both_ready, 1)
                pl = plan[:, :].rearrange("p (c e) -> p c e", c=4)
                upto = upto_[:, :].rearrange("p (e t) -> p e t", t=T)
                by_expert = lambda a: a.rearrange("p (t e) -> p e t", e=E)
                dve.wait_ge(ranked, n + 1)
                link(nc.vector.tensor_tensor_scan(upto_[:, :], part(tok_c, TOK_PACK, "reset"), ps[:, 6, 0:T * E], 0.0,
                                                  ALU.mult, ALU.add))
                link(nc.vector.tensor_scalar(pl[:, 0, :], upto[:, :, T - 1], float(P - 1), None, ALU.add))
                link(nc.vector.tensor_copy(plan_i[:, :], pl[:, 0, :]))
                nc.vector.tensor_tensor(by_expert(posn[:, :]), by_expert(ps[:, 5, 0:T * E]), upto, ALU.add)
                link(nc.vector.tensor_scalar(plan_i[:, :], plan_i[:, :], 7, None, ALU.arith_shift_right))
                link(nc.vector.tensor_copy(pl[:, 1, :], plan_i[:, :]))
                link(nc.vector.tensor_tensor_scan(pl[:, 2, :], ones[:, 0:E], pl[:, 1, :], 0.0, ALU.mult, ALU.add))
                nc.vector.tensor_copy(ends[:, :], pl[:, 2, :])
                link(nc.vector.tensor_tensor(pl[:, 3, :], pl[:, 2, :], pl[:, 1, :], ALU.subtract))
                link(nc.vector.tensor_scalar(pl[:, 3, :], pl[:, 3, :], float(P), None, ALU.mult))
                q3 = posn[:, :].rearrange("p (t e) -> p t e", e=E)
                link(nc.vector.tensor_tensor(q3, q3, pl[:, 3, :].unsqueeze(1).to_broadcast([P, T, E]), ALU.add))
                own = own_[:, :].rearrange("p (c t e) -> p c t e", c=2, e=E)
                for c in range(TOP):
                    last = nc.vector.tensor_tensor(own[:, c], p4[:, c], q3, ALU.mult)
                link(last)
                link(nc.vector.tensor_reduce(slot_f[:, :], own.rearrange("p c t e -> p (c t) e"), AX.X, ALU.add))
                nc.vector.tensor_copy(slot[:, :], slot_f[:, :]).then_inc(slots_ready, 1)
                s3 = step_c[:, :].rearrange("p (s e) -> p s e", e=E)
                steps_ = part(tok_c, TOK_PACK, "steps")
                link(nc.vector.tensor_tensor(s3, pl[:, 2, :].unsqueeze(1).to_broadcast([P, STEPS, E]),
                                             steps_.unsqueeze(2).to_broadcast([P, STEPS, E]), ALU.is_le))
                link(nc.vector.tensor_reduce(step_f[:, :], s3, AX.X, ALU.add))
                link(nc.vector.tensor_scalar(step_f[:, :], step_f[:, :], float(E - 1), None, ALU.min))
                link(nc.vector.tensor_copy(step_e[:, :], step_f[:, :]))
                wrap = step_c[:, 0:STEPS]
                for _ in range((E - 1) // BUFS[n]):
                    link(nc.vector.tensor_scalar(wrap, step_f[:, :], float(BUFS[n]), float(BUFS[n]), ALU.is_ge, ALU.mult))
                    link(nc.vector.tensor_tensor(step_f[:, :], step_f[:, :], wrap, ALU.subtract))
                nc.vector.tensor_copy(step_b[:, :], step_f[:, :]).then_inc(steps_ready, 1)
                dve.wait_ge(top_exp, n + 1)
                link(nc.vector.tensor_scalar(w3[:, 1, :], w3[:, 0, :], 1.0, None, ALU.add))
                link(nc.vector.reciprocal(w3[:, 1, :], w3[:, 1, :]))
                link(nc.vector.tensor_tensor(w3[:, 2, :], w3[:, 0, :], w3[:, 1, :], ALU.mult))
                c3 = comb[:, :].rearrange("p (t e) -> p t e", e=E)
                dve.wait_ge(slots_ready, n + 1)
                if n == 1:
                    for c in range(TOP):
                        last = nc.vector.tensor_tensor(p4[:, c], p4[:, c], w3[:, 1 + c, :].unsqueeze(2).to_broadcast([P, T, E]), ALU.mult)
                    link(last)
                    nc.vector.tensor_tensor(c3, p4[:, 0], p4[:, 1], ALU.add).then_inc(comb_ready, 1)

            def experts(n):

                def x_now(s, b):
                    nc.vector.tensor_scalar(xg_now[:, b, :], xg[:, bass.ds(s, 1), :].rearrange("p o d -> p (o d)"), 1.0, None,
                                            ALU.mult).then_inc(moe["xg_now_ready"], 1)

                def elementwise(s, j, first):
                    dve.wait_ge(moe["gu_filled"], n * (2 * STEPS + 1) + (s * 2 + (j + 2)))
                    if n == 0:
                        if not first:
                            dve.wait_ge(moe["silued"], s * 2 + (j - 1))
                        nc.vector.tensor_scalar(gclip[:, j], ps[:, j, :], -10.0, 10.0, ALU.max, ALU.min).then_inc(moe["clipped"], 1)
                        dve.wait_ge(moe["silued"], s * 2 + (j + 1))
                    if not first:
                        dve.wait_ge(moe["hid_turned"], n * 2 * STEPS + (s * 2 + (j - 1)))
                    if n == 0:
                        nc.vector.tensor_tensor(hid[:, j], gact[:, j], ps[:, 2 + j, :], ALU.mult).then_inc(moe["hid_ready"], 1)
                    else:
                        nc.vector.tensor_copy(hid[:, j], ps[:, j, :]).then_inc(moe["hid_ready"], 1)

                def take_y(s, b):
                    dve.wait_ge(moe["y_free"], n * STEPS + (s + 1))
                    dve.wait_ge(moe["y_filled"], n * (STEPS + 1) + (s + 2))
                    nc.vector.tensor_copy(y_now[:, b], ps[:, 7, 0:D]).then_inc(moe["y_taken"], 1)

                dve.sem_inc(moe["y_taken"], 1)
                dve.wait_ge(xg_in[0], 16 * (n + 1))
                x_now(0, 0)
                x_now(1, 1)
                for c in range(1, len(XG_PARTS)):
                    dve.wait_ge(xg_in[c], 16 * (n + 1))
                elementwise(0, 0, True)
                elementwise(0, 1, True)
                with dve.Fori(0, STEPS // 2) as it:
                    for u in range(2):
                        s, b = it * 2 + (u + 1), (u + 1) % 2
                        dve.wait_ge(moe["xg_turned"], n * (STEPS + 1) + (s))
                        x_now(s + 1, 1 - b)
                        elementwise(s, 0, False)
                        elementwise(s, 1, False)
                        take_y(it * 2 + u, u)
                take_y(STEPS - 1, (STEPS - 1) % 2)
                w3 = wgt[:, :].rearrange("p (c t) -> p c t", c=3)

                def add(half):
                    for c in range(TOP):
                        dve.wait_ge(token_y_in[half][c], 16 * (n + 1))
                        for i in range(HT):
                            t = HT * half + i
                            if c:
                                dve.wait_ge(moe["added"], n * TOP * T + TOP * HT * half + i + 1)
                            nc.vector.scalar_tensor_tensor(h[:, t, :], yg[:, c, t, :], w3[:, 1 + c, t:t + 1], h[:, t, :],
                                                           ALU.mult, ALU.add).then_inc(moe["added"], 1)

                def stats(half):
                    for i in range(HT):
                        dve.wait_ge(moe["added"], n * TOP * T + TOP * HT * half + HT + i + 1)
                        row_stats(h, HT * half + i)
                    rstd_begin(half)

                add(0)
                if n == 0:
                    stats(0)
                add(1)
                if n == 0:
                    dve.wait_ge(rstd_ready, norms[0])
                    norm_to(ya, h, 1, 0, normed)
                    stats(1)
                    norm_to(xh, h, 0, 0)
                    dve.wait_ge(rstd_ready, norms[0])
                    norm_to(ya, h, 1, 1, normed)
                    norm_to(xh, h, 0, 1)

            ones = part(tok_c, TOK_PACK, "ones")
            dve.wait_ge(qk_sum, 1)
            nc.vector.tensor_copy(qk[:, :], ps[:, 7, 0:KD * POOL_HEADS]).then_inc(qk_ready, 1)
            for i in range(1, T + 3):
                if i <= T:
                    t = i - 1
                    a = tsc[:, 32 * (t % 2):32 * (t % 2) + 32].rearrange("p (w h) -> p w h", w=WIN)
                    s = ps[:, 4, 0:32].rearrange("p (w h) -> p w h", w=WIN)
                    mx = tmx[:, 4 * (t % 2):4 * (t % 2) + 4]
                    dve.wait_ge(tok_turned, t + 1)
                    link(nc.vector.tensor_reduce(mx, s.rearrange("p w h -> p h w"), AX.X, ALU.max))
                    nc.vector.tensor_tensor(a, s, mx.unsqueeze(1).to_broadcast([P, WIN, POOL_HEADS]), ALU.subtract).then_inc(tok_shift, 1)
                if 2 <= i <= T + 1:
                    t = i - 2
                    a = tsc[:, 32 * (t % 2):32 * (t % 2) + 32].rearrange("p (w h) -> p w h", w=WIN)
                    sm = tsum[:, 4 * (t % 2):4 * (t % 2) + 4]
                    wb = wbar[:, WIN * (t % 2):WIN * (t % 2) + WIN]
                    dve.wait_ge(tok_exp, t + 1)
                    link(nc.vector.tensor_reduce(sm, a.rearrange("p w h -> p h w"), AX.X, ALU.add))
                    link(nc.vector.reciprocal(sm, sm))
                    link(nc.vector.scalar_tensor_tensor(a, a, 1.0 / POOL_HEADS, sm.unsqueeze(1).to_broadcast([P, WIN, POOL_HEADS]),
                                                        ALU.mult, ALU.mult))
                    link(nc.vector.tensor_reduce(wb, a, AX.X, ALU.add))
                    dve.wait_ge(x_in[t], 16)
                    if t >= 2:
                        dve.wait_ge(pool_turned, t - 1)
                    sums = (pooled[:, t % 2, :], pool_odd)
                    for w in range(WIN):
                        if w < 2:
                            ins = nc.vector.tensor_scalar(sums[w % 2], frames[:, t, w, :], wb[:, w:w + 1], None, ALU.mult)
                        else:
                            dve.wait_ge(dve_step, steps[0] - 1)
                            ins = nc.vector.scalar_tensor_tensor(sums[w % 2], frames[:, t, w, :], wb[:, w:w + 1], sums[w % 2],
                                                                 ALU.mult, ALU.add)
                        ins.then_inc(dve_step, 1)
                        steps[0] += 1
                    dve.wait_ge(dve_step, steps[0])
                    last = nc.vector.tensor_tensor(sums[0], sums[0], sums[1], ALU.add)
                    last.then_inc(tok_pooled, 1)
                if i >= 3:
                    t = i - 3
                    dve.wait_ge(tok_out, t + 1)
                    nc.vector.tensor_copy(h[:, t, :], ps[:, 5, D:2 * D]).then_inc(h_ready, 1)
                    dve.wait_ge(h_ready, t + 1)
                    row_stats(h, t)
                    if t == HT - 1:
                        rstd_begin(0)
                    if t == HT:
                        dve.wait_ge(rstd_ready, norms[0])
                        norm_to(xh, h, 0, 0, normed)
            rstd(1)
            norm_to(xh, h, 0, 1, normed)
            dve.wait_ge(w_l0, 32)
            nc.vector.tensor_copy(mask32[:, :], w0["mask32"])
            link(nc.vector.tensor_copy(iota[:, :], w0["iota"]))

            def finish_0(half):
                mine = range(HT * half, HT * half + HT)
                rstd(half)
                for t in mine:
                    last = nc.vector.scalar_tensor_tensor(ub[:, t, :], ub[:, t, :], mv3[:, t, 0:1], w0["ln_g"], ALU.subtract, ALU.mult)
                link(last)
                for t in mine:
                    if t == 0:
                        dve.wait_ge(h_shifted, T)
                    nc.vector.scalar_tensor_tensor(h[:, t, :], ub[:, t, :], rs[:, t:t + 1], h[:, t, :], ALU.mult, ALU.add).then_inc(h_ready, 1)
                for t in mine:
                    dve.wait_ge(h_ready, T + t + 1)
                    row_stats(h, t)
                rstd(half)
                norm_to(ya, h, 1, half, normed)

            attend(0, w0, True, finish_0)
            route(0)

            def gate_times_up(n):
                def clip():
                    nc.vector.tensor_scalar(gclip[:, n % 2], ps[:, n % 2, :], -10.0, 10.0, ALU.max, ALU.min).then_inc(sh_clipped, 1)

                def mult():
                    nc.vector.tensor_tensor(hid[:, n % 2], gact[:, n % 2], ps[:, 2 + n % 2, :], ALU.mult).then_inc(sh_hid, 1)
                return clip, mult

            for n in range(4):
                clip, mult = gate_times_up(n)
                dve.wait_ge(sh_filled, n + 1)
                clip()
                dve.wait_ge(sh_act, n + 1)
                if n >= 2:
                    dve.wait_ge(sh_down, 1)
                mult()
            for t in range(T):
                dve.wait_ge(sh_down, t // HT + 1)
                nc.vector.tensor_tensor(h[:, t, :], ps[:, 4 + t // 2, D * (t % 2):D * (t % 2) + D], h[:, t, :], ALU.add).then_inc(sh_added, 1)
            dve.wait_ge(sh_added, T)
            experts(0)
            dve.wait_ge(w_ga, 16)
            for j, (a, b) in enumerate((("al", "als"), ("be", "bes"))):
                link(nc.vector.tensor_scalar(rot[:, 0:S], ga["cos"], ga[a], None, ALU.mult))
                link(nc.vector.scalar_tensor_tensor(rot[:, S:2 * S], ga["sin"], ga[b], rot[:, 0:S], ALU.mult, ALU.add))
                o = (rot_a, rot_b)[j].rearrange("p (b s) -> p b s", s=S)
                nc.vector.tensor_copy(o, rot[:, S:2 * S].unsqueeze(1).to_broadcast([P, P // S, S])).then_inc(rot_ready, 1)
                dve.wait_ge(rot_ready, j + 1)
            dve.wait_ge(xd_copied, 2)
            nc.vector.tensor_copy(sel[:, :], ga["sel"])
            link(nc.vector.tensor_copy(xd_parts[:, :], xd[:, :]))
            link(nc.vector.tensor_tensor(rest[64:P, :], xd[64:P, :], xd_parts[64:P, :], ALU.subtract))
            link(nc.vector.tensor_copy(xd_parts[64:P, :], rest[64:P, :]))
            link(nc.vector.tensor_tensor(rest[96:P, :], rest[96:P, :], xd_parts[96:P, :], ALU.subtract))
            nc.vector.tensor_copy(xd_parts[96:P, :], rest[96:P, :]).then_inc(xd_split, 1)
            for j in range(4):
                dve.wait_ge(dt_abs, j + 1)
                nc.vector.tensor_scalar(dt[:, j // 2, HALF * (j % 2):HALF * (j % 2) + HALF], ps[:, j, :],
                                        ga["dtb"][:, j // 2:j // 2 + 1], 0.0, ALU.add, ALU.max).then_inc(dt_relu, 1)

            def take_values(half):
                for t in range(HT * half, HT * half + HT):
                    dve.wait_ge(gv_filled, t + 1)
                    nc.vector.tensor_tensor(v[:, t, :], ps[:, 6 + t % 2, 0:D], ga["vb"], ALU.add).then_inc(gv_done, 1)

            take_values(0)
            dve.wait_ge(dt_relu, 4)
            dve.wait_ge(dt_log, 1)
            dtf = dt.rearrange("p k n -> p (k n)")
            link(nc.vector.tensor_tensor(dtf, dtf, fm[:, 2 * TOK:4 * TOK], ALU.add))
            dve.wait_ge(cols_ready, 12)
            link(nc.vector.tensor_tensor(dtu.rearrange("p k n -> p (k n)"), dtf, xc.rearrange("p k n -> p (k n)"), ALU.mult))
            nc.vector.memset(dA.rearrange("p k (b s) -> p (k b) s", s=S)[:, :, 0:1], 0.0).then_inc(dtu_ready, 1)
            dve.wait_ge(a_exp, 1)
            nc.vector.tensor_scalar(avec[:, :], avec[:, :], -1.0, None, ALU.mult).then_inc(a_ready, 1)
            take_values(1)
            for n in range(NS):
                for dk in range(KD):
                    dve.wait_ge(b_used, KD * n + dk + 1)
                    if n >= 1:
                        dve.wait_ge(c_used, KD * (n - 1) + dk + 1)
                    dve.wait_ge(decay, KD * n + dk + 1)
                    nc.vector.tensor_tensor_scan(hs[:, dk, :], dA[:, dk, :], dBu[:, dk, :], 0.0, ALU.mult, ALU.add).then_inc(scanned, 1)
                dve.wait_ge(c_spread, n + 1)
                for dk in range(KD):
                    dve.wait_ge(scanned, KD * n + dk + 1)
                    if n >= 1:
                        dve.wait_ge(y_summed, KD * (n - 1) + dk + 1)
                    nc.vector.tensor_tensor(hC[:, dk, :], hs[:, dk, :], ps[:, 6:8, :].rearrange("p b n -> p (b n)"), ALU.mult).then_inc(c_used, 1)
            for j in range(4):
                dk, tok = j // 2, slice(HALF * (j % 2), HALF * (j % 2) + HALF)
                dve.wait_ge(y_summed, KD * (NS - 1) + dk + 1)
                nc.vector.scalar_tensor_tensor(ypre[:, dk, tok], xc[:, dk, tok], ga["D"][:, dk:dk + 1], ps[:, j, :],
                                               ALU.mult, ALU.add).then_inc(y_ready, 1)
            dve.wait_ge(rot_filled, 1)
            nc.vector.tensor_tensor(gbias, ps[:, 4, 0:P], ga["mask"], ALU.add).then_inc(gbias_ready, 1)
            dve.wait_ge(zr_done, 2)
            for j, o in enumerate((zq, zk)):
                nc.vector.tensor_scalar(o, zT, ga["gamma"][:, j:j + 1], ga["beta"][:, j:j + 1], ALU.mult, ALU.add).then_inc(qk_cols, 1)
            dve.wait_ge(gbias_ready, 1)
            for i in range(T + 4):
                if i < T:
                    t = i
                    dve.wait_ge(g_scored, t + 1)
                    link(nc.vector.scalar_tensor_tensor(gsc[:, t % 2], ps[:, t % 2, 0:P], Z ** -0.5, gbias, ALU.mult, ALU.add))
                    nc.vector.tensor_reduce(smx[:, t % 2:t % 2 + 1], gsc[:, t % 2], AX.X, ALU.max, negate=True).then_inc(g_shifted, 1)
                if 1 <= i <= T:
                    t = i - 1
                    dve.wait_ge(g_exped, t + 1)
                    sm = ssum[:, t % 2:t % 2 + 1]
                    link(nc.vector.reciprocal(sm, sm))
                    nc.vector.tensor_scalar(gsc[:, t % 2], gsc[:, t % 2], sm, None, ALU.mult).then_inc(g_probs, 1)
                if 2 <= i <= T + 1:
                    t = i - 2
                    dve.wait_ge(g_mixed, t + 1)
                    nc.vector.tensor_tensor(ghr[:, t % 2], ps[:, 4 + t % 2, 0:D].rearrange("p (k n) -> p k n", k=KD),
                                            rT[:, :, P * t:P * t + P], ALU.mult).then_inc(g_gated, 1)
                if i == HT + 4:
                    dve.wait_ge(rstd_ready, norms[0])
                    norm_to(ya, h, 1, 0, normed)
                if i >= 4:
                    t = i - 4
                    dve.wait_ge(g_delta, t + 1)
                    if t == 0:
                        dve.wait_ge(h_plus_x, T)
                    nc.vector.tensor_tensor(h[:, t, :], h[:, t, :], ub[:, t, :], ALU.add).then_inc(g_done, 1)
                    dve.wait_ge(g_done, t + 1)
                    row_stats(h, t)
                    if t % HT == HT - 1:
                        rstd_begin(t // HT)
            dve.wait_ge(rstd_ready, norms[0])
            norm_to(ya, h, 1, 1, normed)
            for half in range(2):
                norm_to(xh, h, 0, half)
            def finish_1(half):
                rstd(half)
                norm_to(ya, ub, 0, half, normed)
                for t in range(HT * half, HT * half + HT):
                    nc.vector.tensor_tensor(h[:, t, :], h[:, t, :], ub[:, t, :], ALU.add).then_inc(h_ready, 1)

            attend(1, w1, False, finish_1)
            dve.wait_ge(h_ready, 3 * T)
            route(1)
            dve.wait_ge(comb_turned, 1)
            for j in range(2):
                nc.vector.tensor_copy(combT[0:E, 4 * j:4 * j + 4].rearrange("p t n -> p (t n)"), ps[0:E, 4 + j, :]).then_inc(comb_copied, 1)
            for t in range(T):
                dve.wait_ge(bias_filled, t // 2 * 2 + 2)
                nc.vector.tensor_tensor(h[:, t, :], ps[:, t // 2, D * (t % 2):D * (t % 2) + D], h[:, t, :], ALU.add).then_inc(bias_added, 1)
            dve.wait_ge(bias_added, T)
            experts(1)




def kernel(**inp):
    import concourse.bacc as _bacc
    from concourse.bass_utils import run_bass_kernel_spmd as _run

    a = {k: np.asarray(v_) for k, v_ in inp.items()}
    f32 = np.float32

    def blocks(w):
        k, n = w.shape
        return w.reshape(k // P, P, n).transpose(1, 0, 2).reshape(P, -1)

    def per_feature(b):
        return b.reshape(-1, P).T

    def everywhere(b):
        return np.broadcast_to(b, (P, b.shape[-1]))

    def padded_heads(w):
        w = w.reshape(w.shape[0], H, HD)
        out = np.zeros((w.shape[0], H, 32), f32)
        out[:, :, :HD] = w
        return out.reshape(w.shape[0], H * 32)

    def on_rows(w, rows=P):
        out = np.zeros((rows, w.shape[1]), f32)
        out[:w.shape[0]] = w
        return out

    def pack(parts, where, n, rows=P):
        out = np.zeros((rows, n), f32)
        for name, (s, e) in where.items():
            out[:, s:e] = parts[name]
        return out

    x = np.zeros((CLIPS, P, D), f32)
    x[:, :FRAMES] = a["x"]
    x = x.reshape(T, P, WIN * D)

    tok_w = pack({"wk": blocks(a["L0_tok_Wk"]), "q": blocks(a["L0_tok_q"].T), "wv": blocks(a["L0_tok_Wv"].T),
                  "ident": np.eye(P, dtype=f32), "tri": -np.tril(np.ones((P, P), f32)), "ones": np.ones((P, P), f32),
                  "steps": everywhere(np.arange(STEPS, dtype=f32)),
                  "reset": everywhere(np.tile(np.arange(T) > 0, E).astype(f32)),
                  "home": np.arange(P, dtype=f32)[:, None] + P * np.arange(TOP * T + STEPS + 1, dtype=f32)}, TOK_PACK, TOK_N)

    tok = np.arange(P)
    same = (tok[:, None] // S == tok[None, :] // S) & (tok[None, :] <= tok[:, None])
    mask128 = np.where(same, 0.0, NEG).astype(f32)
    mask32 = np.stack([mask128[p, 32 * (p // 32):32 * (p // 32) + 32] for p in range(P)])
    half = Z // 2
    freqs = np.exp(np.arange(half, dtype=f32) * f32(-np.log(10000.0) / half)).astype(f32)
    ang = (np.arange(S, dtype=f32)[:, None] * freqs[None, :]).astype(f32)
    cos = np.concatenate([np.cos(ang), np.cos(ang)], 1).T.astype(f32)
    sin = np.concatenate([-np.sin(ang), np.sin(ang)], 1).T.astype(f32)

    rpb = a["L0_attn_rpb"]
    pos = np.clip(np.arange(32)[None, :] % S - tok[:, None] % S, -S + 1, S - 1) + S - 1
    heads = [G * m + j for j in range(G) for m in range(G)]
    rel = rpb[pos][:, :, heads].transpose(0, 2, 1).reshape(P, H * 32)
    w = a["L0_attn_W_w"]
    bq, bk, bv = np.split(a["L0_attn_W_b"], 3)
    l0_w = pack({
        "wq": blocks(padded_heads(w[0:D].T)), "wk": blocks(padded_heads(w[D:2 * D].T)), "wv": blocks(w[2 * D:].T),
        "wo": blocks(a["L0_attn_proj_w"].T), "bq": per_feature(padded_heads(bq[None])[0]),
        "bk": per_feature(padded_heads(bk[None])[0]), "bv": everywhere(bv), "bo": everywhere(a["L0_attn_proj_b"]), "rel": rel, "mask32": mask32,
        "ln_g": everywhere(a["L0_attn_ln_g"]), "ln_b": everywhere(a["L0_attn_ln_b"]),
        "gamma": per_feature(a["L0_ffn_ln_gamma"]), "beta": per_feature(a["L0_ffn_ln_beta"]),
        "router": blocks(a["L0_ffn_router_w"]), "sgu": blocks(a["L0_ffn_shared_gate_up_w"]),
        "sdn": blocks(a["L0_ffn_shared_down_w"]), "iota": everywhere(np.arange(E, dtype=f32))}, L0_PACK, L0_N)

    mx_b = a["L1_attn_mx_b"]
    swap = np.r_[half:Z, 0:half]
    al, be = a["L1_attn_alpha_rb"][0], a["L1_attn_beta_rb"][0]
    xproj = np.zeros((D, P), f32)
    xproj[:, :DTR] = a["L1_attn_xproj_w"].T[:, :DTR]
    for r in range(32, P, 32):
        xproj[:, r:r + 32] = a["L1_attn_xproj_w"].T[:, DTR:]
    ga_w = pack({
        "norm": per_feature(a["L1_attn_norm_w"]), "v": blocks(a["L1_attn_v_w"].T), "vb": everywhere(a["L1_attn_v_b"]), "mx": blocks(a["L1_attn_mx_w"].T),
        "mxb": per_feature(mx_b[D:D + 3 * P]), "h": blocks(a["L1_attn_h_w"].T), "xproj": blocks(xproj),
        "dt": on_rows(a["L1_attn_dt_w"].T), "A": blocks(a["L1_attn_A_log"]), "D": per_feature(a["L1_attn_D_p"]),
        "dtb": per_feature(a["L1_attn_dt_b"]), "gamma": a["L1_attn_gamma"].T, "beta": a["L1_attn_beta"].T,
        "sel": (tok[:, None] >= 32) * (tok[:, None] % 32 == np.arange(2 * NS)[None]).astype(f32),
        "cos": cos, "sin": sin, "al": al[:, None], "als": al[swap][:, None], "be": be[:, None],
        "bes": be[swap][:, None], "mask": mask128}, GA_PACK, GA_N)

    wq, wk, wv = np.split(a["L1_ffn_w_qkv"], 3, axis=1)
    l1_w = pack({
        "wq": blocks(padded_heads(wq)), "wk": blocks(padded_heads(wk)), "wv": blocks(wv), "wo": blocks(a["L1_ffn_w_o"]),
        "g1": per_feature(a["L1_ffn_ln1_g"]), "b1": per_feature(a["L1_ffn_ln1_b"]),
        "g2": per_feature(a["L1_ffn_ln2_g"]), "b2": per_feature(a["L1_ffn_ln2_b"]), "router": blocks(a["L1_ffn_w_gate"]),
        "eb1": a["L1_ffn_b1"].reshape(E, FB, P).transpose(2, 0, 1).reshape(P, E * FB),
        "eb2": on_rows(a["L1_ffn_b2"])}, L1_PACK, L1_N)

    first = np.zeros((32, P), f32)
    first[0:2] = 1.0
    rows_w = pack({
        "one": first,
        "u": on_rows(mx_b[None, 0:D], 32),
        "h": on_rows(np.stack([mx_b[640:896], a["L1_attn_h_b"]]), 32)}, ROW_PACK, ROW_N, 32)

    def expert_blocks(w3):
        e, k, n = w3.shape
        return np.ascontiguousarray(w3.reshape(e, k // P, P, n).transpose(0, 2, 1, 3))

    arrays = {
        "x": x, "tok_w": tok_w, "l0_w": l0_w, "ga_w": ga_w, "l1_w": l1_w, "rows_w": rows_w,
        "moe0_gu": expert_blocks(a["L0_ffn_gate_up_w"]), "moe0_dn": expert_blocks(a["L0_ffn_down_w"]),
        "moe1_up": expert_blocks(a["L1_ffn_w1"]), "moe1_dn": expert_blocks(a["L1_ffn_w2"])}

    nc = _bacc.Bacc("TRN2", target_bir_lowering=False, num_devices=1)
    args = [nc.dram_tensor(n, v_.shape, F32, kind="ExternalInput").ap() for n, v_ in arrays.items()]
    out = nc.dram_tensor("out", (TOK, D), F32, kind="ExternalOutput").ap()
    scratch = [[nc.dram_tensor(f"{n}{i}", shape, dt, kind="Internal").ap() for i in range(2)]
               for n, shape, dt in (("sorted_x", ((STEPS + 1) * P, D), F32), ("slot_home", ((STEPS + 1) * P, 1), U32),
                                    ("token_y", (TOP * TOK + (STEPS + 1) * P, D), F32))]
    tower(nc, *args, out, *scratch)
    r = _run(nc, [arrays], core_ids=[0])
    return r.results[0]["out"].reshape(CLIPS, S, D)
```
